# Optimizing a Trainium2 kernel written in Bass

```python
import numpy as np
import jax
import jax.numpy as jnp

def _softmax(x, axis=-1):
    return jax.nn.softmax(x, axis=axis)

def _gelu(x):
    return jax.nn.gelu(x, approximate=True)

def _silu(x):
    return jax.nn.silu(x)

def _sigmoid(x):
    return jax.nn.sigmoid(x)

def _layernorm(x, axis=-1, eps=1e-05):
    m = jnp.mean(x, axis=axis, keepdims=True)
    v = jnp.var(x, axis=axis, keepdims=True)
    return (x - m) / jnp.sqrt(v + eps)

def _scatter_add(tgt, idx, src, axis=0):
    return tgt.at[idx].add(src)

def _segment_sum(src, seg, n):
    return jax.ops.segment_sum(src, seg, n)
kernel_name = 'mk_vit_tower_d4_tok_img512_r4_fbfe20'

def setup_inputs(seed: int=0):
    np.random.seed(seed)
    _w = jnp.asarray

    def _rec_inputs():
        import jax
        import jax.numpy as jnp
        _rk = jax.random.key(seed)
        x = -0.000356955 + 1 * jax.random.normal(jax.random.fold_in(_rk, 1), (64, 3, 96, 96), jnp.float32)
        return x
    x = _rec_inputs()

    def _L0_tok_setup():
        import jax, jax.numpy as jnp
        import numpy as np
        key = jax.random.key(seed)
        k1, k2, k3 = jax.random.split(key, 3)
        B, C, H, W = (128, 3, 224, 224)
        E, p = (128, 16)
        K = C * p * p
        img = jax.random.normal(k1, (B, C, H, W), dtype=jnp.float32)
        w = jax.random.normal(k2, (E, K), dtype=jnp.float32) * (1.0 / np.sqrt(K))
        b = jax.random.normal(k3, (E,), dtype=jnp.float32)
        return {'img': img, 'w': w, 'b': b, 'patch_size': p}
    _L0_tok_all = _L0_tok_setup()
    _L0_tok_in = {k: v for k, v in _L0_tok_all.items() if k in ('w', 'b')}
    del _L0_tok_all

    def _L0_attn_setup():
        import jax, jax.numpy as jnp
        import numpy as np
        DIM = 128
        NUM_HEADS = 8
        HEAD_DIM = DIM // NUM_HEADS
        SCALE = HEAD_DIM ** (-0.5)

        def _attention(x, w_qkv, w_proj, b_proj, ln_gamma, ln_beta):
            B, N, C = x.shape
            qkv = jnp.einsum('bnc,dc->bnd', x, w_qkv)
            qkv = qkv.reshape(B, N, 3, NUM_HEADS, HEAD_DIM)
            qkv = jnp.transpose(qkv, (2, 0, 3, 1, 4))
            q, k, v = (qkv[0], qkv[1], qkv[2])
            attn = jnp.einsum('bhnd,bhmd->bhnm', q, k) * SCALE
            attn = jax.nn.softmax(attn, axis=-1)
            out = jnp.einsum('bhnm,bhmd->bhnd', attn, v)
            out = jnp.transpose(out, (0, 2, 1, 3)).reshape(B, N, C)
            out = jnp.einsum('bnc,dc->bnd', out, w_proj) + b_proj
            y = x + out
            mean = jnp.mean(y, axis=-1, keepdims=True)
            var = jnp.var(y, axis=-1, keepdims=True)
            return (y - mean) / jnp.sqrt(var + 1e-05) * ln_gamma + ln_beta
        key = jax.random.key(seed)
        ks = jax.random.split(key, 6)
        B, N = (2, 1024)
        x = jax.random.normal(ks[0], (B, N, DIM), dtype=jnp.float32)
        lim_qkv = float(np.sqrt(6.0 / (3 * DIM + DIM)))
        w_qkv = jax.random.uniform(ks[1], (3 * DIM, DIM), minval=-lim_qkv, maxval=lim_qkv, dtype=jnp.float32)
        lim_p = float(np.sqrt(6.0 / (DIM + DIM)))
        w_proj = jax.random.uniform(ks[2], (DIM, DIM), minval=-lim_p, maxval=lim_p, dtype=jnp.float32)
        b_proj = jnp.zeros((DIM,), dtype=jnp.float32)
        ln_gamma = jnp.ones((DIM,), dtype=jnp.float32)
        ln_beta = jnp.zeros((DIM,), dtype=jnp.float32)
        return {'x': x, 'w_qkv': w_qkv, 'w_proj': w_proj, 'b_proj': b_proj, 'ln_gamma': ln_gamma, 'ln_beta': ln_beta}
    _L0_attn_all = _L0_attn_setup()
    _L0_attn_in = {k: v for k, v in _L0_attn_all.items() if k in ('w_qkv', 'w_proj', 'b_proj', 'ln_gamma', 'ln_beta')}
    del _L0_attn_all

    def _L0_ffn_setup():
        import jax, jax.numpy as jnp
        import numpy as np
        DIM, DEPTH, MULT = (128, 3, 4)
        E = 2 ** DEPTH
        HID = MULT * DIM
        B, S = (4, 256)

        def _leaf_probs(flat_x, rw, rb):
            n_tok = flat_x.shape[0]
            leaf = jnp.ones((n_tok, 1), dtype=flat_x.dtype)
            for d in range(DEPTH):
                off, n = (2 ** d - 1, 2 ** d)
                logits = flat_x @ rw[off:off + n].T + rb[off:off + n]
                p = jax.nn.sigmoid(logits)
                leaf = (leaf[:, :, None] * jnp.stack([1.0 - p, p], axis=2)).reshape(n_tok, 2 * n)
            return leaf
        key = jax.random.key(seed)
        ks = jax.random.split(key, 7)
        sd = 1.0 / np.sqrt(DIM)
        sh = 1.0 / np.sqrt(HID)
        return {'x': jax.random.normal(ks[0], (B, S, DIM), dtype=jnp.float32), 'rw': jax.random.normal(ks[1], (E - 1, DIM), dtype=jnp.float32) * sd, 'rb': jax.random.normal(ks[2], (E - 1,), dtype=jnp.float32) * sd, 'w1': jax.random.normal(ks[3], (E, DIM, HID), dtype=jnp.float32) * sd, 'b1': jax.random.normal(ks[4], (E, HID), dtype=jnp.float32) * sd, 'w2': jax.random.normal(ks[5], (E, HID, DIM), dtype=jnp.float32) * sh, 'b2': jax.random.normal(ks[6], (E, DIM), dtype=jnp.float32) * sh}
    _L0_ffn_all = _L0_ffn_setup()
    _L0_ffn_in = {k: v for k, v in _L0_ffn_all.items() if k in ('rw', 'rb', 'w1', 'b1', 'w2', 'b2')}
    del _L0_ffn_all

    def _L1_attn_setup():
        import jax, jax.numpy as jnp
        import numpy as np
        D_MODEL = 128
        FF = 512
        D_STATE = 128
        D_CONV = 4
        EXPAND = 2
        D_INNER = EXPAND * D_MODEL
        HEADDIM = 64
        NHEADS = D_INNER // HEADDIM
        NGROUPS = 1
        CONV_DIM = D_INNER + 2 * NGROUPS * D_STATE
        D_IN_PROJ = 2 * D_INNER + 2 * NGROUPS * D_STATE + NHEADS
        B_SZ = 2
        SEQ = 512

        def _layernorm(x, g, b, eps=1e-05):
            m = jnp.mean(x, -1, keepdims=True)
            v = jnp.var(x, -1, keepdims=True)
            return (x - m) * jax.lax.rsqrt(v + eps) * g + b

        def _mamba2(x, W_in, conv_w, conv_b, dt_bias, A_log, D_skip, gnorm_w, W_out):
            Bb, S, _ = x.shape
            zxbcdt = x @ W_in
            z = zxbcdt[..., :D_INNER]
            xBC = zxbcdt[..., D_INNER:D_INNER + CONV_DIM]
            dt = zxbcdt[..., D_INNER + CONV_DIM:]
            xc = jnp.moveaxis(xBC, 1, 2)
            xp = jnp.pad(xc, ((0, 0), (0, 0), (D_CONV - 1, 0)))
            yc = sum((conv_w[None, :, k:k + 1] * xp[:, :, k:k + S] for k in range(D_CONV)))
            xBC = jax.nn.silu(jnp.moveaxis(yc, 1, 2) + conv_b)
            xs = xBC[..., :D_INNER].reshape(Bb, S, NHEADS, HEADDIM)
            Bc = xBC[..., D_INNER:D_INNER + D_STATE]
            Cc = xBC[..., D_INNER + D_STATE:]
            dt = jax.nn.softplus(dt + dt_bias)
            A = -jnp.exp(A_log)
            dA = jnp.exp(dt * A)
            tm = lambda a: jnp.moveaxis(a, 1, 0)

            def step(h, inp):
                dA_t, dt_t, B_t, C_t, x_t = inp
                h = h * dA_t[:, :, None, None] + (dt_t[:, :, None] * x_t)[..., None] * B_t[:, None, None, :]
                y_t = jnp.einsum('bhpn,bn->bhp', h, C_t)
                return (h, y_t)
            h0 = jnp.zeros((Bb, NHEADS, HEADDIM, D_STATE), x.dtype)
            _, ys = jax.lax.scan(step, h0, (tm(dA), tm(dt), tm(Bc), tm(Cc), tm(xs)))
            y = jnp.moveaxis(ys, 0, 1) + D_skip[None, None, :, None] * xs
            y = y.reshape(Bb, S, D_INNER)
            y = y * jax.nn.silu(z)
            y = y * jax.lax.rsqrt(jnp.mean(y * y, -1, keepdims=True) + 1e-05) * gnorm_w
            return y @ W_out
        key = jax.random.key(seed)
        ks = jax.random.split(key, 10)
        s = 0.02
        return dict(tgt=jax.random.normal(ks[0], (B_SZ, SEQ, D_MODEL), jnp.float32), W_in=jax.random.normal(ks[1], (D_MODEL, D_IN_PROJ), jnp.float32) * s, conv_w=jax.random.normal(ks[2], (CONV_DIM, D_CONV), jnp.float32) * s, conv_b=jnp.zeros((CONV_DIM,), jnp.float32), dt_bias=jax.random.uniform(ks[3], (NHEADS,), jnp.float32, -4.0, -1.0), A_log=jnp.log(jax.random.uniform(ks[4], (NHEADS,), jnp.float32, 1.0, 16.0)), D_skip=jnp.ones((NHEADS,), jnp.float32), gnorm_w=jnp.ones((D_INNER,), jnp.float32), W_out=jax.random.normal(ks[5], (D_INNER, D_MODEL), jnp.float32) * s, n1_g=jnp.ones((D_MODEL,), jnp.float32), n1_b=jnp.zeros((D_MODEL,), jnp.float32), ffn_w1=jax.random.normal(ks[6], (D_MODEL, FF), jnp.float32) * s, ffn_b1=jnp.zeros((FF,), jnp.float32), ffn_w2=jax.random.normal(ks[7], (FF, D_MODEL), jnp.float32) * s, ffn_b2=jnp.zeros((D_MODEL,), jnp.float32), n3_g=jnp.ones((D_MODEL,), jnp.float32), n3_b=jnp.zeros((D_MODEL,), jnp.float32))
    _L1_attn_all = _L1_attn_setup()
    _L1_attn_in = {k: v for k, v in _L1_attn_all.items() if k in ('W_in', 'conv_w', 'conv_b', 'dt_bias', 'A_log', 'D_skip', 'gnorm_w', 'W_out', 'n1_g', 'n1_b', 'ffn_w1', 'ffn_b1', 'ffn_w2', 'ffn_b2', 'n3_g', 'n3_b')}
    del _L1_attn_all

    def _L1_ffn_setup():
        import jax, jax.numpy as jnp
        import numpy as np
        E, D, H = (8, 128, 512)
        B, N = (8, 128)
        key = jax.random.key(seed)
        ks = jax.random.split(key, 4)

        def init(k, shape, fan_in):
            return jax.random.normal(k, shape, jnp.float32) * (1.0 / np.sqrt(fan_in))
        return {'x': jax.random.normal(ks[0], (B, N, D), jnp.float32), 'Wr': init(ks[1], (D, E), D), 'br': jnp.zeros((E,), jnp.float32), 'W1': init(ks[2], (E, D, H), D), 'b1': jnp.zeros((E, H), jnp.float32), 'W2': init(ks[3], (E, H, D), H), 'b2': jnp.zeros((E, D), jnp.float32)}
    _L1_ffn_all = _L1_ffn_setup()
    _L1_ffn_in = {k: v for k, v in _L1_ffn_all.items() if k in ('Wr', 'br', 'W1', 'b1', 'W2', 'b2')}
    del _L1_ffn_all

    def _L2_attn_setup():
        import jax, jax.numpy as jnp
        import numpy as np
        N_HEADS = 8
        HEAD_SIZE = 64
        CONTEXT = 64
        D_MODEL = 128
        MASK_NEG = 1000000000.0
        key = jax.random.key(seed)
        k1, k2, k3, k4 = jax.random.split(key, 4)
        B, T, D = (2, 1024, D_MODEL)

        def glorot(k, shape):
            fan_in, fan_out = (shape[-2], shape[-1])
            lim = jnp.sqrt(6.0 / (fan_in + fan_out))
            return jax.random.uniform(k, shape, jnp.float32, -lim, lim)
        inputs = jax.random.normal(k1, (B, T, D), dtype=jnp.float32)
        WQ = glorot(k2, (N_HEADS, D, HEAD_SIZE))
        WV = glorot(k3, (N_HEADS, D, HEAD_SIZE))
        WU = glorot(k4, (N_HEADS * HEAD_SIZE, D))
        return {'inputs': inputs, 'WQ': WQ, 'WV': WV, 'WU': WU}
    _L2_attn_all = _L2_attn_setup()
    _L2_attn_in = {k: v for k, v in _L2_attn_all.items() if k in ('WQ', 'WV', 'WU')}
    del _L2_attn_all

    def _L2_ffn_setup():
        import jax, jax.numpy as jnp
        import numpy as np
        B, S, D, H, O, E, TOPK = (4, 512, 128, 256, 128, 8, 2)
        key = jax.random.key(seed)
        ks = jax.random.split(key, 6)
        s = lambda d: 1.0 / np.sqrt(d)
        return {'x': jax.random.normal(ks[0], (B, S, D), dtype=jnp.float32), 'Wg': jax.random.normal(ks[1], (D, E), dtype=jnp.float32) * s(D), 'W1': jax.random.normal(ks[2], (E, D, H), dtype=jnp.float32) * s(D), 'b1': jnp.zeros((E, H), dtype=jnp.float32), 'W2': jax.random.normal(ks[3], (E, H, O), dtype=jnp.float32) * s(H), 'b2': jnp.zeros((E, O), dtype=jnp.float32)}
    _L2_ffn_all = _L2_ffn_setup()
    _L2_ffn_in = {k: v for k, v in _L2_ffn_all.items() if k in ('Wg', 'W1', 'b1', 'W2', 'b2')}
    del _L2_ffn_all

    def _L3_attn_setup():
        import jax, jax.numpy as jnp
        import numpy as np
        HEADS = 8
        DIM_HEAD = 64
        DIM = 128
        SCALE = DIM_HEAD ** (-0.5)
        BN_EPS = 1e-05
        key = jax.random.key(seed)
        ks = jax.random.split(key, 5)
        b, p = (8, 512)
        init = 0.05
        return {'x': jax.random.normal(ks[0], (b, p, DIM), jnp.float32), 'wq': jax.random.normal(ks[1], (HEADS, DIM_HEAD, DIM // HEADS), jnp.float32) * init, 'wk': jax.random.normal(ks[2], (HEADS, DIM_HEAD, DIM // HEADS), jnp.float32) * init, 'wv': jax.random.normal(ks[3], (HEADS, DIM_HEAD, DIM // HEADS), jnp.float32) * init, 'wo': jax.random.normal(ks[4], (DIM, HEADS * DIM_HEAD), jnp.float32) * init, 'gamma': jnp.ones((DIM,), jnp.float32), 'beta': jnp.zeros((DIM,), jnp.float32)}
    _L3_attn_all = _L3_attn_setup()
    _L3_attn_in = {k: v for k, v in _L3_attn_all.items() if k in ('wq', 'wk', 'wv', 'wo', 'gamma', 'beta')}
    del _L3_attn_all

    def _L3_ffn_setup():
        import jax, jax.numpy as jnp
        import numpy as np
        D_MODEL = 128
        N_HEADS = 8
        KV_OPTS = (8, 4, 1)
        D_K = D_MODEL // N_HEADS

        def gqa(x, wq, wk, wv, wo, n_kv):
            B, S, _ = x.shape
            groups = N_HEADS // n_kv
            q = (x @ wq).reshape(B, S, N_HEADS, D_K).transpose(0, 2, 1, 3)
            k = (x @ wk).reshape(B, S, n_kv, D_K).transpose(0, 2, 1, 3)
            v = (x @ wv).reshape(B, S, n_kv, D_K).transpose(0, 2, 1, 3)
            k = jnp.repeat(k, groups, axis=1)
            v = jnp.repeat(v, groups, axis=1)
            scores = jnp.einsum('bhqd,bhkd->bhqk', q, k) / jnp.sqrt(jnp.float32(D_K))
            attn = jax.nn.softmax(scores, axis=-1)
            out = jnp.einsum('bhqk,bhkd->bhqd', attn, v)
            out = out.transpose(0, 2, 1, 3).reshape(B, S, D_MODEL)
            return out @ wo
        key = jax.random.key(seed)
        ks = jax.random.split(key, 32)
        it = iter(ks)
        s = 0.02
        inp = {'x': jax.random.normal(next(it), (64, 256, D_MODEL), dtype=jnp.float32)}
        inp['r_w1'] = jax.random.normal(next(it), (D_MODEL, D_MODEL // 4), jnp.float32) * s
        inp['r_b1'] = jnp.zeros((D_MODEL // 4,), jnp.float32)
        inp['r_w2'] = jax.random.normal(next(it), (D_MODEL // 4, len(KV_OPTS)), jnp.float32) * s
        inp['r_b2'] = jnp.zeros((len(KV_OPTS),), jnp.float32)
        for i, nkv in enumerate(KV_OPTS):
            inp[f'wq{i}'] = jax.random.normal(next(it), (D_MODEL, D_MODEL), jnp.float32) * s
            inp[f'wk{i}'] = jax.random.normal(next(it), (D_MODEL, nkv * D_K), jnp.float32) * s
            inp[f'wv{i}'] = jax.random.normal(next(it), (D_MODEL, nkv * D_K), jnp.float32) * s
            inp[f'wo{i}'] = jax.random.normal(next(it), (D_MODEL, D_MODEL), jnp.float32) * s
        return inp
    _L3_ffn_all = _L3_ffn_setup()
    _L3_ffn_in = {k: v for k, v in _L3_ffn_all.items() if k in ('r_w1', 'r_b1', 'r_w2', 'r_b2', 'wq0', 'wk0', 'wv0', 'wo0', 'wq1', 'wk1', 'wv1', 'wo1', 'wq2', 'wk2', 'wv2', 'wo2')}
    del _L3_ffn_all
    return {'x': x, 'L0_tok_w': _L0_tok_in['w'], 'L0_tok_b': _L0_tok_in['b'], 'L0_attn_w_qkv': _L0_attn_in['w_qkv'], 'L0_attn_w_proj': _L0_attn_in['w_proj'], 'L0_attn_b_proj': _L0_attn_in['b_proj'], 'L0_attn_ln_gamma': _L0_attn_in['ln_gamma'], 'L0_attn_ln_beta': _L0_attn_in['ln_beta'], 'L0_ffn_rw': _L0_ffn_in['rw'], 'L0_ffn_rb': _L0_ffn_in['rb'], 'L0_ffn_w1': _L0_ffn_in['w1'], 'L0_ffn_b1': _L0_ffn_in['b1'], 'L0_ffn_w2': _L0_ffn_in['w2'], 'L0_ffn_b2': _L0_ffn_in['b2'], 'L1_attn_W_in': _L1_attn_in['W_in'], 'L1_attn_conv_w': _L1_attn_in['conv_w'], 'L1_attn_conv_b': _L1_attn_in['conv_b'], 'L1_attn_dt_bias': _L1_attn_in['dt_bias'], 'L1_attn_A_log': _L1_attn_in['A_log'], 'L1_attn_D_skip': _L1_attn_in['D_skip'], 'L1_attn_gnorm_w': _L1_attn_in['gnorm_w'], 'L1_attn_W_out': _L1_attn_in['W_out'], 'L1_attn_n1_g': _L1_attn_in['n1_g'], 'L1_attn_n1_b': _L1_attn_in['n1_b'], 'L1_attn_ffn_w1': _L1_attn_in['ffn_w1'], 'L1_attn_ffn_b1': _L1_attn_in['ffn_b1'], 'L1_attn_ffn_w2': _L1_attn_in['ffn_w2'], 'L1_attn_ffn_b2': _L1_attn_in['ffn_b2'], 'L1_attn_n3_g': _L1_attn_in['n3_g'], 'L1_attn_n3_b': _L1_attn_in['n3_b'], 'L1_ffn_Wr': _L1_ffn_in['Wr'], 'L1_ffn_br': _L1_ffn_in['br'], 'L1_ffn_W1': _L1_ffn_in['W1'], 'L1_ffn_b1': _L1_ffn_in['b1'], 'L1_ffn_W2': _L1_ffn_in['W2'], 'L1_ffn_b2': _L1_ffn_in['b2'], 'L2_attn_WQ': _L2_attn_in['WQ'], 'L2_attn_WV': _L2_attn_in['WV'], 'L2_attn_WU': _L2_attn_in['WU'], 'L2_ffn_Wg': _L2_ffn_in['Wg'], 'L2_ffn_W1': _L2_ffn_in['W1'], 'L2_ffn_b1': _L2_ffn_in['b1'], 'L2_ffn_W2': _L2_ffn_in['W2'], 'L2_ffn_b2': _L2_ffn_in['b2'], 'L3_attn_wq': _L3_attn_in['wq'], 'L3_attn_wk': _L3_attn_in['wk'], 'L3_attn_wv': _L3_attn_in['wv'], 'L3_attn_wo': _L3_attn_in['wo'], 'L3_attn_gamma': _L3_attn_in['gamma'], 'L3_attn_beta': _L3_attn_in['beta'], 'L3_ffn_r_w1': _L3_ffn_in['r_w1'], 'L3_ffn_r_b1': _L3_ffn_in['r_b1'], 'L3_ffn_r_w2': _L3_ffn_in['r_w2'], 'L3_ffn_r_b2': _L3_ffn_in['r_b2'], 'L3_ffn_wq0': _L3_ffn_in['wq0'], 'L3_ffn_wk0': _L3_ffn_in['wk0'], 'L3_ffn_wv0': _L3_ffn_in['wv0'], 'L3_ffn_wo0': _L3_ffn_in['wo0'], 'L3_ffn_wq1': _L3_ffn_in['wq1'], 'L3_ffn_wk1': _L3_ffn_in['wk1'], 'L3_ffn_wv1': _L3_ffn_in['wv1'], 'L3_ffn_wo1': _L3_ffn_in['wo1'], 'L3_ffn_wq2': _L3_ffn_in['wq2'], 'L3_ffn_wk2': _L3_ffn_in['wk2'], 'L3_ffn_wv2': _L3_ffn_in['wv2'], 'L3_ffn_wo2': _L3_ffn_in['wo2']}

def reference(x, L0_tok_w, L0_tok_b, L0_attn_w_qkv, L0_attn_w_proj, L0_attn_b_proj, L0_attn_ln_gamma, L0_attn_ln_beta, L0_ffn_rw, L0_ffn_rb, L0_ffn_w1, L0_ffn_b1, L0_ffn_w2, L0_ffn_b2, L1_attn_W_in, L1_attn_conv_w, L1_attn_conv_b, L1_attn_dt_bias, L1_attn_A_log, L1_attn_D_skip, L1_attn_gnorm_w, L1_attn_W_out, L1_attn_n1_g, L1_attn_n1_b, L1_attn_ffn_w1, L1_attn_ffn_b1, L1_attn_ffn_w2, L1_attn_ffn_b2, L1_attn_n3_g, L1_attn_n3_b, L1_ffn_Wr, L1_ffn_br, L1_ffn_W1, L1_ffn_b1, L1_ffn_W2, L1_ffn_b2, L2_attn_WQ, L2_attn_WV, L2_attn_WU, L2_ffn_Wg, L2_ffn_W1, L2_ffn_b1, L2_ffn_W2, L2_ffn_b2, L3_attn_wq, L3_attn_wk, L3_attn_wv, L3_attn_wo, L3_attn_gamma, L3_attn_beta, L3_ffn_r_w1, L3_ffn_r_b1, L3_ffn_r_w2, L3_ffn_r_b2, L3_ffn_wq0, L3_ffn_wk0, L3_ffn_wv0, L3_ffn_wo0, L3_ffn_wq1, L3_ffn_wk1, L3_ffn_wv1, L3_ffn_wo1, L3_ffn_wq2, L3_ffn_wk2, L3_ffn_wv2, L3_ffn_wo2):
    import jax
    import jax.numpy as jnp

    def _L0_tok_ref(img, w, b, patch_size):
        import jax, jax.numpy as jnp
        import numpy as np
        B, C, H, W = img.shape
        p = patch_size
        Hp, Wp = (H // p, W // p)
        S = Hp * Wp
        patches = img.reshape(B, C, Hp, p, Wp, p)
        patches = patches.transpose(0, 2, 4, 1, 3, 5).reshape(B, S, C * p * p)
        out = jnp.einsum('bsk,ek->bse', patches, w) + b
        return out

    def _L0_attn_ref(x, w_qkv, w_proj, b_proj, ln_gamma, ln_beta):
        import jax, jax.numpy as jnp
        import numpy as np
        DIM = 128
        NUM_HEADS = 8
        HEAD_DIM = DIM // NUM_HEADS
        SCALE = HEAD_DIM ** (-0.5)

        def _attention(x, w_qkv, w_proj, b_proj, ln_gamma, ln_beta):
            B, N, C = x.shape
            qkv = jnp.einsum('bnc,dc->bnd', x, w_qkv)
            qkv = qkv.reshape(B, N, 3, NUM_HEADS, HEAD_DIM)
            qkv = jnp.transpose(qkv, (2, 0, 3, 1, 4))
            q, k, v = (qkv[0], qkv[1], qkv[2])
            attn = jnp.einsum('bhnd,bhmd->bhnm', q, k) * SCALE
            attn = jax.nn.softmax(attn, axis=-1)
            out = jnp.einsum('bhnm,bhmd->bhnd', attn, v)
            out = jnp.transpose(out, (0, 2, 1, 3)).reshape(B, N, C)
            out = jnp.einsum('bnc,dc->bnd', out, w_proj) + b_proj
            y = x + out
            mean = jnp.mean(y, axis=-1, keepdims=True)
            var = jnp.var(y, axis=-1, keepdims=True)
            return (y - mean) / jnp.sqrt(var + 1e-05) * ln_gamma + ln_beta
        return _attention(x, w_qkv, w_proj, b_proj, ln_gamma, ln_beta)

    def _L0_ffn_ref(x, rw, rb, w1, b1, w2, b2):
        import jax, jax.numpy as jnp
        import numpy as np
        DIM, DEPTH, MULT = (128, 3, 4)
        E = 2 ** DEPTH
        HID = MULT * DIM
        B, S = (4, 256)

        def _leaf_probs(flat_x, rw, rb):
            n_tok = flat_x.shape[0]
            leaf = jnp.ones((n_tok, 1), dtype=flat_x.dtype)
            for d in range(DEPTH):
                off, n = (2 ** d - 1, 2 ** d)
                logits = flat_x @ rw[off:off + n].T + rb[off:off + n]
                p = jax.nn.sigmoid(logits)
                leaf = (leaf[:, :, None] * jnp.stack([1.0 - p, p], axis=2)).reshape(n_tok, 2 * n)
            return leaf
        b, s, dim = x.shape
        flat_x = x.reshape(b * s, dim)
        leaf_probs = _leaf_probs(flat_x, rw, rb)
        h = jnp.einsum('nd,edh->neh', flat_x, w1) + b1[None]
        h = jax.nn.gelu(h, approximate=False)
        y = jnp.einsum('neh,ehd->ned', h, w2) + b2[None]
        out = jnp.einsum('ned,ne->nd', y, leaf_probs)
        return out.reshape(b, s, dim)

    def _L1_attn_ref(tgt, W_in, conv_w, conv_b, dt_bias, A_log, D_skip, gnorm_w, W_out, n1_g, n1_b, ffn_w1, ffn_b1, ffn_w2, ffn_b2, n3_g, n3_b):
        import jax, jax.numpy as jnp
        import numpy as np
        D_MODEL = 128
        FF = 512
        D_STATE = 128
        D_CONV = 4
        EXPAND = 2
        D_INNER = EXPAND * D_MODEL
        HEADDIM = 64
        NHEADS = D_INNER // HEADDIM
        NGROUPS = 1
        CONV_DIM = D_INNER + 2 * NGROUPS * D_STATE
        D_IN_PROJ = 2 * D_INNER + 2 * NGROUPS * D_STATE + NHEADS
        B_SZ = 2
        SEQ = 512

        def _layernorm(x, g, b, eps=1e-05):
            m = jnp.mean(x, -1, keepdims=True)
            v = jnp.var(x, -1, keepdims=True)
            return (x - m) * jax.lax.rsqrt(v + eps) * g + b

        def _mamba2(x, W_in, conv_w, conv_b, dt_bias, A_log, D_skip, gnorm_w, W_out):
            Bb, S, _ = x.shape
            zxbcdt = x @ W_in
            z = zxbcdt[..., :D_INNER]
            xBC = zxbcdt[..., D_INNER:D_INNER + CONV_DIM]
            dt = zxbcdt[..., D_INNER + CONV_DIM:]
            xc = jnp.moveaxis(xBC, 1, 2)
            xp = jnp.pad(xc, ((0, 0), (0, 0), (D_CONV - 1, 0)))
            yc = sum((conv_w[None, :, k:k + 1] * xp[:, :, k:k + S] for k in range(D_CONV)))
            xBC = jax.nn.silu(jnp.moveaxis(yc, 1, 2) + conv_b)
            xs = xBC[..., :D_INNER].reshape(Bb, S, NHEADS, HEADDIM)
            Bc = xBC[..., D_INNER:D_INNER + D_STATE]
            Cc = xBC[..., D_INNER + D_STATE:]
            dt = jax.nn.softplus(dt + dt_bias)
            A = -jnp.exp(A_log)
            dA = jnp.exp(dt * A)
            tm = lambda a: jnp.moveaxis(a, 1, 0)

            def step(h, inp):
                dA_t, dt_t, B_t, C_t, x_t = inp
                h = h * dA_t[:, :, None, None] + (dt_t[:, :, None] * x_t)[..., None] * B_t[:, None, None, :]
                y_t = jnp.einsum('bhpn,bn->bhp', h, C_t)
                return (h, y_t)
            h0 = jnp.zeros((Bb, NHEADS, HEADDIM, D_STATE), x.dtype)
            _, ys = jax.lax.scan(step, h0, (tm(dA), tm(dt), tm(Bc), tm(Cc), tm(xs)))
            y = jnp.moveaxis(ys, 0, 1) + D_skip[None, None, :, None] * xs
            y = y.reshape(Bb, S, D_INNER)
            y = y * jax.nn.silu(z)
            y = y * jax.lax.rsqrt(jnp.mean(y * y, -1, keepdims=True) + 1e-05) * gnorm_w
            return y @ W_out
        t = tgt + _mamba2(tgt, W_in, conv_w, conv_b, dt_bias, A_log, D_skip, gnorm_w, W_out)
        t = _layernorm(t, n1_g, n1_b)
        h = jax.nn.gelu(t @ ffn_w1 + ffn_b1, approximate=False) @ ffn_w2 + ffn_b2
        return _layernorm(t + h, n3_g, n3_b)

    def _L1_ffn_ref(x, Wr, br, W1, b1, W2, b2):
        import jax, jax.numpy as jnp
        import numpy as np
        E, D, H = (8, 128, 512)
        B, N = (8, 128)
        b, n, d = x.shape
        xt = x.reshape(-1, d)
        route_prob = jax.nn.softmax(xt.astype(jnp.float32) @ Wr + br, axis=-1)
        routes = jnp.argmax(route_prob, axis=-1)
        p_max = jnp.max(route_prob, axis=-1)

        def expert_step(acc, inp):
            w1, bb1, w2, bb2, e = inp
            h = jax.nn.gelu(xt @ w1 + bb1, approximate=False)
            y = h @ w2 + bb2
            return (acc + y * (routes == e)[:, None].astype(y.dtype), None)
        out, _ = jax.lax.scan(expert_step, jnp.zeros_like(xt), (W1, b1, W2, b2, jnp.arange(E)))
        out = out * (p_max / jax.lax.stop_gradient(p_max))[:, None]
        return out.reshape(b, n, d)

    def _L2_attn_ref(inputs, WQ, WV, WU):
        import jax, jax.numpy as jnp
        import numpy as np
        N_HEADS = 8
        HEAD_SIZE = 64
        CONTEXT = 64
        D_MODEL = 128
        MASK_NEG = 1000000000.0
        B, T, D = inputs.shape
        H, _, S = WQ.shape
        Q = jnp.einsum('btd,hds->bhts', inputs, WQ)
        V = jnp.einsum('btd,hds->bhts', inputs, WV)
        scores = jnp.einsum('bhts,bhus->bhtu', Q, V) / jnp.sqrt(jnp.float32(S))
        idx = jnp.arange(T)
        band = jnp.abs(idx[:, None] - idx[None, :]) <= CONTEXT
        scores = scores - MASK_NEG * (~band).astype(scores.dtype)
        W = jax.nn.softmax(scores, axis=-1)
        C = jnp.einsum('bhtu,bhus->bhts', W, V)
        C = C.transpose(0, 2, 1, 3).reshape(B, T, H * S)
        return C @ WU

    def _L2_ffn_ref(x, Wg, W1, b1, W2, b2):
        import jax, jax.numpy as jnp
        import numpy as np
        B, S, D, H, O, E, TOPK = (4, 512, 128, 256, 128, 8, 2)
        Bsz, Seq, Din = x.shape
        T = Bsz * Seq
        xm = x.reshape(T, Din)
        probs = jax.nn.softmax(xm @ Wg, axis=-1)
        top_p, top_i = jax.lax.top_k(probs, TOPK)
        gates = jnp.zeros((T, E), dtype=probs.dtype).at[jnp.arange(T)[:, None], top_i].set(top_p)
        h = jax.nn.gelu(jnp.einsum('td,edh->teh', xm, W1) + b1[None])
        y = jnp.einsum('teh,eho->teo', h, W2) + b2[None]
        out = jnp.einsum('te,teo->to', gates, y)
        return out.reshape(Bsz, Seq, O)

    def _L3_attn_ref(x, wq, wk, wv, wo, gamma, beta):
        import jax, jax.numpy as jnp
        import numpy as np
        HEADS = 8
        DIM_HEAD = 64
        DIM = 128
        SCALE = DIM_HEAD ** (-0.5)
        BN_EPS = 1e-05
        b, p, d = x.shape
        h, e = (HEADS, DIM_HEAD)
        xg = x.reshape(b, p, h, d // h)
        q = jnp.einsum('bphc,hec->bhpe', xg, wq)
        k = jnp.einsum('bphc,hec->bhpe', xg, wk)
        v = jnp.einsum('bphc,hec->bhpe', xg, wv)
        dots = jnp.einsum('bhie,bhje->bhij', q, k) * SCALE
        attn = jax.nn.softmax(dots, axis=-1)
        out = jnp.einsum('bhij,bhje->bhie', attn, v)
        out = out.transpose(0, 2, 1, 3).reshape(b, p, h * e)
        out = jnp.einsum('bpi,di->bpd', out, wo)
        mean = out.mean(axis=(0, 1))
        var = out.var(axis=(0, 1))
        out = (out - mean) * jax.lax.rsqrt(var + BN_EPS) * gamma + beta
        return jax.nn.relu(out)

    def _L3_ffn_ref(x, r_w1, r_b1, r_w2, r_b2, wq0, wk0, wv0, wo0, wq1, wk1, wv1, wo1, wq2, wk2, wv2, wo2):
        import jax, jax.numpy as jnp
        import numpy as np
        D_MODEL = 128
        N_HEADS = 8
        KV_OPTS = (8, 4, 1)
        D_K = D_MODEL // N_HEADS

        def gqa(x, wq, wk, wv, wo, n_kv):
            B, S, _ = x.shape
            groups = N_HEADS // n_kv
            q = (x @ wq).reshape(B, S, N_HEADS, D_K).transpose(0, 2, 1, 3)
            k = (x @ wk).reshape(B, S, n_kv, D_K).transpose(0, 2, 1, 3)
            v = (x @ wv).reshape(B, S, n_kv, D_K).transpose(0, 2, 1, 3)
            k = jnp.repeat(k, groups, axis=1)
            v = jnp.repeat(v, groups, axis=1)
            scores = jnp.einsum('bhqd,bhkd->bhqk', q, k) / jnp.sqrt(jnp.float32(D_K))
            attn = jax.nn.softmax(scores, axis=-1)
            out = jnp.einsum('bhqk,bhkd->bhqd', attn, v)
            out = out.transpose(0, 2, 1, 3).reshape(B, S, D_MODEL)
            return out @ wo
        routing_input = x.mean(axis=1)
        logits = jax.nn.relu(routing_input @ r_w1 + r_b1) @ r_w2 + r_b2
        sel = jnp.argmax(jax.nn.softmax(logits, axis=-1), axis=-1)
        params = [(wq0, wk0, wv0, wo0), (wq1, wk1, wv1, wo1), (wq2, wk2, wv2, wo2)]
        out = jnp.zeros_like(x)
        for i, nkv in enumerate(KV_OPTS):
            yi = gqa(x, *params[i], nkv)
            mask = (sel == i)[:, None, None]
            out = jnp.where(mask, yi, out)
        return out
    h = _L0_tok_ref(x, L0_tok_w, L0_tok_b, 16)
    h = h + _L0_attn_ref(_layernorm(h, axis=-1), L0_attn_w_qkv, L0_attn_w_proj, L0_attn_b_proj, L0_attn_ln_gamma, L0_attn_ln_beta)
    h = h + _L0_ffn_ref(_layernorm(h, axis=-1), L0_ffn_rw, L0_ffn_rb, L0_ffn_w1, L0_ffn_b1, L0_ffn_w2, L0_ffn_b2)
    h = h + _L1_attn_ref(_layernorm(h, axis=-1), L1_attn_W_in, L1_attn_conv_w, L1_attn_conv_b, L1_attn_dt_bias, L1_attn_A_log, L1_attn_D_skip, L1_attn_gnorm_w, L1_attn_W_out, L1_attn_n1_g, L1_attn_n1_b, L1_attn_ffn_w1, L1_attn_ffn_b1, L1_attn_ffn_w2, L1_attn_ffn_b2, L1_attn_n3_g, L1_attn_n3_b)
    h = h + _L1_ffn_ref(_layernorm(h, axis=-1), L1_ffn_Wr, L1_ffn_br, L1_ffn_W1, L1_ffn_b1, L1_ffn_W2, L1_ffn_b2)
    h = h + _L2_attn_ref(_layernorm(h, axis=-1), L2_attn_WQ, L2_attn_WV, L2_attn_WU)
    h = h + _L2_ffn_ref(_layernorm(h, axis=-1), L2_ffn_Wg, L2_ffn_W1, L2_ffn_b1, L2_ffn_W2, L2_ffn_b2)
    h = h + _L3_attn_ref(_layernorm(h, axis=-1), L3_attn_wq, L3_attn_wk, L3_attn_wv, L3_attn_wo, L3_attn_gamma, L3_attn_beta)
    h = h + _L3_ffn_ref(_layernorm(h, axis=-1), L3_ffn_r_w1, L3_ffn_r_b1, L3_ffn_r_w2, L3_ffn_r_b2, L3_ffn_wq0, L3_ffn_wk0, L3_ffn_wv0, L3_ffn_wo0, L3_ffn_wq1, L3_ffn_wk1, L3_ffn_wv1, L3_ffn_wo1, L3_ffn_wq2, L3_ffn_wk2, L3_ffn_wv2, L3_ffn_wo2)
    return h

_drawn_inputs = setup_inputs


def setup_inputs(seed=0):
    import zlib

    import numpy as np

    out = dict(_drawn_inputs(seed))
    spreads = {'L0_attn_b_proj': (0.0, 0.1),
     'L0_attn_ln_gamma': (1.0, 0.2),
     'L0_attn_ln_beta': (0.0, 0.1),
     'L1_attn_conv_b': (0.0, 0.1),
     'L1_attn_D_skip': (1.0, 0.2),
     'L1_attn_gnorm_w': (1.0, 0.2),
     'L1_attn_n1_g': (1.0, 0.2),
     'L1_attn_n1_b': (0.0, 0.1),
     'L1_attn_ffn_b1': (0.0, 0.281),
     'L1_attn_ffn_b2': (0.0, 0.1),
     'L1_attn_n3_g': (1.0, 0.2),
     'L1_attn_n3_b': (0.0, 0.1),
     'L1_ffn_br': (0.0, 0.1),
     'L1_ffn_b1': (0.0, 0.399),
     'L1_ffn_b2': (0.0, 0.267),
     'L2_ffn_b1': (0.0, 0.8),
     'L2_ffn_b2': (0.0, 0.649),
     'L3_attn_gamma': (1.0, 0.2),
     'L3_attn_beta': (0.0, 0.422),
     'L3_ffn_r_b1': (0.0, 0.1),
     'L3_ffn_r_b2': (0.0, 0.472)}
    factors = {'L0_ffn_rb': 3.061,
     'L0_ffn_b2': 2.731,
     'L1_attn_dt_bias': 8.0,
     'L1_attn_A_log': 8.0,
     'L3_attn_wq': 8.0,
     'L3_attn_wk': 8.0,
     'L3_ffn_wq2': 8.0,
     'L3_ffn_wk2': 8.0,
     'L3_ffn_wv2': 5.014,
     'L3_ffn_wo2': 4.068}
    for name, (base, spread) in spreads.items():
        noise = np.random.default_rng([zlib.crc32(name.encode()), seed]).standard_normal(out[name].shape)
        drawn = base * np.exp(spread * noise) if base else spread * noise
        out[name] = jnp.asarray(drawn.astype(out[name].dtype))
    for name, factor in factors.items():
        out[name] = (out[name] * factor).astype(out[name].dtype)
    return out
```

```python
from contextlib import ExitStack, contextmanager

import numpy as np

import concourse.bass as bass
from concourse import mybir

F32 = mybir.dt.float32
BF16 = mybir.dt.bfloat16
ALU = mybir.AluOpType
ACT = mybir.ActivationFunctionType
AX = mybir.AxisListType.X

BATCH = 64
S = 36
D = 128
PATCH_K = 3 * 16 * 16
KC = PATCH_K // 128
TB = 3
P = TB * S
G = -(-BATCH // TB)
NH = 8
HD = 16
SLOT = 32
QUAD = 4
CHUNKS = [(c, min(QUAD, G - c)) for c in range(0, G, QUAD)]
EPS = 1e-5
NEG = -1.0e30


def steps(eng, step, depth):
    first = (depth + 2) // 2 * 2
    for t in range(first):
        step(t, t % 2)
    with eng.Fori(0, (G - first) // 2) as j:
        for u in range(2):
            step(j * 2 + (first + u), u)
    for t in range(G, G + depth - 1):
        step(t, t % 2)


def live(t, k):
    return not isinstance(t, int) or 0 <= t - k < G


def at_least(eng, sem, value):
    if not isinstance(value, int) or value > 0:
        eng.wait_ge(sem, value)


class Shared:
    pass


class Weights:

    def __init__(self, wv, scale, wqk=None, wo=None, own=None, factors=None):
        self.wqk, self.wv, self.wo, self.scale, self.own, self.factors = wqk, wv, wo, scale, own, factors
        self.fold = factors is not None


@contextmanager
def semaphores(nc, prefix):
    made = []
    with ExitStack() as ctx:
        def sem(name):
            made.append(ctx.enter_context(nc.semaphore(f"{prefix}_{name}")))
            return made[-1]
        yield sem
        with nc.Block() as block:
            @block.gpsimd
            def _(pool):
                for s in made:
                    pool.sem_clear(s)


def patch_phase(nc, m, io):
    with ExitStack() as ctx:
        sem = ctx.enter_context(semaphores(nc, "tok"))
        loaded = [sem(f"loaded{c}") for c in range(len(CHUNKS))]
        w_loaded = sem("w_loaded")
        proj_psum = sem("proj_psum")
        biased = sem("biased")
        turned = sem("turned")
        h_ready = sem("h_ready")
        pats = ctx.enter_context(nc.sbuf_tensor("pats", [128, KC, G * P], F32))
        tokw = ctx.enter_context(nc.sbuf_tensor("tokw", [128, KC * D], F32))
        bload = ctx.enter_context(nc.sbuf_tensor("bload", list(io["bconst"].shape), F32))
        hT = ctx.enter_context(nc.sbuf_tensor("tok_hT", [128, 2, QUAD * P], F32))
        block = ctx.enter_context(nc.Block())

        @block.sync
        def _(sp):
            sp.dma_start(m.const[:, :], io["const"]).then_inc(w_loaded, 16)
            sp.dma_start(tokw[:, :], io["tokw"]).then_inc(w_loaded, 16)
            for n, (c, k) in enumerate(CHUNKS):
                sp.dma_start(pats[:, :, c * P:(c + k) * P], io["patches"][:, :, c * P:(c + k) * P]).then_inc(loaded[n], 16)

        @block.tensor
        def _(pe):
            pe.wait_ge(w_loaded, 80)

            def project(n):
                c, k = CHUNKS[n]
                pe.wait_ge(loaded[n], 16)
                at_least(pe, biased, n - 1)
                for kc in range(KC):
                    mm = pe.matmul(m.bank[n % 2][:, 0:k * P], tokw[:, kc * D:(kc + 1) * D],
                                   pats[:, kc, c * P:(c + k) * P], start=(kc == 0), stop=(kc == KC - 1))
                mm.then_inc(proj_psum, 1)

            def turn(n):
                c, k = CHUNKS[n]
                pe.wait_ge(biased, n + 1)
                at_least(pe, h_ready, n - 1)
                for g in range(k):
                    mm = pe.transpose(m.bank[2 + n % 2][0:P, g * D:(g + 1) * D],
                                      hT[:, n % 2, g * P:(g + 1) * P], m.ident[:, :])
                mm.then_inc(turned, 1)

            project(0)
            for n in range(1, len(CHUNKS)):
                project(n)
                turn(n - 1)
            turn(len(CHUNKS) - 1)

        @block.scalar
        def _(act):
            act.dma_start(m.cols[:, :], io["cols"]).then_inc(w_loaded, 16)
            act.dma_start(m.rows[:, :], io["rows"]).then_inc(w_loaded, 16)
            act.dma_start(bload[:, :], io["bconst"]).then_inc(w_loaded, 16)
            act.wait_ge(w_loaded, 80)
            act.activation(m.bconst[:, :], bload[:, :], ACT.Copy)
            for n, (c, k) in enumerate(CHUNKS):
                act.wait_ge(proj_psum, n + 1)
                at_least(act, turned, n - 1)
                act.activation(hT[:, n % 2, 0:k * P], m.bank[n % 2][:, 0:k * P], ACT.Identity,
                               bias=m.col("tok_b")).then_inc(biased, 1)

        @block.vector
        def _(dve):
            for n, (c, k) in enumerate(CHUNKS):
                dve.wait_ge(turned, n + 1)
                dve.tensor_copy(m.H[:, c * D:(c + k) * D], m.bank[2 + n % 2][0:P, 0:k * D]).then_inc(h_ready, 1)
            dve.wait_ge(h_ready, len(CHUNKS))


def attention_phase(nc, m, name, w, hd=HD, nx=1, ending="add", masks=False):
    row = SLOT if hd == HD else hd
    heads_tile = 128 // row
    tiles = NH // heads_tile
    rounds = 2 * tiles // 4
    head_at = [n % tiles * heads_tile + n // tiles for n in range(NH)]
    post_norm = ending == "post_norm"
    depth = 7 if post_norm else 6
    with ExitStack() as ctx:
        sem = ctx.enter_context(semaphores(nc, name))
        sb = lambda s, shape, dt=F32: ctx.enter_context(nc.sbuf_tensor(f"{name}_{s}", shape, dt))
        w_loaded = sem("w_loaded")
        stat_chain = sem("stat_chain")
        var_eps = sem("var_eps")
        rstd_ready = sem("rstd_ready")
        xbase = sem("xbase")
        xn_ready = sem("xn_ready")
        xt_psum = sem("xt_psum")
        xt_ready = sem("xt_ready")
        qk_psum = sem("qk_psum")
        qk_ready = sem("qk_ready")
        v_psum = sem("v_psum")
        v_ready = sem("v_ready")
        s_psum = sem("s_psum")
        max_ready = sem("max_ready")
        shift_ready = sem("shift_ready")
        exps = sem("exps")
        pt_psum = sem("pt_psum")
        pt_ready = sem("pt_ready")
        rec_ready = sem("rec_ready")
        recs_ready = sem("recs_ready")
        o_psum = sem("o_psum")
        o_done = sem("o_done")
        y_psum = sem("y_psum")
        y_sum = sem("y_sum")
        y_done = sem("y_done")
        o_read = sem("o_read")
        pads_set = sem("pads_set")
        wqk = sb("wqk", [128, nx, 2 * tiles * 128])
        wv = sb("wv", [128, nx, NH * hd])
        wo = sb("wo", [128, tiles, nx * D])
        bn6 = sb("bn6", [P, 2, 6])
        mv = sb("mv", [P, 2, 2])
        ve = sb("ve", [P, 2, 1])
        rstd = sb("rstd", [P, 2, 1])
        xn = sb("xn", [P, 2, nx, D])
        xT = sb("xT", [128, 2, nx, P])
        qk = sb("qk", [128, 2, 2 * tiles, P])
        v = sb("v", [P, 2, NH, row])
        mx = sb("mx", [P, NH])
        shift = sb("shift", [P, 2, NH])
        total = sb("total", [P, 2, NH])
        E = sb("E", [P, 2, NH, P])
        pT = sb("pT", [P, 2, NH, P])
        rec = sb("rec", [P, NH])
        recs = sb("recs", [P, 2, NH, row])
        recT = sb("recT", [128, tiles * P])
        oT = sb("oT", [128, tiles * P])
        if w.fold:
            f_in = sb("f_in", [128, 128 + 256 + 256 + 4 * 256 + 4 * 128])
            f_wk, f_wq, f_same = f_in[:, 0:128], f_in[:, 128:384], f_in[:, 384:640]
            f_wv = lambda c, tile: f_in[:, 640 + c * 256 + tile * 128:640 + c * 256 + (tile + 1) * 128]
            f_wo = lambda c: f_in[:, 1664 + c * 128:1664 + (c + 1) * 128]
            fold_psum = sem("fold_psum")
            folded = sem("folded")
        if masks:
            xb = sb("xb", [P, D])
        if post_norm:
            xres_ready = sem("xres_ready")
            post_stats = sem("post_stats")
            post_eps = sem("post_eps")
            post_rstd = sem("post_rstd")
            post_normed = sem("post_normed")
            post_scaled = sem("post_scaled")
            h_done = sem("h_done")
            yt = sb("yt", [P, 2, D])
            bnb = sb("bnb", [P, 2, 6])
            mvb = sb("mvb", [P, 2, 2])
            veb = sb("veb", [P, 2, 1])
            rstdb = sb("rstdb", [P, 2, 1])
        xbank, obank, ptbank, sbank = m.bank[0], m.bank[2], m.bank[3], m.quad_bank
        qkbank = [m.bank[1], m.quad_bank[:, 2, :]][0:rounds]
        o_at = obank[:, 0:tiles * P]
        z_at = obank[:, tiles * P:2 * tiles * P] if 2 * tiles * P <= 512 else m.quad_bank[:, 3, 0:tiles * P]
        scores = sbank[0:P, 0:heads_tile, 0:tiles * P].rearrange("p b (s j) -> p b s j", s=tiles)
        block = ctx.enter_context(nc.Block())

        @block.sync
        def _(sp):
            if not w.fold:
                sp.dma_start(wqk[:, :, :], w.wqk).then_inc(w_loaded, 16)
                sp.dma_start(wo[:, :, :], w.wo).then_inc(w_loaded, 16)
            else:
                sp.dma_start(wqk[:, 0, 0:256], w.own).then_inc(w_loaded, 16)
                sp.dma_start(f_in[:, :], w.factors).then_inc(w_loaded, 16)
            sp.dma_start(wv[:, :, :], w.wv).then_inc(w_loaded, 16)

        @block.gpsimd
        def _(pool):
            def step(t, par):
                q = 1 - par
                if live(t, 0):
                    g = t
                    pool.wait_ge(stat_chain, g * 2 + 2)
                    at_least(pool, rstd_ready, g)
                    pool.tensor_tensor(ve[:, par, :], mv[:, par, 1:2], m.eps[0:P, :], ALU.add).then_inc(var_eps, 1)
                    pool.wait_ge(var_eps, g + 1)
                    at_least(pool, xn_ready, (g - 1) * nx)
                    pool.tensor_tensor(rstd[:, par, :], ve[:, par, :], m.mhalf[0:P, :], ALU.pow).then_inc(rstd_ready, 1)
                if post_norm and live(t, 1):
                    g = t - 1
                    pool.wait_ge(xn_ready, g + 1)
                    pool.tensor_tensor(m.XN[:, bass.ts(g, D)], xn[:, q, 0, :], m.row("a0_b_proj"), ALU.add).then_inc(xres_ready, 1)
                if post_norm and live(t, 6):
                    g = t - 6
                    pool.wait_ge(post_normed, g + 1)
                    pool.tensor_tensor(yt[:, par, :], yt[:, par, :], m.row("a0_gamma"), ALU.mult).then_inc(post_scaled, 1)
                    pool.wait_ge(post_scaled, g * 2 + 1)
                    pool.tensor_tensor(yt[:, par, :], yt[:, par, :], m.row("a0_beta"), ALU.add).then_inc(post_scaled, 1)
                    pool.wait_ge(post_scaled, g * 2 + 2)
                    h = m.H[:, bass.ts(g, D)]
                    pool.tensor_tensor(h, h, yt[:, par, :], ALU.add).then_inc(h_done, 1)
                if post_norm and live(t, 5):
                    g = t - 5
                    pool.wait_ge(post_stats, g * 2 + 2)
                    pool.tensor_tensor(veb[:, q, :], mvb[:, q, 1:2], m.eps[0:P, :], ALU.add).then_inc(post_eps, 1)
                    pool.wait_ge(post_eps, g + 1)
                    pool.tensor_tensor(rstdb[:, q, :], veb[:, q, :], m.mhalf[0:P, :], ALU.pow).then_inc(post_rstd, 1)
            steps(pool, step, depth)

        @block.tensor
        def _(pe):
            pe.wait_ge(w_loaded, 48)
            if w.fold:
                pe.matmul(m.bank[0][:, 0:256], f_wk, f_wq, start=True, stop=True).then_inc(fold_psum, 1)
                for tile in range(tiles):
                    for c in range(4):
                        mm = pe.matmul(m.bank[1][:, tile * 128:(tile + 1) * 128], f_wv(c, tile), f_wo(c), start=(c == 0), stop=(c == 3))
                mm.then_inc(fold_psum, 1)
                pe.wait_ge(folded, 2)
            pe.wait_ge(pads_set, 1)

            def probabilities(g, q, half):
                pe.wait_ge(exps, g * 2 + (half + 1))
                at_least(pe, pt_ready, g * 2 + half)
                for n in range(4 * half, 4 * half + 4):
                    mm = pe.transpose(ptbank[0:P, n % 4 * P:(n % 4 + 1) * P], E[:, q, n, :], m.ident[0:P, 0:P])
                mm.then_inc(pt_psum, 1)

            def queries_keys(g, par, r):
                at_least(pe, qk_ready, g * rounds + (r - (rounds - 1)))
                for n in range(4):
                    for x in range(nx):
                        c = (4 * r + n) * 128
                        mm = pe.matmul(qkbank[r][:, n * P:(n + 1) * P], wqk[:, x, c:c + 128],
                                       xT[:, par, x, :], start=(x == 0), stop=(x == nx - 1))
                mm.then_inc(qk_psum, 1)

            def scores_half(g, q, half):
                pe.wait_ge(qk_ready, g * rounds + rounds)
                at_least(pe, exps, g * 2 + (half - 1))
                banks = range(heads_tile // 2 * half, heads_tile // 2 * (half + 1))
                for b in banks:
                    pe.matmul(sbank[0:P, b, 0:tiles * P], m.img[row * b:row * b + TB, :],
                              m.not_img[row * b:row * b + TB, 0:tiles * P], start=True, stop=False, skip_group_check=True)
                for tile in range(tiles):
                    for b in banks:
                        mm = pe.matmul(sbank[0:P, b, tile * P:(tile + 1) * P], qk[row * b:row * b + hd, q, tile, :],
                                       qk[row * b:row * b + hd, q, tiles + tile, :], start=False, stop=(tile == tiles - 1),
                                       skip_group_check=True)
                mm.then_inc(s_psum, 1)

            def step(t, par):
                q = 1 - par
                if live(t, 3):
                    scores_half(t - 3, q, 0)
                if live(t, 2):
                    g = t - 2
                    pe.wait_ge(xn_ready, g * nx + nx)
                    at_least(pe, v_ready, g - 1)
                    for x in range(nx):
                        mm = pe.transpose(xbank[:, x * P:(x + 1) * P], xn[:, par, x, :], m.ident[0:P, 0:P])
                    mm.then_inc(xt_psum, 1)
                if live(t, 4):
                    probabilities(t - 4, par, 0)
                if live(t, 5):
                    g = t - 5
                    pe.wait_ge(o_done, g + 1)
                    if live(t, 2):
                        pe.wait_ge(xt_ready, g + 4)
                    elif live(t, 4):
                        pe.wait_ge(v_ready, g + 2)
                    for tile in range(tiles):
                        o = oT[:, tile * P:(tile + 1) * P]
                        if ending == "channels":
                            mm = pe.matmul(xbank[:, 0:P], wo[:, tile, :], o, start=(tile == 0), stop=(tile == tiles - 1))
                        else:
                            mm = pe.matmul(xbank[0:P, 0:nx * D], o, wo[:, tile, :], start=(tile == 0), stop=(tile == tiles - 1))
                    mm.then_inc(y_psum, 1)
                if live(t, 3):
                    scores_half(t - 3, q, 1)
                if live(t, 2):
                    pe.wait_ge(xt_ready, t - 2 + 1)
                    queries_keys(t - 2, par, 0)
                if live(t, 4):
                    probabilities(t - 4, par, 1)
                if live(t, 3):
                    g = t - 3
                    if live(t, 5):
                        pe.wait_ge(y_done, g - 1)
                    elif live(t, 2):
                        pe.wait_ge(xt_ready, g + 2)
                    for x in range(nx):
                        mm = pe.matmul(xbank[0:P, 0:NH * hd], xT[:, q, x, :], wv[:, x, :], start=(x == 0), stop=(x == nx - 1))
                    mm.then_inc(v_psum, 1)
                if live(t, 2) and rounds == 2:
                    queries_keys(t - 2, par, 1)
                if live(t, 4):
                    g = t - 4
                    at_least(pe, o_done, g)
                    pe.wait_ge(recs_ready, g + 1)
                    for tile in range(tiles):
                        pe.matmul(z_at[:, tile * P:(tile + 1) * P],
                                  recs[:, par, tile * heads_tile:(tile + 1) * heads_tile, :].rearrange("p n c -> p (n c)"),
                                  m.ident[0:P, 0:P], start=True, stop=True)
                    pe.wait_ge(pt_ready, g * 2 + 2)
                    pe.wait_ge(v_ready, g + 1)
                    for tile in range(tiles):
                        for r in range(heads_tile):
                            h = tile * heads_tile + r
                            mm = pe.matmul(o_at[row * r:row * (r + 1), tile * P:(tile + 1) * P], v[:, par, h, :],
                                           pT[:, par, head_at.index(h), :], start=True, stop=True)
                    mm.then_inc(o_psum, 1)
            steps(pe, step, depth)

        @block.scalar
        def _(act):
            act.wait_ge(pads_set, 1)

            def turned(g, par, half):
                act.wait_ge(pt_psum, g * 2 + half + 1)
                at_least(act, o_psum, g - 1)
                act.activation(pT[:, par, 4 * half:4 * half + 4, :].rearrange("p n j -> p (n j)"),
                               ptbank[0:P, 0:4 * P], ACT.Copy).then_inc(pt_ready, 1)

            def exponentials(g, q, half):
                act.wait_ge(shift_ready, g * 2 + half + 1)
                at_least(act, pt_psum, (g - 1) * 2)
                at_least(act, rec_ready, g - 1)
                for n in range(4 * half, 4 * half + 4):
                    e = act.activation(E[:, q, n, :], scores[:, n // tiles, n % tiles, :], ACT.Exp, scale=w.scale,
                                       bias=shift[:, q, n:n + 1], accum_out=total[:, q, n:n + 1])
                e.then_inc(exps, 1)

            def queries_keys(g, par, r):
                act.wait_ge(qk_psum, g * rounds + r + 1)
                at_least(act, s_psum, (g - 1) * 2)
                act.activation(qk[:, par, 4 * r:4 * r + 4, :].rearrange("p n j -> p (n j)"), qkbank[r][:, 0:4 * P],
                               ACT.Copy).then_inc(qk_ready, 1)

            def step(t, par):
                q = 1 - par
                if live(t, 2):
                    g = t - 2
                    act.wait_ge(xt_psum, g + 1)
                    at_least(act, v_psum, g - 1)
                    act.activation(xT[:, par, :, :].rearrange("p x j -> p (x j)"), xbank[:, 0:nx * P], ACT.Copy).then_inc(xt_ready, 1)
                if live(t, 4):
                    turned(t - 4, par, 0)
                if live(t, 3):
                    exponentials(t - 3, q, 0)
                if live(t, 2):
                    queries_keys(t - 2, par, 0)
                if live(t, 4):
                    turned(t - 4, par, 1)
                if live(t, 3):
                    g = t - 3
                    act.wait_ge(v_psum, g + 1)
                    at_least(act, o_psum, g - 1)
                    act.activation(v[:, q, :, 0:hd], xbank[0:P, 0:NH * hd].rearrange("p (n c) -> p n c", n=NH),
                                   ACT.Copy).then_inc(v_ready, 1)
                if live(t, 2) and rounds == 2:
                    queries_keys(t - 2, par, 1)
                if live(t, 3):
                    exponentials(t - 3, q, 1)
            steps(act, step, depth)

        @block.vector
        def _(dve):
            if w.fold:
                dve.wait_ge(fold_psum, 1)
                dve.wait_ge(w_loaded, 48)
                dve.tensor_tensor(wqk[:, 0, 256:512], m.bank[0][:, 0:256], f_same, ALU.mult).then_inc(folded, 1)
                dve.wait_ge(fold_psum, 2)
                dve.tensor_copy(wo[:, :, :].rearrange("p t d -> p (t d)"), m.bank[1][:, 0:tiles * 128]).then_inc(folded, 1)
            if row > hd:
                dve.memset(v[:, :, :, hd:row].rearrange("p a n c -> p (a n) c"), 0.0)
            dve.drain().then_inc(pads_set, 1)

            def maxima(g, q, half):
                dve.wait_ge(s_psum, g * 2 + (half + 1))
                banks = heads_tile // 2
                top = mx[:, 4 * half:4 * half + 4]
                at_least(dve, shift_ready, g * 2 + (half - 1))
                dve.tensor_reduce(top.rearrange("p (b s) -> p b s", s=tiles),
                                  scores[:, banks * half:banks * (half + 1), :, :], AX, ALU.max).then_inc(max_ready, 1)
                dve.wait_ge(max_ready, g * 2 + half + 1)
                at_least(dve, exps, (g - 1) * 2)
                dve.tensor_scalar(shift[:, q, 4 * half:4 * half + 4], top, -w.scale, None, ALU.mult).then_inc(shift_ready, 1)

            def step(t, par):
                q = 1 - par
                if live(t, 3):
                    maxima(t - 3, q, 0)
                if live(t, 5):
                    g = t - 5
                    dve.wait_ge(y_psum, g + 1)
                    h = m.H[:, bass.ts(g, D)]
                    if masks:
                        for x in range(nx):
                            if x:
                                dve.wait_ge(y_sum, g * (nx - 1) + x)
                            dve.scalar_tensor_tensor(out=h, in0=xbank[0:P, x * D:(x + 1) * D], scalar=m.MSK[:, bass.ds(g * nx + x, 1)],
                                                     in1=h, op0=ALU.mult, op1=ALU.add).then_inc(y_sum if x < nx - 1 else y_done, 1)
                    elif ending == "add":
                        dve.tensor_tensor(h, h, xbank[0:P, 0:D], ALU.add).then_inc(y_done, 1)
                    elif ending == "channels":
                        dve.tensor_copy(m.YT[:, bass.ts(g, P)], xbank[:, 0:P]).then_inc(y_done, 1)
                    else:
                        dve.wait_ge(xres_ready, g + 1)
                        at_least(dve, h_done, g - 1)
                        dve.tensor_tensor(yt[:, q, :], m.XN[:, bass.ts(g, D)], xbank[0:P, 0:D], ALU.add).then_inc(y_done, 1)
                if live(t, 4):
                    g = t - 4
                    dve.wait_ge(exps, g * 2 + 2)
                    at_least(dve, recs_ready, g)
                    dve.reciprocal(rec[:, :], total[:, par, :]).then_inc(rec_ready, 1)
                    dve.wait_ge(rec_ready, g + 1)
                    at_least(dve, o_psum, g - 1)
                    dve.tensor_copy(recs[:, par, :, :].rearrange("p (t r) c -> p t r c", t=tiles),
                                    rec[:, :].rearrange("p (r t) -> p t r", t=tiles).unsqueeze(3)
                                    .broadcast_to([P, tiles, heads_tile, row])).then_inc(recs_ready, 1)
                if live(t, 1):
                    g = t - 1
                    dve.wait_ge(rstd_ready, g + 1)
                    at_least(dve, xt_psum, g - 1)
                    if post_norm:
                        at_least(dve, xres_ready, g - 1)
                    x0 = xb[:, :] if masks else xn[:, q, 0, :]
                    if masks:
                        at_least(dve, xn_ready, g * nx)
                    dve.tensor_scalar(x0, m.H[:, bass.ts(g, D)], mv[:, q, 0:1], rstd[:, q, :],
                                      ALU.subtract, ALU.mult).then_inc(xbase if masks else xn_ready, 1)
                    if masks:
                        dve.wait_ge(xbase, g + 1)
                        for x in range(nx):
                            dve.tensor_scalar(xn[:, q, x, :], xb[:, :], m.MSK[:, bass.ds(g * nx + x, 1)], None,
                                              ALU.mult).then_inc(xn_ready, 1)
                if live(t, 3):
                    maxima(t - 3, q, 1)
                if post_norm and live(t, 6):
                    g = t - 6
                    dve.wait_ge(post_rstd, g + 1)
                    dve.tensor_scalar(yt[:, par, :], yt[:, par, :], mvb[:, par, 0:1], rstdb[:, par, :],
                                      ALU.subtract, ALU.mult).then_inc(post_normed, 1)
                if live(t, 0):
                    g = t
                    at_least(dve, var_eps, g - 1)
                    at_least(dve, xn_ready, (g - 1) * nx)
                    dve.bn_stats(bn6[:, par, :], m.H[:, bass.ts(g, D)]).then_inc(stat_chain, 1)
                    dve.drain()
                    dve.bn_aggr(mv[:, par, :], bn6[:, par, :]).then_inc(stat_chain, 1)
                if post_norm and live(t, 5):
                    g = t - 5
                    dve.wait_ge(y_done, g + 1)
                    dve.bn_stats(bnb[:, q, :], yt[:, q, :]).then_inc(post_stats, 1)
                    dve.drain()
                    dve.bn_aggr(mvb[:, q, :], bnb[:, q, :]).then_inc(post_stats, 1)
                if live(t, 4):
                    g = t - 4
                    dve.wait_ge(o_psum, g + 1)
                    at_least(dve, o_done, g)
                    dve.tensor_copy(recT[:, :], z_at).then_inc(o_read, 1)
                    dve.wait_ge(o_read, g + 1)
                    at_least(dve, y_psum, g)
                    dve.tensor_tensor(oT[:, :], o_at, recT[:, :], ALU.mult).then_inc(o_done, 1)
            steps(dve, step, depth)
            dve.wait_ge(y_done, G)


def prepare_phase(nc, m, name, router=None, bias=None, width=8, keep=False, means=False):
    with ExitStack() as ctx:
        sem = ctx.enter_context(semaphores(nc, name))
        sb = lambda s, shape, dt=F32: ctx.enter_context(nc.sbuf_tensor(f"{name}_{s}", shape, dt))
        w_loaded = sem("w_loaded")
        stat_chain = sem("stat_chain")
        var_eps = sem("var_eps")
        rstd_ready = sem("rstd_ready")
        xn_ready = sem("xn_ready")
        xt_psum = sem("xt_psum")
        xt_ready = sem("xt_ready")
        kept = sem("kept")
        lg_psum = sem("lg_psum")
        lg_ready = sem("lg_ready")
        mean_ready = sem("mean_ready")
        bn6 = sb("bn6", [P, 2, 6])
        mv = sb("mv", [P, 2, 2])
        ve = sb("ve", [P, 2, 1])
        rstd = sb("rstd", [P, 2, 1])
        xn = sb("xn", [P, 2, D])
        xT = sb("xT", [128, 2, P])
        wr = sb("wr", [128, width]) if router is not None else None
        keeps = 2 if keep else 1
        block = ctx.enter_context(nc.Block())

        @block.sync
        def _(sp):
            if router is not None:
                sp.dma_start(wr[:, :], router).then_inc(w_loaded, 16)

        @block.gpsimd
        def _(pool):
            def step(t, par):
                q = 1 - par
                if live(t, 0):
                    g = t
                    pool.wait_ge(stat_chain, g * 2 + 2)
                    at_least(pool, rstd_ready, g)
                    pool.tensor_tensor(ve[:, par, :], mv[:, par, 1:2], m.eps[0:P, :], ALU.add).then_inc(var_eps, 1)
                    pool.wait_ge(var_eps, g + 1)
                    at_least(pool, xn_ready, g - 1)
                    pool.tensor_tensor(rstd[:, par, :], ve[:, par, :], m.mhalf[0:P, :], ALU.pow).then_inc(rstd_ready, 1)
                if live(t, 2):
                    g = t - 2
                    pool.wait_ge(xt_ready, g + 1)
                    pool.tensor_copy(m.XT[:, bass.ts(g, P)], xT[:, par, :]).then_inc(kept, 1)
                    if keep:
                        pool.tensor_copy(m.XN[:, bass.ts(g, D)], xn[:, par, :]).then_inc(kept, 1)
            steps(pool, step, 3)

        @block.tensor
        def _(pe):
            if router is not None:
                pe.wait_ge(w_loaded, 16)

            def step(t, par):
                q = 1 - par
                if live(t, 1):
                    g = t - 1
                    pe.wait_ge(xn_ready, g + 1)
                    at_least(pe, xt_ready, g - 1)
                    pe.transpose(m.bank[q][:, 0:P], xn[:, q, :], m.ident[0:P, 0:P]).then_inc(xt_psum, 1)
                if router is not None and live(t, 2):
                    g = t - 2
                    pe.wait_ge(xt_ready, g + 1)
                    at_least(pe, lg_ready, g - 1)
                    pe.matmul(m.bank[2 + par][0:P, 0:width], xT[:, par, :], wr[:, :], start=True, stop=True).then_inc(lg_psum, 1)
            steps(pe, step, 3)

        @block.scalar
        def _(act):
            def step(t, par):
                q = 1 - par
                if live(t, 1):
                    g = t - 1
                    act.wait_ge(xt_psum, g + 1)
                    at_least(act, kept, (g - 1) * keeps)
                    if router is not None:
                        at_least(act, lg_psum, g - 1)
                    if means:
                        at_least(act, mean_ready, g - 1)
                    act.activation(xT[:, q, :], m.bank[q][:, 0:P], ACT.Copy).then_inc(xt_ready, 1)
            steps(act, step, 3)

        @block.vector
        def _(dve):
            def step(t, par):
                q = 1 - par
                if live(t, 0):
                    g = t
                    at_least(dve, var_eps, g - 1)
                    at_least(dve, xn_ready, g - 1)
                    dve.bn_stats(bn6[:, par, :], m.H[:, bass.ts(g, D)]).then_inc(stat_chain, 1)
                    dve.drain()
                    dve.bn_aggr(mv[:, par, :], bn6[:, par, :]).then_inc(stat_chain, 1)
                if live(t, 1):
                    g = t - 1
                    dve.wait_ge(rstd_ready, g + 1)
                    at_least(dve, xt_psum, g - 1)
                    if keep:
                        at_least(dve, kept, (g - 1) * 2)
                    dve.tensor_scalar(xn[:, q, :], m.H[:, bass.ts(g, D)], mv[:, q, 0:1], rstd[:, q, :],
                                      ALU.subtract, ALU.mult).then_inc(xn_ready, 1)
                if live(t, 2):
                    g = t - 2
                    if router is not None:
                        dve.wait_ge(lg_psum, g + 1)
                        dve.tensor_tensor(m.LG[:, bass.ts(g, width)], m.bank[2 + par][0:P, 0:width], bias, ALU.add).then_inc(lg_ready, 1)
                    if means:
                        dve.wait_ge(xt_ready, g + 1)
                        dve.tensor_reduce(m.MEANS[:, bass.ds(g * TB, TB)], xT[:, par, :].rearrange("p (b s) -> p b s", s=S),
                                          AX, ALU.add).then_inc(mean_ready, 1)
            steps(dve, step, 3)


def chained(eng, sem):
    count = [0]

    def then(instruction):
        count[0] += 1
        instruction.then_inc(sem, 1)
        eng.wait_ge(sem, count[0])
    return then


def tree_gates(nc, m, name):
    with ExitStack() as ctx:
        sem = ctx.enter_context(semaphores(nc, name))
        own = sem("chain")
        sig = sem("sigmoid")
        left = ctx.enter_context(nc.sbuf_tensor(f"{name}_left", [P, G, 8], F32))
        right = ctx.enter_context(nc.sbuf_tensor(f"{name}_right", [P, G, 8], F32))
        lv1 = ctx.enter_context(nc.sbuf_tensor(f"{name}_lv2", [P, G, 4], F32))
        block = ctx.enter_context(nc.Block())

        @block.scalar
        def _(act):
            act.activation(right[:, :, :].rearrange("p g e -> p (g e)"), m.LG[:, :], ACT.Sigmoid).then_inc(sig, 1)

        @block.vector
        def _(dve):
            then = chained(dve, own)
            dve.wait_ge(sig, 1)
            then(dve.tensor_scalar(left[:, :, :], right[:, :, :], -1.0, 1.0, ALU.mult, ALU.add))
            gate = m.GATE[:, :].rearrange("p (g e) -> p g e", e=8)
            for i in range(2):
                up = (left, right)[i][:, :, 0:1]
                for side in range(2):
                    then(dve.tensor_tensor(lv1[:, :, 2 * i + side:2 * i + side + 1], up, (left, right)[side][:, :, 1 + i:2 + i], ALU.mult))
            for side in range(2):
                then(dve.tensor_tensor(gate[:, :, side:8:2], lv1[:, :, :], (left, right)[side][:, :, 3:7], ALU.mult))


def first_best(dve, m, then, dst, src, tmp, top, shape):
    w = shape[-1]
    then(dve.tensor_reduce(top, src, AX, ALU.max))
    then(dve.tensor_tensor(tmp, src, top.unsqueeze(2).broadcast_to(shape), ALU.is_ge))
    then(dve.tensor_tensor(tmp, tmp, m.rank[0:shape[0], 0:w].unsqueeze(1).broadcast_to(shape), ALU.mult))
    then(dve.tensor_reduce(top, tmp, AX, ALU.max))
    then(dve.tensor_tensor(dst, tmp, top.unsqueeze(2).broadcast_to(shape), ALU.is_equal))


def best_gates(nc, m, name, best):
    with ExitStack() as ctx:
        sb = lambda s, shape: ctx.enter_context(nc.sbuf_tensor(f"{name}_{s}", shape, F32))
        sem = ctx.enter_context(semaphores(nc, name))
        own = sem("chain")
        exped = sem("exped")
        shifted = sem("shifted")
        top, tot = sb("top", [P, G]), sb("tot", [P, G])
        pr, one, two, tmp = (sb(s, [P, G, 8]) for s in ("pr", "one", "two", "tmp"))
        block = ctx.enter_context(nc.Block())
        shape = [P, G, 8]
        lg = m.LG[:, :].rearrange("p (g e) -> p g e", e=8)
        gate = m.GATE[:, :].rearrange("p (g e) -> p g e", e=8)
        wide = lambda x: x[:, :].unsqueeze(2).broadcast_to(shape)

        @block.scalar
        def _(act):
            act.wait_ge(shifted, 1)
            act.activation(pr[:, :, :].rearrange("p g e -> p (g e)"), pr[:, :, :].rearrange("p g e -> p (g e)"), ACT.Exp).then_inc(exped, 1)

        @block.vector
        def _(dve):
            then = chained(dve, own)
            then(dve.tensor_reduce(top[:, :], lg, AX, ALU.max))
            dve.tensor_tensor(pr[:, :, :], lg, wide(top), ALU.subtract).then_inc(shifted, 1)
            dve.wait_ge(exped, 1)
            then(dve.tensor_reduce(tot[:, :], pr[:, :, :], AX, ALU.add))
            then(dve.reciprocal(tot[:, :], tot[:, :]))
            then(dve.tensor_tensor(pr[:, :, :], pr[:, :, :], wide(tot), ALU.mult))
            first_best(dve, m, then, one[:, :, :], pr[:, :, :], tmp[:, :, :], top[:, :], shape)
            if best == 1:
                then(dve.tensor_tensor(pr[:, :, :], pr[:, :, :], one[:, :, :], ALU.mult))
                then(dve.tensor_reduce(top[:, :], pr[:, :, :], AX, ALU.max))
                then(dve.reciprocal(tot[:, :], top[:, :]))
                then(dve.tensor_tensor(top[:, :], top[:, :], tot[:, :], ALU.mult))
                then(dve.tensor_tensor(gate, one[:, :, :], wide(top), ALU.mult))
            else:
                then(dve.scalar_tensor_tensor(out=two[:, :, :], in0=one[:, :, :], scalar=-2.0, in1=pr[:, :, :], op0=ALU.mult, op1=ALU.add))
                first_best(dve, m, then, two[:, :, :], two[:, :, :], tmp[:, :, :], top[:, :], shape)
                then(dve.tensor_tensor(one[:, :, :], one[:, :, :], two[:, :, :], ALU.add))
                then(dve.tensor_tensor(gate, pr[:, :, :], one[:, :, :], ALU.mult))


def experts_phase(nc, m, name, w1, w2, b1, func, experts, chunks, b2=None, dst=None):
    nb = len(CHUNKS)
    before = 0 if b2 is None else G
    with ExitStack() as ctx:
        sem = ctx.enter_context(semaphores(nc, name))
        sb = lambda s, shape, dt=F32: ctx.enter_context(nc.sbuf_tensor(f"{name}_{s}", shape, dt))
        loaded = [sem("loaded0"), sem("loaded1")]
        b_loaded = sem("b_loaded")
        hid_psum = sem("hid_psum")
        hid_ready = sem("hid_ready")
        y_psum = sem("y_psum")
        y_used = sem("y_used")
        w1s = sb("w1s", [128, 2, chunks * 128])
        w2s = sb("w2s", [128, 2, chunks * 128])
        b1s = sb("b1s", [128, 2, chunks])
        hid = sb("hid", [128, 2, chunks, QUAD * P])
        if b2 is not None:
            b2s = sb("b2s", [8, D])
            gs = sb("gs", [P, 2, 8])
            gT = sb("gT", [8, 2, P])
            gs_ready = sem("gs_ready")
            gt_psum = sem("gt_psum")
            gt_ready = sem("gt_ready")
            gb_psum = sem("gb_psum")
        block = ctx.enter_context(nc.Block())

        @block.sync
        def _(sp):
            if b2 is not None:
                sp.dma_start(b2s[:, :], b2).then_inc(b_loaded, 16)

            def load(e, u):
                sp.dma_start(b1s[:, u, :], b1[bass.ds(e, 1), :, :].rearrange("e p n -> (e p) n")).then_inc(loaded[u], 16)
                sp.dma_start(w1s[:, u, :], w1[bass.ds(e, 1), :, :].rearrange("e p n -> (e p) n")).then_inc(loaded[u], 16)
                sp.dma_start(w2s[:, u, :], w2[bass.ds(e, 1), :, :].rearrange("e p n -> (e p) n")).then_inc(loaded[u], 16)
            for e in range(min(2, experts)):
                load(e, e)
            if experts > 2:
                with sp.Fori(1, experts // 2) as j:
                    for u in range(2):
                        sp.wait_ge(y_psum, (j * 2 + (u - 1)) * nb)
                        load(j * 2 + u, u)

        if b2 is not None:
            @block.gpsimd
            def _(pool):
                def step(t, par):
                    if live(t, 0):
                        at_least(pool, gt_psum, t - 1)
                        pool.tensor_copy(gs[:, par, :], m.GATE[:, bass.ts(t, 8)]).then_inc(gs_ready, 1)
                steps(pool, step, 2)

        @block.tensor
        def _(pe):
            if b2 is not None:
                pe.wait_ge(b_loaded, 16)

            def bias_step(t, par):
                q = 1 - par
                if live(t, 0):
                    pe.wait_ge(gs_ready, t + 1)
                    at_least(pe, gt_ready, t)
                    pe.transpose(m.bank[2][0:8, 0:P], gs[:, par, :], m.ident[0:P, 0:P]).then_inc(gt_psum, 1)
                if live(t, 1):
                    g = t - 1
                    pe.wait_ge(gt_ready, g + 1)
                    at_least(pe, y_used, g)
                    pe.matmul(m.bank[3][0:P, 0:D], gT[:, q, :], b2s[:, :], start=True, stop=True).then_inc(gb_psum, 1)
            if b2 is not None:
                steps(pe, bias_step, 2)

            def expert(e, j, u):
                def up(n):
                    c0, k = CHUNKS[n]
                    for c in range(chunks):
                        i = n * chunks + c
                        if i >= 4:
                            pe.wait_ge(hid_ready, e * (nb * chunks) + (i - 3))
                        pe.matmul(m.quad_bank[:, i % 4, 0:k * P], w1s[:, u, c * 128:(c + 1) * 128],
                                  m.XT[:, c0 * P:(c0 + k) * P], start=True, stop=True).then_inc(hid_psum, 1)

                def down(n):
                    c0, k = CHUNKS[n]
                    pe.wait_ge(hid_ready, e * (nb * chunks) + (n + 1) * chunks)
                    if n == 0:
                        at_least(pe, y_used, e * nb + before)
                    elif n > 1:
                        pe.wait_ge(y_used, e * nb + (n - 1 + before))
                    for g in range(k):
                        for c in range(chunks):
                            mm = pe.matmul(m.bank[n % 2][0:P, g * D:(g + 1) * D], hid[:, n % 2, c, g * P:(g + 1) * P],
                                           w2s[:, u, c * 128:(c + 1) * 128], start=(c == 0), stop=(c == chunks - 1))
                    mm.then_inc(y_psum, 1)
                pe.wait_ge(loaded[u], (j + 1) * 48)
                up(0)
                for n in range(1, nb):
                    up(n)
                    down(n - 1)
                down(nb - 1)
            if experts == 1:
                expert(0, 0, 0)
            else:
                with pe.Fori(0, experts // 2) as j:
                    for u in range(2):
                        expert(j * 2 + u, j, u)

        @block.scalar
        def _(act):
            def bias_step(t, par):
                if live(t, 0):
                    act.wait_ge(gt_psum, t + 1)
                    at_least(act, gb_psum, t - 1)
                    act.activation(gT[:, par, :], m.bank[2][0:8, 0:P], ACT.Copy).then_inc(gt_ready, 1)
            if b2 is not None:
                steps(act, bias_step, 2)

            def expert(e, j, u):
                act.wait_ge(loaded[u], (j + 1) * 48)
                for n, (c0, k) in enumerate(CHUNKS):
                    for c in range(chunks):
                        act.wait_ge(hid_psum, e * (nb * chunks) + (n * chunks + c + 1))
                        if n > 1 and c == 0:
                            act.wait_ge(y_psum, e * nb + (n - 1))
                        act.activation(hid[:, n % 2, c, 0:k * P], m.quad_bank[:, (n * chunks + c) % 4, 0:k * P], func,
                                       bias=b1s[:, u, c:c + 1]).then_inc(hid_ready, 1)
            if experts == 1:
                expert(0, 0, 0)
            else:
                with act.Fori(0, experts // 2) as j:
                    for u in range(2):
                        expert(j * 2 + u, j, u)

        @block.vector
        def _(dve):
            def bias_step(t, par):
                if live(t, 1):
                    g = t - 1
                    dve.wait_ge(gb_psum, g + 1)
                    h = dst[:, bass.ts(g, D)]
                    dve.tensor_tensor(h, h, m.bank[3][0:P, 0:D], ALU.add).then_inc(y_used, 1)
            if b2 is not None:
                steps(dve, bias_step, 2)

            def expert(e):
                at_least(dve, y_used, e * nb + before)
                for n, (c0, k) in enumerate(CHUNKS):
                    dve.wait_ge(y_psum, e * nb + (n + 1))
                    y = m.bank[n % 2][0:P, 0:k * D]
                    if b2 is None:
                        h = dst[:, c0 * D:(c0 + k) * D]
                        dve.tensor_tensor(h, h, y, ALU.add).then_inc(y_used, 1)
                        continue
                    for g in range(c0, c0 + k):
                        h = dst[:, g * D:(g + 1) * D]
                        ins = dve.scalar_tensor_tensor(out=h, in0=y[:, (g - c0) * D:(g - c0 + 1) * D],
                                                       scalar=m.GATE[:, bass.ds(e + g * 8, 1)], in1=h,
                                                       op0=ALU.mult, op1=ALU.add)
                    ins.then_inc(y_used, 1)
            if experts == 1:
                expert(0)
            else:
                with dve.Fori(0, experts) as e:
                    expert(e)
            dve.wait_ge(y_used, experts * nb + before)


NS = 4
CW = 2 * D
TAPS = 4
PADDED = S + TAPS - 1


def time_steps(nc, m):
    with ExitStack() as ctx:
        sb = lambda s, shape: ctx.enter_context(nc.sbuf_tensor(f"dt_{s}", shape, F32))
        sem = ctx.enter_context(semaphores(nc, "dt"))
        own = sem("chain")
        absolute = sem("absolute")
        exped = sem("exped")
        u, r, r2, q = (sb(n, [P, G * 8]) for n in ("u", "r", "r2", "q"))
        a = sb("a", [P, 8])
        block = ctx.enter_context(nc.Block())

        @block.scalar
        def _(act):
            act.activation(a[:, :], m.small("A_log"), ACT.Exp).then_inc(exped, 1)
            act.wait_ge(absolute, 1)
            act.activation(u[:, :], r[:, :], ACT.Exp, scale=-1.0).then_inc(exped, 1)

        @block.vector
        def _(dve):
            then = chained(dve, own)
            dve.scalar_tensor_tensor(out=r[:, :], in0=m.LG[:, :], scalar=-1.0, in1=m.LG[:, :], op0=ALU.mult, op1=ALU.max).then_inc(absolute, 1)
            dve.wait_ge(exped, 2)
            then(dve.tensor_scalar(q[:, :], u[:, :], 2.0, None, ALU.add))
            then(dve.reciprocal(q[:, :], q[:, :]))
            then(dve.tensor_tensor(r[:, :], u[:, :], q[:, :], ALU.mult))
            then(dve.tensor_tensor(r2[:, :], r[:, :], r[:, :], ALU.mult))
            then(dve.tensor_scalar(q[:, :], r2[:, :], 1.0 / 17, None, ALU.mult))
            for k in (15, 13, 11, 9, 7, 5, 3):
                then(dve.scalar_tensor_tensor(out=q[:, :], in0=q[:, :], scalar=1.0 / k, in1=r2[:, :], op0=ALU.add, op1=ALU.mult))
            then(dve.scalar_tensor_tensor(out=q[:, :], in0=q[:, :], scalar=1.0, in1=r[:, :], op0=ALU.add, op1=ALU.mult))
            then(dve.tensor_scalar(u[:, :], m.LG[:, :], 0.0, None, ALU.max))
            then(dve.scalar_tensor_tensor(out=m.DT[:, :], in0=q[:, :], scalar=2.0, in1=u[:, :], op0=ALU.mult, op1=ALU.add))
            then(dve.scalar_tensor_tensor(out=m.DTA[:, :].rearrange("p (g e) -> p g e", e=8), in0=m.DT[:, :].rearrange("p (g e) -> p g e", e=8),
                                          scalar=-1.0, in1=a[:, :].unsqueeze(1).broadcast_to([P, G, 8]), op0=ALU.mult, op1=ALU.mult))


def state_space_phase(nc, m, io):
    with ExitStack() as ctx:
        sem = ctx.enter_context(semaphores(nc, "ss"))
        sb = lambda s, shape, dt=F32: ctx.enter_context(nc.sbuf_tensor(f"ss_{s}", shape, dt))
        w_loaded = sem("w_loaded")
        prepared = sem("prepared")
        xbc_psum = sem("xbc_psum")
        padded = sem("padded")
        conv = sem("conv")
        tanhed = sem("tanhed")
        silu = sem("silu")
        xts_ready = sem("xts_ready")
        xc_psum = sem("xc_psum")
        xc_ready = sem("xc_ready")
        cum_ready = sem("cum_ready")
        seg_psum = sem("seg_psum")
        decay = sem("decay")
        z_psum = sem("z_psum")
        z_tanh = sem("z_tanh")
        z_ready = sem("z_ready")
        masked = sem("masked")
        xdt_ready = sem("xdt_ready")
        mix_ready = sem("mix_ready")
        y_psum = sem("y_psum")
        yz_ready = sem("yz_ready")
        ssq_ready = sem("ssq_ready")
        rms_steps = sem("rms_steps")
        rms_ready = sem("rms_ready")
        yt_psum = sem("yt_psum")
        yt_ready = sem("yt_ready")
        o_psum = sem("o_psum")
        sum_ready = sem("sum_ready")
        stats = sem("stats")
        eps_added = sem("eps_added")
        rstd_ready = sem("rstd_ready")
        normed = sem("normed")
        scaled = sem("scaled")
        t_psum = sem("t_psum")
        t_ready = sem("t_ready")
        win = sb("win", [128, 6 * 128])
        wout = sb("wout", [128, 2, D])
        ch = sb("ch", [128, 24])
        half = sb("half", [128, 20])
        drow = sb("drow", [P, NS])
        dI = sb("dI", [P, NS, P])
        xp = sb("xp", [128, 2, 4 * TB, PADDED])
        cv = sb("cv", [128, 2, 4, P])
        th = sb("th", [128, 4 * P])
        sx = sb("sx", [128, 2, 4, P])
        xTs = sb("xTs", [128, 2, P])
        cum = sb("cum", [P, 2, NS, P])
        xc = sb("xc", [P, 2, CW + P])
        cbm = sb("cbm", [P, P])
        L = sb("L", [P, NS, P])
        M = sb("M", [P, 2, NS, P])
        xdt = sb("xdt", [P, 2, CW])
        zs = sb("zs", [P, 2, CW])
        yz = sb("yz", [P, 2, CW])
        sq = sb("sq", [P, CW])
        ssq = sb("ssq", [P, 2, 1])
        rms = sb("rms", [P, 2, 1])
        yT = sb("yT", [128, 2 * P])
        yt = sb("yt", [P, 2, D])
        bn6 = sb("bn6", [P, 2, 6])
        mv = sb("mv", [P, 2, 2])
        ve = sb("ve", [P, 2, 1])
        rstd = sb("rstd", [P, 2, 1])
        tt = sb("tt", [P, 2, D])
        seg_bank, y_bank, o_bank, t_bank = (m.quad_bank[:, b, :] for b in range(4))
        depth = 7
        block = ctx.enter_context(nc.Block())

        @block.sync
        def _(sp):
            for dst, src in ((win, io["ss_win"]), (ch, io["ss_ch"]), (drow, io["ss_drow"])):
                sp.dma_start(dst[:, :], src).then_inc(w_loaded, 16)
            sp.dma_start(wout[:, :, :], io["ss_wout"]).then_inc(w_loaded, 16)

        @block.gpsimd
        def _(pool):
            def step(t, par):
                q = 1 - par
                if live(t, 1):
                    g = t - 1
                    at_least(pool, z_psum, g - 1)
                    pool.tensor_copy(xTs[:, q, :], m.XT[:, bass.ts(g, P)]).then_inc(xts_ready, 1)
                if live(t, 5):
                    g = t - 5
                    pool.wait_ge(normed, g + 1)
                    at_least(pool, t_psum, g - 1)
                    pool.tensor_tensor(tt[:, q, :], yt[:, q, :], m.row("n1_g"), ALU.mult).then_inc(scaled, 1)
                    pool.wait_ge(scaled, g * 3 + 1)
                    pool.tensor_tensor(tt[:, q, :], tt[:, q, :], m.row("n1_b"), ALU.add).then_inc(scaled, 1)
                    pool.wait_ge(scaled, g * 3 + 2)
                    pool.tensor_tensor(m.T[:, bass.ts(g, D)], tt[:, q, :], m.row("ffn_b2"), ALU.add).then_inc(scaled, 1)
                if live(t, 3):
                    g = t - 3
                    pool.wait_ge(ssq_ready, g + 1)
                    pool.tensor_tensor(ssq[:, q, :], ssq[:, q, :], m.inv_cw[0:P, :], ALU.mult).then_inc(rms_steps, 1)
                    pool.wait_ge(rms_steps, g * 2 + 1)
                    pool.tensor_tensor(ssq[:, q, :], ssq[:, q, :], m.eps[0:P, :], ALU.add).then_inc(rms_steps, 1)
                    pool.wait_ge(rms_steps, g * 2 + 2)
                    at_least(pool, sum_ready, g - 1)
                    pool.tensor_tensor(rms[:, q, :], ssq[:, q, :], m.mhalf[0:P, :], ALU.pow).then_inc(rms_ready, 1)
                if live(t, 4):
                    g = t - 4
                    pool.wait_ge(stats, g * 2 + 2)
                    pool.tensor_tensor(ve[:, par, :], mv[:, par, 1:2], m.eps[0:P, :], ALU.add).then_inc(eps_added, 1)
                    pool.wait_ge(eps_added, g + 1)
                    at_least(pool, normed, g - 1)
                    pool.tensor_tensor(rstd[:, par, :], ve[:, par, :], m.mhalf[0:P, :], ALU.pow).then_inc(rstd_ready, 1)
            steps(pool, step, depth)
            pool.wait_ge(scaled, 3 * G)

        @block.tensor
        def _(pe):
            pe.wait_ge(w_loaded, 64)
            pe.wait_ge(prepared, 3)

            def step(t, par):
                q = 1 - par
                if live(t, 0):
                    g = t
                    at_least(pe, padded, g)
                    for c in range(4):
                        mm = pe.matmul(m.bank[2][:, c * P:(c + 1) * P], win[:, (2 + c) * 128:(3 + c) * 128],
                                       m.XT[:, bass.ts(g, P)], start=True, stop=True)
                    mm.then_inc(xbc_psum, 1)
                if live(t, 2):
                    g = t - 2
                    pe.wait_ge(cum_ready, g + 1)
                    at_least(pe, decay, g)
                    pe.matmul(seg_bank[0:P, 0:NS * P], m.later, cum[:, par, :, :].rearrange("p n j -> p (n j)"),
                              start=True, stop=True).then_inc(seg_psum, 1)
                    pe.wait_ge(silu, g + 1)
                    at_least(pe, xc_ready, g)
                    for c in range(2):
                        pe.transpose(m.bank[3][0:P, c * 128:(c + 1) * 128], sx[:, par, c, :], m.ident[:, :])
                    pe.matmul(m.bank[3][0:P, CW:CW + P], sx[:, par, 2, :], sx[:, par, 3, :], start=True, stop=True).then_inc(xc_psum, 1)
                    pe.wait_ge(xts_ready, g + 1)
                    at_least(pe, z_ready, g)
                    pe.matmul(m.bank[1][0:P, 0:CW], xTs[:, par, :], win[:, 0:CW], start=True, stop=True).then_inc(z_psum, 1)
                if live(t, 4):
                    g = t - 4
                    pe.wait_ge(yz_ready, g + 1)
                    at_least(pe, yt_ready, g)
                    for c in range(2):
                        mm = pe.transpose(m.bank[0][:, c * P:(c + 1) * P], yz[:, par, c * 128:(c + 1) * 128], m.ident[0:P, 0:P])
                    mm.then_inc(yt_psum, 1)
                if live(t, 3):
                    g = t - 3
                    pe.wait_ge(mix_ready, g + 1)
                    pe.wait_ge(xdt_ready, g + 1)
                    at_least(pe, yz_ready, g)
                    for n in range(NS):
                        cols = slice(n * 64, (n + 1) * 64)
                        pe.matmul(y_bank[0:P, cols], dI[:, n, :], xc[:, q, cols], start=True, stop=False, skip_group_check=True)
                        mm = pe.matmul(y_bank[0:P, cols], M[:, q, n, :], xdt[:, q, cols], start=False, stop=True, skip_group_check=True)
                    mm.then_inc(y_psum, 1)
                if live(t, 4):
                    g = t - 4
                    pe.wait_ge(yt_ready, g + 1)
                    at_least(pe, sum_ready, g)
                    for c in range(2):
                        mm = pe.matmul(o_bank[0:P, 0:D], yT[:, c * P:(c + 1) * P], wout[:, c, :], start=(c == 0), stop=(c == 1))
                    mm.then_inc(o_psum, 1)
                if live(t, 6):
                    g = t - 6
                    pe.wait_ge(scaled, g * 3 + 2)
                    at_least(pe, t_ready, g)
                    pe.transpose(t_bank[:, 0:P], tt[:, par, :], m.ident[0:P, 0:P]).then_inc(t_psum, 1)
            steps(pe, step, depth)

        @block.scalar
        def _(act):
            act.wait_ge(prepared, 3)

            def step(t, par):
                q = 1 - par
                if live(t, 0):
                    g = t
                    act.wait_ge(xbc_psum, g + 1)
                    at_least(act, conv, (g - 1) * 16)
                    act.activation(xp[:, par, :, TAPS - 1:PADDED], m.bank[2][:, 0:4 * P].rearrange("p (b s) -> p b s", s=S),
                                   ACT.Copy).then_inc(padded, 1)
                if live(t, 1):
                    g = t - 1
                    act.wait_ge(conv, g * 16 + 16)
                    at_least(act, silu, g)
                    act.activation(th[:, :], cv[:, q, :, :].rearrange("p c j -> p (c j)"), ACT.Tanh).then_inc(tanhed, 1)
                if live(t, 2):
                    g = t - 2
                    act.wait_ge(seg_psum, g + 1)
                    at_least(act, mix_ready, g)
                    act.activation(L[:, :, :].rearrange("p n j -> p (n j)"), seg_bank[0:P, 0:NS * P], ACT.Exp).then_inc(decay, 1)
                    act.wait_ge(xc_psum, g + 1)
                    at_least(act, y_psum, g - 1)
                    act.activation(xc[:, par, :], m.bank[3][0:P, 0:CW + P], ACT.Copy).then_inc(xc_ready, 1)
                    act.wait_ge(z_psum, g + 1)
                    at_least(act, yz_ready, g - 1)
                    act.activation(zs[:, par, :], m.bank[1][0:P, 0:CW], ACT.Tanh, scale=0.5).then_inc(z_tanh, 1)
                if live(t, 4):
                    g = t - 4
                    act.wait_ge(yt_psum, g + 1)
                    at_least(act, o_psum, g)
                    act.activation(yT[:, :], m.bank[0][:, 0:2 * P], ACT.Copy).then_inc(yt_ready, 1)
                if live(t, 3):
                    g = t - 3
                    act.wait_ge(yz_ready, g + 1)
                    at_least(act, rms_ready, g - 1)
                    at_least(act, ssq_ready, g)
                    act.activation(sq[:, :], yz[:, q, :], ACT.Square, accum_out=ssq[:, q, :]).then_inc(ssq_ready, 1)
                if live(t, 6):
                    g = t - 6
                    act.wait_ge(t_psum, g + 1)
                    act.activation(m.XT[:, bass.ts(g, P)], t_bank[:, 0:P], ACT.Copy).then_inc(t_ready, 1)
            steps(act, step, depth)

        @block.vector
        def _(dve):
            dve.wait_ge(w_loaded, 64)
            dve.memset(xp[:, :, :, 0:TAPS - 1].rearrange("p a b k -> p (a b) k"), 0.0).then_inc(prepared, 1)
            dve.tensor_scalar(half[:, :], ch[:, 0:20], 0.5, None, ALU.mult).then_inc(prepared, 1)
            for c in range(2):
                dve.tensor_scalar(wout[:, c, :], wout[:, c, :], ch[:, 20 + c:21 + c], None, ALU.mult)
            for n in range(NS):
                ins = dve.tensor_scalar(dI[:, n, :], m.ident[0:P, 0:P], drow[:, n:n + 1], None, ALU.mult)
            ins.then_inc(prepared, 1)
            dve.wait_ge(prepared, 3)

            def step(t, par):
                q = 1 - par
                if live(t, 1):
                    g = t - 1
                    dve.wait_ge(padded, g + 1)
                    at_least(dve, tanhed, g - 1)
                    at_least(dve, silu, g - 1)
                    for k in range(TAPS):
                        for c in range(4):
                            x = xp[:, q, c * TB:(c + 1) * TB, k:k + S]
                            y = cv[:, q, c, :].rearrange("p (b s) -> p b s", s=S)
                            tap = half[:, c * TAPS + k:c * TAPS + k + 1]
                            if k == 0:
                                dve.tensor_scalar(y, x, tap, half[:, 16 + c:17 + c], ALU.mult, ALU.add).then_inc(conv, 1)
                            else:
                                dve.wait_ge(conv, g * 16 + (4 * k + c - 3))
                                dve.scalar_tensor_tensor(out=y, in0=x, scalar=tap, in1=y, op0=ALU.mult, op1=ALU.add).then_inc(conv, 1)
                    at_least(dve, seg_psum, g - 1)
                    dve.tensor_tensor(cum[:, q, :, :], m.upto.unsqueeze(1).broadcast_to([P, NS, P]),
                                      m.DTA[:, bass.ds(g * 8, NS)].unsqueeze(2).broadcast_to([P, NS, P]), ALU.mult).then_inc(cum_ready, 1)
                if live(t, 2):
                    g = t - 2
                    dve.wait_ge(xc_ready, g + 1)
                    at_least(dve, mix_ready, g)
                    dve.tensor_tensor(cbm[:, :], xc[:, par, CW:CW + P], m.upto, ALU.mult).then_inc(masked, 1)
                    at_least(dve, y_psum, g - 1)
                    dve.tensor_tensor(xdt[:, par, :].rearrange("p (n c) -> p n c", n=NS), xc[:, par, 0:CW].rearrange("p (n c) -> p n c", n=NS),
                                      m.DT[:, bass.ds(g * 8, NS)].unsqueeze(2).broadcast_to([P, NS, 64]), ALU.mult).then_inc(xdt_ready, 1)
                    dve.wait_ge(decay, g + 1)
                    dve.wait_ge(masked, g + 1)
                    dve.tensor_tensor(M[:, par, :, :], L[:, :, :], cbm[:, :].unsqueeze(1).broadcast_to([P, NS, P]), ALU.mult).then_inc(mix_ready, 1)
                    dve.wait_ge(z_tanh, g + 1)
                    dve.scalar_tensor_tensor(out=zs[:, par, :], in0=zs[:, par, :], scalar=1.0, in1=m.bank[1][0:P, 0:CW],
                                             op0=ALU.add, op1=ALU.mult).then_inc(z_ready, 1)
                if live(t, 5):
                    g = t - 5
                    dve.wait_ge(rstd_ready, g + 1)
                    dve.tensor_scalar(yt[:, q, :], yt[:, q, :], mv[:, q, 0:1], rstd[:, q, :], ALU.subtract, ALU.mult).then_inc(normed, 1)
                if live(t, 1):
                    g = t - 1
                    dve.wait_ge(tanhed, g + 1)
                    at_least(dve, xc_psum, g - 1)
                    dve.scalar_tensor_tensor(out=sx[:, q, :, :].rearrange("p c j -> p (c j)"), in0=th[:, :], scalar=1.0,
                                             in1=cv[:, q, :, :].rearrange("p c j -> p (c j)"), op0=ALU.add, op1=ALU.mult).then_inc(silu, 1)
                if live(t, 3):
                    g = t - 3
                    dve.wait_ge(y_psum, g + 1)
                    at_least(dve, yt_psum, g - 1)
                    at_least(dve, ssq_ready, g - 1)
                    dve.wait_ge(z_ready, g + 1)
                    dve.scalar_tensor_tensor(out=yz[:, q, :], in0=y_bank[0:P, 0:CW], scalar=0.5, in1=zs[:, q, :],
                                             op0=ALU.mult, op1=ALU.mult).then_inc(yz_ready, 1)
                if live(t, 4):
                    g = t - 4
                    dve.wait_ge(o_psum, g + 1)
                    dve.wait_ge(rms_ready, g + 1)
                    at_least(dve, normed, g - 1)
                    at_least(dve, scaled, (g - 2) * 3 + 1) if not isinstance(t, int) or g > 1 else None
                    dve.scalar_tensor_tensor(out=yt[:, par, :], in0=o_bank[0:P, 0:D], scalar=rms[:, par, :],
                                             in1=m.XN[:, bass.ts(g, D)], op0=ALU.mult, op1=ALU.add).then_inc(sum_ready, 1)
                    dve.wait_ge(sum_ready, g + 1)
                    at_least(dve, eps_added, g - 1)
                    dve.bn_stats(bn6[:, par, :], yt[:, par, :]).then_inc(stats, 1)
                    dve.drain()
                    dve.bn_aggr(mv[:, par, :], bn6[:, par, :]).then_inc(stats, 1)
            steps(dve, step, depth)


def close_phase(nc, m):
    with ExitStack() as ctx:
        sem = ctx.enter_context(semaphores(nc, "cl"))
        sb = lambda s, shape: ctx.enter_context(nc.sbuf_tensor(f"cl_{s}", shape, F32))
        stats, eps_added, rstd_ready, normed, scaled, h_done = (sem(n) for n in ("stats", "eps_added", "rstd_ready", "normed", "scaled", "h_done"))
        bn6, mv, ve, rstd, tt = sb("bn6", [P, 2, 6]), sb("mv", [P, 2, 2]), sb("ve", [P, 2, 1]), sb("rstd", [P, 2, 1]), sb("tt", [P, 2, D])
        block = ctx.enter_context(nc.Block())

        @block.gpsimd
        def _(pool):
            def step(t, par):
                q = 1 - par
                if live(t, 0):
                    g = t
                    pool.wait_ge(stats, g * 2 + 2)
                    pool.tensor_tensor(ve[:, par, :], mv[:, par, 1:2], m.eps[0:P, :], ALU.add).then_inc(eps_added, 1)
                    pool.wait_ge(eps_added, g + 1)
                    at_least(pool, normed, g - 1)
                    pool.tensor_tensor(rstd[:, par, :], ve[:, par, :], m.mhalf[0:P, :], ALU.pow).then_inc(rstd_ready, 1)
                if live(t, 1):
                    g = t - 1
                    pool.wait_ge(normed, g + 1)
                    pool.tensor_tensor(tt[:, q, :], tt[:, q, :], m.row("n3_g"), ALU.mult).then_inc(scaled, 1)
                    pool.wait_ge(scaled, g + 1)
                    pool.tensor_tensor(m.T[:, bass.ts(g, D)], tt[:, q, :], m.row("n3_b"), ALU.add).then_inc(h_done, 1)
            steps(pool, step, 3)

        @block.vector
        def _(dve):
            def step(t, par):
                q = 1 - par
                if live(t, 0):
                    g = t
                    at_least(dve, normed, g - 1)
                    at_least(dve, eps_added, g - 1)
                    dve.bn_stats(bn6[:, par, :], m.T[:, bass.ts(g, D)]).then_inc(stats, 1)
                    dve.drain()
                    dve.bn_aggr(mv[:, par, :], bn6[:, par, :]).then_inc(stats, 1)
                if live(t, 1):
                    g = t - 1
                    dve.wait_ge(rstd_ready, g + 1)
                    at_least(dve, h_done, g - 1)
                    dve.tensor_scalar(tt[:, q, :], m.T[:, bass.ts(g, D)], mv[:, q, 0:1], rstd[:, q, :], ALU.subtract, ALU.mult).then_inc(normed, 1)
                if live(t, 2):
                    g = t - 2
                    dve.wait_ge(h_done, g + 1)
                    h = m.H[:, bass.ts(g, D)]
                    dve.tensor_tensor(h, h, m.T[:, bass.ts(g, D)], ALU.add)
            steps(dve, step, 3)


def batch_norm_phase(nc, m):
    real = BATCH * S
    parts = -(-real // 512)
    while real % parts:
        parts += 1
    part = real // parts
    with ExitStack() as ctx:
        sem = ctx.enter_context(semaphores(nc, "bn"))
        sb = lambda s, shape: ctx.enter_context(nc.sbuf_tensor(f"bn_{s}", shape, F32))
        own = sem("own")
        stats_ready = sem("stats_ready")
        pool_own = sem("pool_own")
        rstd_ready = sem("rstd_ready")
        affine_ready = sem("affine_ready")
        relued = sem("relued")
        turned = sem("turned")
        h_ready = sem("h_ready")
        bn6, mv, ve, rstd = sb("bn6", [128, parts, 6]), sb("mv", [128, 2]), sb("ve", [128, 1]), sb("rstd", [128, 1])
        scale, shift = sb("scale", [128, 1]), sb("shift", [128, 1])
        block = ctx.enter_context(nc.Block())

        @block.gpsimd
        def _(pool):
            pool.wait_ge(stats_ready, 1)
            pool.tensor_tensor(ve[:, :], mv[:, 1:2], m.eps, ALU.add).then_inc(pool_own, 1)
            pool.wait_ge(pool_own, 1)
            pool.tensor_tensor(rstd[:, :], ve[:, :], m.mhalf, ALU.pow).then_inc(rstd_ready, 1)

        @block.tensor
        def _(pe):
            for n, (c, k) in enumerate(CHUNKS):
                pe.wait_ge(relued, n + 1)
                at_least(pe, h_ready, n - 1)
                for g in range(k):
                    mm = pe.transpose(m.bank[n % 2][0:P, g * D:(g + 1) * D], m.YT[:, (c + g) * P:(c + g + 1) * P], m.ident[:, :])
                mm.then_inc(turned, 1)

        @block.scalar
        def _(act):
            act.wait_ge(affine_ready, 1)
            for n, (c, k) in enumerate(CHUNKS):
                y = m.YT[:, c * P:(c + k) * P]
                act.activation(y, y, ACT.Relu, scale=scale[:, :], bias=shift[:, :]).then_inc(relued, 1)

        @block.vector
        def _(dve):
            for n in range(parts):
                dve.bn_stats(bn6[:, n, :], m.YT[:, n * part:(n + 1) * part])
            dve.drain()
            dve.bn_aggr(mv[:, :], bn6[:, :, :]).then_inc(stats_ready, 1)
            then = chained(dve, own)
            dve.wait_ge(rstd_ready, 1)
            then(dve.tensor_tensor(scale[:, :], m.col("bn_gamma"), rstd[:, :], ALU.mult))
            then(dve.tensor_tensor(shift[:, :], mv[:, 0:1], scale[:, :], ALU.mult))
            dve.tensor_tensor(shift[:, :], m.col("bn_beta"), shift[:, :], ALU.subtract).then_inc(affine_ready, 1)
            for n, (c, k) in enumerate(CHUNKS):
                dve.wait_ge(turned, n + 1)
                h = m.H[:, c * D:(c + k) * D]
                dve.tensor_tensor(h, h, m.bank[n % 2][0:P, 0:k * D], ALU.add).then_inc(h_ready, 1)
            dve.wait_ge(h_ready, len(CHUNKS))


SETS = 3


def routes_phase(nc, m, io):
    B = G * TB
    with ExitStack() as ctx:
        sem = ctx.enter_context(semaphores(nc, "rt"))
        sb = lambda s, shape: ctx.enter_context(nc.sbuf_tensor(f"rt_{s}", shape, F32))
        w_loaded = sem("w_loaded")
        psum = sem("psum")
        hid_ready = sem("hid_ready")
        shifted = sem("shifted")
        exped = sem("exped")
        own = sem("own")
        spread_ready = sem("spread_ready")
        rw = sb("rw", [128, 128 + 1 + 8 + P + G])
        hid = sb("hid", [128, B])
        lg, pr, one, tmp = (sb(n, [B, 1, SETS]) for n in ("lg", "pr", "one", "tmp"))
        top, tot = sb("top", [B, 1]), sb("tot", [B, 1])
        spread = sb("spread", [B, G, SETS])
        block = ctx.enter_context(nc.Block())
        wide = lambda x: x[:, :].unsqueeze(2).broadcast_to([B, 1, SETS])

        @block.sync
        def _(sp):
            sp.dma_start(rw[:, :], io["rt_w"]).then_inc(w_loaded, 16)

        @block.tensor
        def _(pe):
            pe.wait_ge(w_loaded, 16)
            pe.matmul(m.bank[0][:, 0:B], rw[:, 0:128], m.MEANS[:, :], start=True, stop=True).then_inc(psum, 1)
            pe.wait_ge(hid_ready, 1)
            pe.matmul(m.bank[1][0:B, 0:8], hid[:, :], rw[:, 129:137], start=True, stop=True).then_inc(psum, 1)
            pe.wait_ge(spread_ready, 1)
            pe.matmul(m.bank[2][0:P, 0:G * SETS], rw[0:B, 137:137 + P], spread[:, :, :].rearrange("p g x -> p (g x)"),
                      start=True, stop=True).then_inc(psum, 1)

        @block.scalar
        def _(act):
            act.wait_ge(psum, 1)
            act.activation(hid[:, :], m.bank[0][:, 0:B], ACT.Relu, scale=1.0 / S, bias=rw[:, 128:129]).then_inc(hid_ready, 1)
            act.wait_ge(shifted, 1)
            act.activation(pr[:, 0, :], lg[:, 0, :], ACT.Exp).then_inc(exped, 1)

        @block.vector
        def _(dve):
            then = chained(dve, own)
            dve.wait_ge(w_loaded, 16)
            dve.wait_ge(psum, 2)
            then(dve.tensor_tensor(lg[:, 0, :], m.bank[1][0:B, 0:SETS], m.small("r_b2", SETS)[0:B, :], ALU.add))
            then(dve.tensor_reduce(top[:, :], lg[:, :, :], AX, ALU.max))
            dve.tensor_tensor(lg[:, :, :], lg[:, :, :], wide(top), ALU.subtract).then_inc(shifted, 1)
            dve.wait_ge(exped, 1)
            then(dve.tensor_reduce(tot[:, :], pr[:, :, :], AX, ALU.add))
            then(dve.reciprocal(tot[:, :], tot[:, :]))
            then(dve.tensor_tensor(pr[:, :, :], pr[:, :, :], wide(tot), ALU.mult))
            first_best(dve, m, then, one[:, :, :], pr[:, :, :], tmp[:, :, :], top[:, :], [B, 1, SETS])
            dve.tensor_tensor(spread[:, :, :], rw[0:B, 137 + P:137 + P + G].unsqueeze(2).broadcast_to([B, G, SETS]),
                              one[:, :, :].broadcast_to([B, G, SETS]), ALU.mult).then_inc(spread_ready, 1)
            dve.wait_ge(psum, 3)
            then(dve.tensor_copy(m.MSK[:, :], m.bank[2][0:P, 0:G * SETS]))


COLS = ["tok_b", "bn_gamma", "bn_beta"]
ROWS = ["a0_b_proj", "a0_gamma", "a0_beta", "small", "n1_g", "n1_b", "n3_g", "n3_b", "ffn_b2"]
SMALL = {"rb0": 0, "br": 8, "none": 16, "dt_bias": 24, "A_log": 32, "rank": 40, "r_b2": 48}


def build(nc, io, out):
    with ExitStack() as ctx:
        m = Shared()
        m.bank = [ctx.enter_context(nc.psum_tensor(f"bank{b}", [128, 512], F32)) for b in range(4)]
        m.quad_bank = ctx.enter_context(nc.psum_tensor("quad_bank", [128, 4, 512], F32))
        m.H = ctx.enter_context(nc.sbuf_tensor("H", [P, G * D], F32))
        m.const = ctx.enter_context(nc.sbuf_tensor("const", list(io["const"].shape), F32))
        m.cols = ctx.enter_context(nc.sbuf_tensor("cols", list(io["cols"].shape), F32))
        m.rows = ctx.enter_context(nc.sbuf_tensor("rows", list(io["rows"].shape), F32))
        m.bconst = ctx.enter_context(nc.sbuf_tensor("bconst", list(io["bconst"].shape), BF16))
        m.XN = ctx.enter_context(nc.sbuf_tensor("XN", [P, G * D], F32))
        m.row = lambda n: m.rows[:, ROWS.index(n) * D:(ROWS.index(n) + 1) * D]
        m.small = lambda n, w=8: m.row("small")[:, SMALL[n]:SMALL[n] + w]
        m.rank = m.small("rank")
        m.XT = ctx.enter_context(nc.sbuf_tensor("XT", [128, G * P], F32))
        m.LG = ctx.enter_context(nc.sbuf_tensor("LG", [P, G * 8], F32))
        m.GATE = ctx.enter_context(nc.sbuf_tensor("GATE", [P, G * 8], F32))
        m.ident = m.const[:, 0:128]
        m.mhalf = m.const[:, 128:129]
        m.eps = m.const[:, 129:130]
        m.inv_cw = m.const[:, 130:131]
        m.later = m.const[0:P, 131:131 + P]
        m.upto = m.const[0:P, 131 + P:131 + 2 * P]
        m.T = ctx.enter_context(nc.sbuf_tensor("T", [P, G * D], F32))
        m.DT = ctx.enter_context(nc.sbuf_tensor("DT", [P, G * 8], F32))
        m.DTA = ctx.enter_context(nc.sbuf_tensor("DTA", [P, G * 8], F32))
        m.YT = ctx.enter_context(nc.sbuf_tensor("YT", [128, G * P], F32))
        m.MSK = ctx.enter_context(nc.sbuf_tensor("MSK", [P, G * SETS], F32))
        m.MEANS = ctx.enter_context(nc.sbuf_tensor("MEANS", [128, G * TB], F32))
        m.img = m.bconst[:, 0:P]
        m.not_img = m.bconst[:, P:5 * P]
        m.col = lambda n: m.cols[:, COLS.index(n):COLS.index(n) + 1]
        patch_phase(nc, m, io)
        w = Weights(io["a0_wv"], HD ** -0.5, io["a0_wqk"], io["a0_wo"])
        attention_phase(nc, m, "a0", w, ending="post_norm")
        prepare_phase(nc, m, "p0", io["f0_router"], m.small("rb0"))
        tree_gates(nc, m, "t0")
        experts_phase(nc, m, "f0", io["f0_w1"], io["f0_w2"], io["f0_b1"], ACT.Gelu, 8, 4, io["f0_b2"], m.H)
        prepare_phase(nc, m, "p1", io["ss_router"], m.small("dt_bias"), keep=True)
        time_steps(nc, m)
        state_space_phase(nc, m, io)
        experts_phase(nc, m, "fs", io["fs_w1"], io["fs_w2"], io["fs_b1"], ACT.Gelu, 1, 4, None, m.T)
        close_phase(nc, m)
        prepare_phase(nc, m, "p2", io["f1_router"], m.small("br"))
        best_gates(nc, m, "t1", 1)
        experts_phase(nc, m, "f1", io["f1_w1"], io["f1_w2"], io["f1_b1"], ACT.Gelu, 8, 4, io["f1_b2"], m.H)
        w = Weights(io["a1_wv"], 64 ** -0.5, io["a1_wqk"], io["a1_wo"])
        attention_phase(nc, m, "a1", w, hd=64)
        prepare_phase(nc, m, "p3", io["f2_router"], m.small("none"))
        best_gates(nc, m, "t2", 2)
        experts_phase(nc, m, "f2", io["f2_w1"], io["f2_w2"], io["f2_b1"], ACT.Gelu_apprx_tanh, 8, 2, io["f2_b2"], m.H)
        w = Weights(io["a2_wv"], 64 ** -0.5, own=io["a2_own"], factors=io["a2_factors"])
        attention_phase(nc, m, "a2", w, ending="channels")
        batch_norm_phase(nc, m)
        prepare_phase(nc, m, "p4", means=True)
        routes_phase(nc, m, io)
        w = Weights(io["a3_wv"], HD ** -0.5, io["a3_wqk"], io["a3_wo"])
        attention_phase(nc, m, "a3", w, nx=SETS, masks=True)
        with ExitStack() as ctx2:
            stored = ctx2.enter_context(nc.semaphore("stored"))
            block = ctx2.enter_context(nc.Block())

            @block.sync
            def _(sp):
                h = m.H[:, :].rearrange("p (g d) -> p g d", d=D)
                full = BATCH // TB
                dst = out[0:full * TB].rearrange("(g b) s d -> (b s) g d", b=TB)
                sp.dma_start(dst, h[:, 0:full, :]).then_inc(stored, 16)
                sp.dma_start(out[full * TB:BATCH].rearrange("b s d -> (b s) d"),
                             h[0:(BATCH - full * TB) * S, full, :]).then_inc(stored, 16)
                sp.wait_ge(stored, 32)


def qk_tiles(wq, wk):
    z = np.zeros((128, 2, 2, 4, SLOT), wq.dtype)
    for i, w in enumerate((wq, wk)):
        z[:, i, :, :, 0:HD] = w.reshape(128, 2, 4, HD)
    return z.reshape(128, 512)


def head_rows(w):
    z = np.zeros((2, 4, SLOT, w.shape[1]), w.dtype)
    z[:, :, 0:HD] = w.reshape(2, 4, HD, w.shape[1])
    return z.reshape(2, 128, w.shape[1]).transpose(1, 0, 2)


def laid_out(a):
    f = np.float32
    x = a["x"]
    pad = np.zeros((G * TB, 3, 6, 16, 6, 16), f)
    pad[:BATCH] = x.reshape(BATCH, 3, 6, 16, 6, 16)
    pats = pad.transpose(1, 3, 5, 0, 2, 4).reshape(KC, 128, G * P).transpose(1, 0, 2)
    r = {}
    r["patches"] = pats
    r["tokw"] = a["L0_tok_w"].T.reshape(KC, 128, D).transpose(1, 0, 2).reshape(128, KC * D)
    const = np.zeros((128, 131 + 2 * P), f)
    tok = np.arange(P)
    same = tok[:, None] // S == tok[None, :] // S
    const[:, 130] = 1.0 / CW
    const[0:P, 131:131 + P] = same & (tok[:, None] > tok[None, :])
    const[0:P, 131 + P:131 + 2 * P] = same & (tok[:, None] <= tok[None, :])
    const[:, 0:128] = np.eye(128, dtype=f)
    const[:, 128] = -0.5
    const[:, 129] = EPS
    r["const"] = const
    r["cols"] = np.stack([a["L0_tok_b"], a["L3_attn_gamma"], a["L3_attn_beta"]], 1)
    small = np.zeros(D, f)
    small[SMALL["rank"]:SMALL["rank"] + 8] = np.arange(8, 0, -1)
    for n, x in (("rb0", "L0_ffn_rb"), ("br", "L1_ffn_br"), ("dt_bias", "L1_attn_dt_bias"), ("A_log", "L1_attn_A_log"), ("r_b2", "L3_ffn_r_b2")):
        small[SMALL[n]:SMALL[n] + a[x].size] = a[x]
    rows = [a["L0_attn_b_proj"], a["L0_attn_ln_gamma"], a["L0_attn_ln_beta"], small] + [a["L1_attn_" + n] for n in ("n1_g", "n1_b", "n3_g", "n3_b", "ffn_b2")]
    r["rows"] = np.broadcast_to(np.concatenate(rows), (P, sum(x.size for x in rows)))
    b = np.zeros((128, 5 * P), f)
    for k in range(4):
        for i in range(TB):
            b[SLOT * k + i, i * S:(i + 1) * S] = 1
            for c in range(4):
                b[SLOT * k + i, P * (1 + c):P * (2 + c)] = NEG
                b[SLOT * k + i, P * (1 + c) + i * S:P * (1 + c) + (i + 1) * S] = 0
    r["bconst"] = b
    wqkv = a["L0_attn_w_qkv"].T
    r["a0_wqk"] = qk_tiles(wqkv[:, 0:128], wqkv[:, 128:256]).reshape(128, 1, 512)
    r["a0_wv"] = wqkv[:, 256:384].reshape(128, 1, 128)
    r["a0_wo"] = head_rows(a["L0_attn_w_proj"].T)
    padded = lambda w, n: np.concatenate([w, np.zeros((w.shape[0], n - w.shape[1]), f)], 1)
    r["f0_router"] = padded(a["L0_ffn_rw"].T, 8)
    for n, w1, b1, w2, b2 in (("f0", "L0_ffn_w1", "L0_ffn_b1", "L0_ffn_w2", "L0_ffn_b2"),
                              ("f1", "L1_ffn_W1", "L1_ffn_b1", "L1_ffn_W2", "L1_ffn_b2"),
                              ("f2", "L2_ffn_W1", "L2_ffn_b1", "L2_ffn_W2", "L2_ffn_b2")):
        e, hid = a[b1].shape
        r[n + "_w1"] = a[w1]
        r[n + "_b1"] = a[b1].reshape(e, hid // 128, 128).transpose(0, 2, 1)
        r[n + "_w2"] = a[w2].reshape(e, hid // 128, 128, D).transpose(0, 2, 1, 3).reshape(e, 128, hid // 128 * D)
        r[n + "_b2"] = a[b2]
    win = a["L1_attn_W_in"]
    r["ss_router"] = padded(win[:, 768:772], 8)
    r["ss_win"] = win[:, 0:768]
    ch = np.zeros((128, 24), f)
    ch[:, 0:16] = a["L1_attn_conv_w"].reshape(4, 128, TAPS).transpose(1, 0, 2).reshape(128, 16)
    ch[:, 16:20] = a["L1_attn_conv_b"].reshape(4, 128).T
    ch[:, 20:22] = a["L1_attn_gnorm_w"].reshape(2, 128).T
    r["ss_ch"] = ch
    r["ss_drow"] = np.broadcast_to(a["L1_attn_D_skip"], (P, NS))
    r["ss_wout"] = a["L1_attn_W_out"].reshape(2, 128, D).transpose(1, 0, 2)
    r["fs_w1"] = a["L1_attn_ffn_w1"][None]
    r["fs_b1"] = a["L1_attn_ffn_b1"].reshape(1, 4, 128).transpose(0, 2, 1)
    r["fs_w2"] = a["L1_attn_ffn_w2"].reshape(1, 4, 128, D).transpose(0, 2, 1, 3).reshape(1, 128, 4 * D)
    r["f1_router"] = a["L1_ffn_Wr"]
    r["f2_router"] = a["L2_ffn_Wg"]
    wq, wv = (a[n].transpose(1, 0, 2).reshape(128, 512) for n in ("L2_attn_WQ", "L2_attn_WV"))
    r["a1_wqk"] = np.concatenate([wq, wv], 1).reshape(128, 1, 1024)
    r["a1_wv"] = wv.reshape(128, 1, 512)
    r["a1_wo"] = a["L2_attn_WU"].reshape(4, 128, 128).transpose(1, 0, 2)
    eye = np.eye(128, dtype=f)
    r["a2_own"] = qk_tiles(eye, eye)[:, 0:256]
    r["a2_wv"] = eye.reshape(128, 1, 128)
    by_e = lambda w: np.concatenate([w.transpose(1, 0, 2).reshape(64, 128), np.zeros((64, 128), f)])
    same = np.kron(np.eye(NH, dtype=f), np.ones((HD, HD), f))
    wvb = np.zeros((4, 2, 64, NH, SLOT), f)
    for h in range(NH):
        wvb[h // 2, h % 2, :, h, 0:HD] = a["L3_attn_wv"][h]
    r["a2_factors"] = np.concatenate([by_e(a["L3_attn_wk"]), qk_tiles(by_e(a["L3_attn_wq"]), eye)[:, 0:256],
                                      qk_tiles(same, eye)[:, 0:256],
                                      wvb.reshape(4, 128, 256).transpose(1, 0, 2).reshape(128, 1024),
                                      a["L3_attn_wo"].T.reshape(4, 128, 128).transpose(1, 0, 2).reshape(128, 512)], 1)
    rt = np.zeros((128, 128 + 1 + 8 + P + G), f)
    rt[:, 0:32] = a["L3_ffn_r_w1"]
    rt[0:32, 128] = a["L3_ffn_r_b1"]
    rt[0:32, 129:132] = a["L3_ffn_r_w2"]
    image = np.arange(G * TB)
    rt[0:G * TB, 137:137 + P] = image[:, None] % TB == tok[None, :] // S
    rt[0:G * TB, 137 + P:] = image[:, None] // TB == np.arange(G)[None, :]
    r["rt_w"] = rt
    heads = lambda w: w.reshape(128, -1, HD).repeat(NH * HD // w.shape[1], axis=1).reshape(128, 128)
    ws = [[a[f"L3_ffn_{n}{i}"] for n in ("wq", "wk", "wv", "wo")] for i in range(SETS)]
    r["a3_wqk"] = np.stack([qk_tiles(wq, heads(wk)) for wq, wk, _, _ in ws], 1)
    r["a3_wv"] = np.stack([heads(wv) for _, _, wv, _ in ws], 1)
    r["a3_wo"] = np.concatenate([head_rows(wo) for _, _, _, wo in ws], 2)
    return {k: np.ascontiguousarray(v) for k, v in r.items()}


def kernel(**inputs):
    import concourse.bacc as bacc
    from concourse.bass_utils import run_bass_kernel_spmd

    nc = bacc.Bacc("TRN2", target_bir_lowering=False, num_devices=1)
    arrays = laid_out({k: np.asarray(v) for k, v in inputs.items()})
    aps = {k: nc.dram_tensor(f"in_{k}", v.shape, mybir.dt.from_np(v.dtype), kind="ExternalInput").ap()
           for k, v in arrays.items()}
    out = nc.dram_tensor("out", (BATCH, S, D), F32, kind="ExternalOutput").ap()
    build(nc, aps, out)
    r = run_bass_kernel_spmd(nc, [{f"in_{k}": v for k, v in arrays.items()}], core_ids=[0])
    return r.results[0]["out"]
```

```python
from contextlib import ExitStack, contextmanager

import numpy as np

import concourse.bass as bass
from concourse import mybir

F32 = mybir.dt.float32
BF16 = mybir.dt.bfloat16
F32R = mybir.dt.float32r
ALU = mybir.AluOpType
ACT = mybir.ActivationFunctionType
AX = mybir.AxisListType.X

BATCH = 64
S = 36
D = 128
PATCH_K = 3 * 16 * 16
KC = PATCH_K // 128
TB = 3
P = TB * S
G = -(-BATCH // TB)
NH = 8
HD = 16
SLOT = 32
QUAD = 4
CHUNKS = [(c, min(QUAD, G - c)) for c in range(0, G, QUAD)]
EPS = 1e-5
NEG = -1.0e30


def steps(eng, step, depth):
    first = (depth + 2) // 2 * 2
    for t in range(first):
        step(t, t % 2)
    with eng.Fori(0, (G - first) // 2) as j:
        for u in range(2):
            step(j * 2 + (first + u), u)
    for t in range(G, G + depth - 1):
        step(t, t % 2)


def live(t, k):
    return not isinstance(t, int) or 0 <= t - k < G


def at_least(eng, sem, value):
    if not isinstance(value, int) or value > 0:
        eng.wait_ge(sem, value)


class Shared:
    pass


class Weights:

    def __init__(self, wv, scale, wqk=None, wo=None, own=None, factors=None):
        self.wqk, self.wv, self.wo, self.scale, self.own, self.factors = wqk, wv, wo, scale, own, factors
        self.fold = factors is not None


@contextmanager
def semaphores(nc, prefix):
    made = []
    with ExitStack() as ctx:
        def sem(name):
            made.append(ctx.enter_context(nc.semaphore(f"{prefix}_{name}")))
            return made[-1]
        yield sem
        with nc.Block() as block:
            @block.gpsimd
            def _(pool):
                for s in made:
                    pool.sem_clear(s)


def patch_phase(nc, m, io):
    with ExitStack() as ctx:
        sem = ctx.enter_context(semaphores(nc, "tok"))
        loaded = [sem(f"loaded{c}") for c in range(len(CHUNKS))]
        w_loaded = sem("w_loaded")
        proj_psum = sem("proj_psum")
        biased = sem("biased")
        turned = sem("turned")
        h_ready = sem("h_ready")
        pats = ctx.enter_context(nc.sbuf_tensor("pats", [128, KC, G * P], F32))
        tokw = ctx.enter_context(nc.sbuf_tensor("tokw", [128, KC * D], F32))
        bload = ctx.enter_context(nc.sbuf_tensor("bload", list(io["bconst"].shape), F32))
        hT = ctx.enter_context(nc.sbuf_tensor("tok_hT", [128, 2, QUAD * P], F32))
        block = ctx.enter_context(nc.Block())

        @block.sync
        def _(sp):
            sp.dma_start(m.const[:, :], io["const"]).then_inc(w_loaded, 16)
            sp.dma_start(tokw[:, :], io["tokw"]).then_inc(w_loaded, 16)
            for n, (c, k) in enumerate(CHUNKS):
                sp.dma_start(pats[:, :, c * P:(c + k) * P], io["patches"][:, :, c * P:(c + k) * P]).then_inc(loaded[n], 16)

        @block.tensor
        def _(pe):
            pe.wait_ge(w_loaded, 80)

            def project(n):
                c, k = CHUNKS[n]
                pe.wait_ge(loaded[n], 16)
                at_least(pe, biased, n - 1)
                for kc in range(KC):
                    mm = pe.matmul(m.bank[n % 2][:, 0:k * P], tokw[:, kc * D:(kc + 1) * D],
                                   pats[:, kc, c * P:(c + k) * P], start=(kc == 0), stop=(kc == KC - 1))
                mm.then_inc(proj_psum, 1)

            def turn(n):
                c, k = CHUNKS[n]
                pe.wait_ge(biased, n + 1)
                at_least(pe, h_ready, n - 1)
                for g in range(k):
                    mm = pe.transpose(m.bank[2 + n % 2][0:P, g * D:(g + 1) * D],
                                      hT[:, n % 2, g * P:(g + 1) * P], m.ident[:, :])
                mm.then_inc(turned, 1)

            project(0)
            for n in range(1, len(CHUNKS)):
                project(n)
                turn(n - 1)
            turn(len(CHUNKS) - 1)

        @block.scalar
        def _(act):
            act.dma_start(m.cols[:, :], io["cols"]).then_inc(w_loaded, 16)
            act.dma_start(m.rows[:, :], io["rows"]).then_inc(w_loaded, 16)
            act.dma_start(bload[:, :], io["bconst"]).then_inc(w_loaded, 16)
            act.wait_ge(w_loaded, 80)
            act.activation(m.bconst[:, :], bload[:, :], ACT.Copy)
            for n, (c, k) in enumerate(CHUNKS):
                act.wait_ge(proj_psum, n + 1)
                at_least(act, turned, n - 1)
                act.activation(hT[:, n % 2, 0:k * P], m.bank[n % 2][:, 0:k * P], ACT.Identity,
                               bias=m.col("tok_b")).then_inc(biased, 1)

        @block.vector
        def _(dve):
            for n, (c, k) in enumerate(CHUNKS):
                dve.wait_ge(turned, n + 1)
                dve.tensor_copy(m.H[:, c * D:(c + k) * D], m.bank[2 + n % 2][0:P, 0:k * D]).then_inc(h_ready, 1)
            dve.wait_ge(h_ready, len(CHUNKS))


def attention_phase(nc, m, name, w, hd=HD, nx=1, ending="add", masks=False):
    row = SLOT if hd == HD else hd
    heads_tile = 128 // row
    tiles = NH // heads_tile
    rounds = 2 * tiles // 4
    head_at = [n % tiles * heads_tile + n // tiles for n in range(NH)]
    post_norm = ending == "post_norm"
    depth = 7 if post_norm else 6
    with ExitStack() as ctx:
        sem = ctx.enter_context(semaphores(nc, name))
        sb = lambda s, shape, dt=F32: ctx.enter_context(nc.sbuf_tensor(f"{name}_{s}", shape, dt))
        w_loaded = sem("w_loaded")
        stat_chain = sem("stat_chain")
        var_eps = sem("var_eps")
        rstd_ready = sem("rstd_ready")
        xbase = sem("xbase")
        xn_ready = sem("xn_ready")
        xt_psum = sem("xt_psum")
        xt_ready = sem("xt_ready")
        qk_psum = sem("qk_psum")
        qk_ready = sem("qk_ready")
        v_psum = sem("v_psum")
        v_ready = sem("v_ready")
        s_psum = sem("s_psum")
        max_ready = sem("max_ready")
        shift_ready = sem("shift_ready")
        exps = sem("exps")
        pt_psum = sem("pt_psum")
        pt_ready = sem("pt_ready")
        rec_ready = sem("rec_ready")
        recs_ready = sem("recs_ready")
        o_psum = sem("o_psum")
        o_done = sem("o_done")
        y_psum = sem("y_psum")
        y_sum = sem("y_sum")
        y_done = sem("y_done")
        o_read = sem("o_read")
        pads_set = sem("pads_set")
        wqk = sb("wqk", [128, nx, 2 * tiles * 128])
        wv = sb("wv", [128, nx, NH * hd])
        wo = sb("wo", [128, tiles, nx * D])
        bn6 = sb("bn6", [P, 2, 6])
        mv = sb("mv", [P, 2, 2])
        ve = sb("ve", [P, 2, 1])
        rstd = sb("rstd", [P, 2, 1])
        xn = sb("xn", [P, 2, nx, D])
        xT = sb("xT", [128, 2, nx, P])
        qk = sb("qk", [128, 2, 2 * tiles, P])
        v = sb("v", [P, 2, NH, row])
        mx = sb("mx", [P, NH])
        shift = sb("shift", [P, 2, NH])
        total = sb("total", [P, 2, NH])
        E = sb("E", [P, 2, NH, P])
        pT = sb("pT", [P, 2, NH, P])
        rec = sb("rec", [P, NH])
        recs = sb("recs", [P, 2, NH, row])
        recT = sb("recT", [128, tiles * P])
        oT = sb("oT", [128, tiles * P])
        if w.fold:
            f_in = sb("f_in", [128, 128 + 256 + 256 + 4 * 256 + 4 * 128])
            f_wk, f_wq, f_same = f_in[:, 0:128], f_in[:, 128:384], f_in[:, 384:640]
            f_wv = lambda c, tile: f_in[:, 640 + c * 256 + tile * 128:640 + c * 256 + (tile + 1) * 128]
            f_wo = lambda c: f_in[:, 1664 + c * 128:1664 + (c + 1) * 128]
            fold_psum = sem("fold_psum")
            folded = sem("folded")
        if masks:
            xb = sb("xb", [P, D])
        if post_norm:
            xres_ready = sem("xres_ready")
            post_stats = sem("post_stats")
            post_eps = sem("post_eps")
            post_rstd = sem("post_rstd")
            post_normed = sem("post_normed")
            post_scaled = sem("post_scaled")
            h_done = sem("h_done")
            yt = sb("yt", [P, 2, D])
            bnb = sb("bnb", [P, 2, 6])
            mvb = sb("mvb", [P, 2, 2])
            veb = sb("veb", [P, 2, 1])
            rstdb = sb("rstdb", [P, 2, 1])
        xbank, obank, ptbank, sbank = m.bank[0], m.bank[2], m.bank[3], m.quad_bank
        qkbank = [m.bank[1], m.quad_bank[:, 2, :]][0:rounds]
        o_at = obank[:, 0:tiles * P]
        z_at = obank[:, tiles * P:2 * tiles * P] if 2 * tiles * P <= 512 else m.quad_bank[:, 3, 0:tiles * P]
        scores = sbank[0:P, 0:heads_tile, 0:tiles * P].rearrange("p b (s j) -> p b s j", s=tiles)
        block = ctx.enter_context(nc.Block())

        @block.sync
        def _(sp):
            if not w.fold:
                sp.dma_start(wqk[:, :, :], w.wqk).then_inc(w_loaded, 16)
                sp.dma_start(wo[:, :, :], w.wo).then_inc(w_loaded, 16)
            else:
                sp.dma_start(wqk[:, 0, 0:256], w.own).then_inc(w_loaded, 16)
                sp.dma_start(f_in[:, :], w.factors).then_inc(w_loaded, 16)
            sp.dma_start(wv[:, :, :], w.wv).then_inc(w_loaded, 16)

        @block.gpsimd
        def _(pool):
            def step(t, par):
                q = 1 - par
                if live(t, 0):
                    g = t
                    pool.wait_ge(stat_chain, g * 2 + 2)
                    at_least(pool, rstd_ready, g)
                    pool.tensor_tensor(ve[:, par, :], mv[:, par, 1:2], m.eps[0:P, :], ALU.add).then_inc(var_eps, 1)
                    pool.wait_ge(var_eps, g + 1)
                    at_least(pool, xn_ready, (g - 1) * nx)
                    pool.tensor_tensor(rstd[:, par, :], ve[:, par, :], m.mhalf[0:P, :], ALU.pow).then_inc(rstd_ready, 1)
                if post_norm and live(t, 1):
                    g = t - 1
                    pool.wait_ge(xn_ready, g + 1)
                    pool.tensor_tensor(m.XN[:, bass.ts(g, D)], xn[:, q, 0, :], m.row("a0_b_proj"), ALU.add).then_inc(xres_ready, 1)
                if post_norm and live(t, 6):
                    g = t - 6
                    pool.wait_ge(post_normed, g + 1)
                    pool.tensor_tensor(yt[:, par, :], yt[:, par, :], m.row("a0_gamma"), ALU.mult).then_inc(post_scaled, 1)
                    pool.wait_ge(post_scaled, g * 2 + 1)
                    pool.tensor_tensor(yt[:, par, :], yt[:, par, :], m.row("a0_beta"), ALU.add).then_inc(post_scaled, 1)
                    pool.wait_ge(post_scaled, g * 2 + 2)
                    h = m.H[:, bass.ts(g, D)]
                    pool.tensor_tensor(h, h, yt[:, par, :], ALU.add).then_inc(h_done, 1)
                if post_norm and live(t, 5):
                    g = t - 5
                    pool.wait_ge(post_stats, g * 2 + 2)
                    pool.tensor_tensor(veb[:, q, :], mvb[:, q, 1:2], m.eps[0:P, :], ALU.add).then_inc(post_eps, 1)
                    pool.wait_ge(post_eps, g + 1)
                    pool.tensor_tensor(rstdb[:, q, :], veb[:, q, :], m.mhalf[0:P, :], ALU.pow).then_inc(post_rstd, 1)
            steps(pool, step, depth)

        @block.tensor
        def _(pe):
            pe.wait_ge(w_loaded, 48)
            if w.fold:
                pe.matmul(m.bank[0][:, 0:256], f_wk, f_wq, start=True, stop=True).then_inc(fold_psum, 1)
                for tile in range(tiles):
                    for c in range(4):
                        mm = pe.matmul(m.bank[1][:, tile * 128:(tile + 1) * 128], f_wv(c, tile), f_wo(c), start=(c == 0), stop=(c == 3))
                mm.then_inc(fold_psum, 1)
                pe.wait_ge(folded, 2)
            pe.wait_ge(pads_set, 1)

            def probabilities(g, q, half):
                pe.wait_ge(exps, g * 2 + (half + 1))
                at_least(pe, pt_ready, g * 2 + half)
                for n in range(4 * half, 4 * half + 4):
                    mm = pe.transpose(ptbank[0:P, n % 4 * P:(n % 4 + 1) * P], E[:, q, n, :], m.ident[0:P, 0:P])
                mm.then_inc(pt_psum, 1)

            def queries_keys(g, par, r):
                at_least(pe, qk_ready, g * rounds + (r - (rounds - 1)))
                for n in range(4):
                    for x in range(nx):
                        c = (4 * r + n) * 128
                        mm = pe.matmul(qkbank[r][:, n * P:(n + 1) * P], wqk[:, x, c:c + 128],
                                       xT[:, par, x, :], start=(x == 0), stop=(x == nx - 1))
                mm.then_inc(qk_psum, 1)

            def scores_half(g, q, half):
                pe.wait_ge(qk_ready, g * rounds + rounds)
                at_least(pe, exps, g * 2 + (half - 1))
                banks = range(heads_tile // 2 * half, heads_tile // 2 * (half + 1))
                for b in banks:
                    pe.matmul(sbank[0:P, b, 0:tiles * P], m.img[row * b:row * b + TB, :],
                              m.not_img[row * b:row * b + TB, 0:tiles * P], start=True, stop=False, skip_group_check=True)
                for tile in range(tiles):
                    for b in banks:
                        mm = pe.matmul(sbank[0:P, b, tile * P:(tile + 1) * P], qk[row * b:row * b + hd, q, tile, :],
                                       qk[row * b:row * b + hd, q, tiles + tile, :], start=False, stop=(tile == tiles - 1),
                                       skip_group_check=True)
                mm.then_inc(s_psum, 1)

            def step(t, par):
                q = 1 - par
                if live(t, 3):
                    scores_half(t - 3, q, 0)
                if live(t, 2):
                    g = t - 2
                    pe.wait_ge(xn_ready, g * nx + nx)
                    at_least(pe, v_ready, g - 1)
                    for x in range(nx):
                        mm = pe.transpose(xbank[:, x * P:(x + 1) * P], xn[:, par, x, :], m.ident[0:P, 0:P])
                    mm.then_inc(xt_psum, 1)
                if live(t, 4):
                    probabilities(t - 4, par, 0)
                if live(t, 5):
                    g = t - 5
                    pe.wait_ge(o_done, g + 1)
                    if live(t, 2):
                        pe.wait_ge(xt_ready, g + 4)
                    elif live(t, 4):
                        pe.wait_ge(v_ready, g + 2)
                    for tile in range(tiles):
                        o = oT[:, tile * P:(tile + 1) * P]
                        if ending == "channels":
                            mm = pe.matmul(xbank[:, 0:P], wo[:, tile, :], o, start=(tile == 0), stop=(tile == tiles - 1))
                        else:
                            mm = pe.matmul(xbank[0:P, 0:nx * D], o, wo[:, tile, :], start=(tile == 0), stop=(tile == tiles - 1))
                    mm.then_inc(y_psum, 1)
                if live(t, 3):
                    scores_half(t - 3, q, 1)
                if live(t, 2):
                    pe.wait_ge(xt_ready, t - 2 + 1)
                    queries_keys(t - 2, par, 0)
                if live(t, 4):
                    probabilities(t - 4, par, 1)
                if live(t, 3):
                    g = t - 3
                    if live(t, 5):
                        pe.wait_ge(y_done, g - 1)
                    elif live(t, 2):
                        pe.wait_ge(xt_ready, g + 2)
                    for x in range(nx):
                        mm = pe.matmul(xbank[0:P, 0:NH * hd], xT[:, q, x, :], wv[:, x, :], start=(x == 0), stop=(x == nx - 1))
                    mm.then_inc(v_psum, 1)
                if live(t, 2) and rounds == 2:
                    queries_keys(t - 2, par, 1)
                if live(t, 4):
                    g = t - 4
                    at_least(pe, o_done, g)
                    pe.wait_ge(recs_ready, g + 1)
                    for tile in range(tiles):
                        pe.matmul(z_at[:, tile * P:(tile + 1) * P],
                                  recs[:, par, tile * heads_tile:(tile + 1) * heads_tile, :].rearrange("p n c -> p (n c)"),
                                  m.ident[0:P, 0:P], start=True, stop=True)
                    pe.wait_ge(pt_ready, g * 2 + 2)
                    pe.wait_ge(v_ready, g + 1)
                    for tile in range(tiles):
                        for r in range(heads_tile):
                            h = tile * heads_tile + r
                            mm = pe.matmul(o_at[row * r:row * (r + 1), tile * P:(tile + 1) * P], v[:, par, h, :],
                                           pT[:, par, head_at.index(h), :], start=True, stop=True)
                    mm.then_inc(o_psum, 1)
            steps(pe, step, depth)

        @block.scalar
        def _(act):
            act.wait_ge(pads_set, 1)

            def turned(g, par, half):
                act.wait_ge(pt_psum, g * 2 + half + 1)
                at_least(act, o_psum, g - 1)
                act.activation(pT[:, par, 4 * half:4 * half + 4, :].rearrange("p n j -> p (n j)"),
                               ptbank[0:P, 0:4 * P], ACT.Copy).then_inc(pt_ready, 1)

            def exponentials(g, q, half):
                act.wait_ge(shift_ready, g * 2 + half + 1)
                at_least(act, pt_psum, (g - 1) * 2)
                at_least(act, rec_ready, g - 1)
                for n in range(4 * half, 4 * half + 4):
                    e = act.activation(E[:, q, n, :], scores[:, n // tiles, n % tiles, :], ACT.Exp, scale=w.scale,
                                       bias=shift[:, q, n:n + 1], accum_out=total[:, q, n:n + 1])
                e.then_inc(exps, 1)

            def queries_keys(g, par, r):
                act.wait_ge(qk_psum, g * rounds + r + 1)
                at_least(act, s_psum, (g - 1) * 2)
                act.activation(qk[:, par, 4 * r:4 * r + 4, :].rearrange("p n j -> p (n j)"), qkbank[r][:, 0:4 * P],
                               ACT.Copy).then_inc(qk_ready, 1)

            def step(t, par):
                q = 1 - par
                if live(t, 2):
                    g = t - 2
                    act.wait_ge(xt_psum, g + 1)
                    at_least(act, v_psum, g - 1)
                    act.activation(xT[:, par, :, :].rearrange("p x j -> p (x j)"), xbank[:, 0:nx * P], ACT.Copy).then_inc(xt_ready, 1)
                if live(t, 4):
                    turned(t - 4, par, 0)
                if live(t, 3):
                    exponentials(t - 3, q, 0)
                if live(t, 2):
                    queries_keys(t - 2, par, 0)
                if live(t, 4):
                    turned(t - 4, par, 1)
                if live(t, 3):
                    g = t - 3
                    act.wait_ge(v_psum, g + 1)
                    at_least(act, o_psum, g - 1)
                    act.activation(v[:, q, :, 0:hd], xbank[0:P, 0:NH * hd].rearrange("p (n c) -> p n c", n=NH),
                                   ACT.Copy).then_inc(v_ready, 1)
                if live(t, 2) and rounds == 2:
                    queries_keys(t - 2, par, 1)
                if live(t, 3):
                    exponentials(t - 3, q, 1)
            steps(act, step, depth)

        @block.vector
        def _(dve):
            if w.fold:
                dve.wait_ge(fold_psum, 1)
                dve.wait_ge(w_loaded, 48)
                dve.tensor_tensor(wqk[:, 0, 256:512], m.bank[0][:, 0:256], f_same, ALU.mult).then_inc(folded, 1)
                dve.wait_ge(fold_psum, 2)
                dve.tensor_copy(wo[:, :, :].rearrange("p t d -> p (t d)"), m.bank[1][:, 0:tiles * 128]).then_inc(folded, 1)
            if row > hd:
                dve.memset(v[:, :, :, hd:row].rearrange("p a n c -> p (a n) c"), 0.0)
            dve.drain().then_inc(pads_set, 1)

            def maxima(g, q, half):
                dve.wait_ge(s_psum, g * 2 + (half + 1))
                banks = heads_tile // 2
                top = mx[:, 4 * half:4 * half + 4]
                at_least(dve, shift_ready, g * 2 + (half - 1))
                dve.tensor_reduce(top.rearrange("p (b s) -> p b s", s=tiles),
                                  scores[:, banks * half:banks * (half + 1), :, :], AX, ALU.max).then_inc(max_ready, 1)
                dve.wait_ge(max_ready, g * 2 + half + 1)
                at_least(dve, exps, (g - 1) * 2)
                dve.tensor_scalar(shift[:, q, 4 * half:4 * half + 4], top, -w.scale, None, ALU.mult).then_inc(shift_ready, 1)

            def step(t, par):
                q = 1 - par
                if live(t, 3):
                    maxima(t - 3, q, 0)
                if live(t, 5):
                    g = t - 5
                    dve.wait_ge(y_psum, g + 1)
                    h = m.H[:, bass.ts(g, D)]
                    if masks:
                        for x in range(nx):
                            if x:
                                dve.wait_ge(y_sum, g * (nx - 1) + x)
                            dve.scalar_tensor_tensor(out=h, in0=xbank[0:P, x * D:(x + 1) * D], scalar=m.MSK[:, bass.ds(g * nx + x, 1)],
                                                     in1=h, op0=ALU.mult, op1=ALU.add).then_inc(y_sum if x < nx - 1 else y_done, 1)
                    elif ending == "add":
                        dve.tensor_tensor(h, h, xbank[0:P, 0:D], ALU.add).then_inc(y_done, 1)
                    elif ending == "channels":
                        dve.tensor_copy(m.YT[:, bass.ts(g, P)], xbank[:, 0:P]).then_inc(y_done, 1)
                    else:
                        dve.wait_ge(xres_ready, g + 1)
                        at_least(dve, h_done, g - 1)
                        dve.tensor_tensor(yt[:, q, :], m.XN[:, bass.ts(g, D)], xbank[0:P, 0:D], ALU.add).then_inc(y_done, 1)
                if live(t, 4):
                    g = t - 4
                    dve.wait_ge(exps, g * 2 + 2)
                    at_least(dve, recs_ready, g)
                    dve.reciprocal(rec[:, :], total[:, par, :]).then_inc(rec_ready, 1)
                    dve.wait_ge(rec_ready, g + 1)
                    at_least(dve, o_psum, g - 1)
                    dve.tensor_copy(recs[:, par, :, :].rearrange("p (t r) c -> p t r c", t=tiles),
                                    rec[:, :].rearrange("p (r t) -> p t r", t=tiles).unsqueeze(3)
                                    .broadcast_to([P, tiles, heads_tile, row])).then_inc(recs_ready, 1)
                if live(t, 1):
                    g = t - 1
                    dve.wait_ge(rstd_ready, g + 1)
                    at_least(dve, xt_psum, g - 1)
                    if post_norm:
                        at_least(dve, xres_ready, g - 1)
                    x0 = xb[:, :] if masks else xn[:, q, 0, :]
                    if masks:
                        at_least(dve, xn_ready, g * nx)
                    dve.tensor_scalar(x0, m.H[:, bass.ts(g, D)], mv[:, q, 0:1], rstd[:, q, :],
                                      ALU.subtract, ALU.mult).then_inc(xbase if masks else xn_ready, 1)
                    if masks:
                        dve.wait_ge(xbase, g + 1)
                        for x in range(nx):
                            dve.tensor_scalar(xn[:, q, x, :], xb[:, :], m.MSK[:, bass.ds(g * nx + x, 1)], None,
                                              ALU.mult).then_inc(xn_ready, 1)
                if live(t, 3):
                    maxima(t - 3, q, 1)
                if post_norm and live(t, 6):
                    g = t - 6
                    dve.wait_ge(post_rstd, g + 1)
                    dve.tensor_scalar(yt[:, par, :], yt[:, par, :], mvb[:, par, 0:1], rstdb[:, par, :],
                                      ALU.subtract, ALU.mult).then_inc(post_normed, 1)
                if live(t, 0):
                    g = t
                    at_least(dve, var_eps, g - 1)
                    at_least(dve, xn_ready, (g - 1) * nx)
                    dve.bn_stats(bn6[:, par, :], m.H[:, bass.ts(g, D)]).then_inc(stat_chain, 1)
                    dve.drain()
                    dve.bn_aggr(mv[:, par, :], bn6[:, par, :]).then_inc(stat_chain, 1)
                if post_norm and live(t, 5):
                    g = t - 5
                    dve.wait_ge(y_done, g + 1)
                    dve.bn_stats(bnb[:, q, :], yt[:, q, :]).then_inc(post_stats, 1)
                    dve.drain()
                    dve.bn_aggr(mvb[:, q, :], bnb[:, q, :]).then_inc(post_stats, 1)
                if live(t, 4):
                    g = t - 4
                    dve.wait_ge(o_psum, g + 1)
                    at_least(dve, o_done, g)
                    dve.tensor_copy(recT[:, :], z_at).then_inc(o_read, 1)
                    dve.wait_ge(o_read, g + 1)
                    at_least(dve, y_psum, g)
                    dve.tensor_tensor(oT[:, :], o_at, recT[:, :], ALU.mult).then_inc(o_done, 1)
            steps(dve, step, depth)
            dve.wait_ge(y_done, G)


def group_statistics(dve, src, bn6, mv, done):
    for g in range(G):
        dve.bn_stats(bn6[:, g, :], src[:, g * D:(g + 1) * D])
    dve.drain()
    for g in range(G):
        ins = dve.bn_aggr(mv[:, g, :], bn6[:, g, :])
    ins.then_inc(done, 1)


def inverse_deviations(pool, m, mv, rstd, stats_ready, var_eps, rstd_ready):
    pool.wait_ge(stats_ready, 1)
    pool.tensor_tensor(rstd[:, :], mv[:, :, 1:2].rearrange("p g c -> p (g c)"), m.eps[0:P, :].broadcast_to([P, G]), ALU.add).then_inc(var_eps, 1)
    pool.wait_ge(var_eps, 1)
    pool.tensor_tensor(rstd[:, :], rstd[:, :], m.mhalf[0:P, :].broadcast_to([P, G]), ALU.pow).then_inc(rstd_ready, 1)


def prepare_phase(nc, m, name, router=None, bias=None, means=False):
    with ExitStack() as ctx:
        sem = ctx.enter_context(semaphores(nc, name))
        sb = lambda s, shape, dt=F32: ctx.enter_context(nc.sbuf_tensor(f"{name}_{s}", shape, dt))
        w_loaded = sem("w_loaded")
        stats_ready = sem("stats_ready")
        var_eps = sem("var_eps")
        rstd_ready = sem("rstd_ready")
        xn_ready = sem("xn_ready")
        xt_psum = sem("xt_psum")
        xt_ready = sem("xt_ready")
        lg_psum = sem("lg_psum")
        done = sem("done")
        bn6 = sb("bn6", [P, G, 6])
        mv = sb("mv", [P, G, 2])
        rstd = sb("rstd", [P, G])
        wr = sb("wr", [128, 8]) if router is not None else None
        block = ctx.enter_context(nc.Block())

        @block.sync
        def _(sp):
            if router is not None:
                sp.dma_start(wr[:, :], router).then_inc(w_loaded, 16)

        @block.gpsimd
        def _(pool):
            inverse_deviations(pool, m, mv, rstd, stats_ready, var_eps, rstd_ready)

        @block.tensor
        def _(pe):
            if router is not None:
                pe.wait_ge(w_loaded, 16)

            def route(n):
                c, k = CHUNKS[n]
                pe.wait_ge(xt_ready, n + 1)
                for g in range(c, c + k):
                    mm = pe.matmul(m.bank[2][0:P, g * 8:(g + 1) * 8], m.XT[:, g * P:(g + 1) * P], wr[:, :], start=True, stop=True)
                return mm
            for n, (c, k) in enumerate(CHUNKS):
                pe.wait_ge(xn_ready, n + 1)
                at_least(pe, xt_ready, n - 1)
                for g in range(k):
                    mm = pe.transpose(m.bank[n % 2][:, g * P:(g + 1) * P], m.XN[:, (c + g) * D:(c + g + 1) * D], m.ident[0:P, 0:P])
                mm.then_inc(xt_psum, 1)
                if router is not None and n:
                    route(n - 1)
            if router is not None:
                route(len(CHUNKS) - 1).then_inc(lg_psum, 1)

        @block.scalar
        def _(act):
            for n, (c, k) in enumerate(CHUNKS):
                act.wait_ge(xt_psum, n + 1)
                act.activation(m.XT[:, c * P:(c + k) * P], m.bank[n % 2][:, 0:k * P], ACT.Copy).then_inc(xt_ready, 1)

        @block.vector
        def _(dve):
            group_statistics(dve, m.H, bn6, mv, stats_ready)
            dve.wait_ge(rstd_ready, 1)
            dve.wait_ge(stats_ready, 1)
            for c, k in CHUNKS:
                for g in range(c, c + k):
                    ins = dve.tensor_scalar(m.XN[:, g * D:(g + 1) * D], m.H[:, g * D:(g + 1) * D], mv[:, g, 0:1],
                                            rstd[:, g:g + 1], ALU.subtract, ALU.mult)
                ins.then_inc(xn_ready, 1)
            if means:
                for n, (c, k) in enumerate(CHUNKS):
                    dve.wait_ge(xt_ready, n + 1)
                    dve.tensor_reduce(m.MEANS[:, c * TB:(c + k) * TB], m.XT[:, c * P:(c + k) * P].rearrange("p (b s) -> p b s", s=S),
                                      AX, ALU.add).then_inc(done, 1)
                dve.wait_ge(done, len(CHUNKS))
            if router is not None:
                dve.wait_ge(lg_psum, 1)
                dve.tensor_tensor(m.LG[:, :].rearrange("p (g e) -> p g e", e=8), m.bank[2][0:P, 0:G * 8].rearrange("p (g e) -> p g e", e=8),
                                  bias.unsqueeze(1).broadcast_to([P, G, 8]), ALU.add).then_inc(done, 1)
                dve.wait_ge(done, 1)


def chained(eng, sem):
    count = [0]

    def then(instruction):
        count[0] += 1
        instruction.then_inc(sem, 1)
        eng.wait_ge(sem, count[0])
    return then


def tree_gates(nc, m, name):
    with ExitStack() as ctx:
        sem = ctx.enter_context(semaphores(nc, name))
        own = sem("chain")
        sig = sem("sigmoid")
        left = ctx.enter_context(nc.sbuf_tensor(f"{name}_left", [P, G, 8], F32))
        right = ctx.enter_context(nc.sbuf_tensor(f"{name}_right", [P, G, 8], F32))
        lv1 = ctx.enter_context(nc.sbuf_tensor(f"{name}_lv2", [P, G, 4], F32))
        block = ctx.enter_context(nc.Block())

        @block.scalar
        def _(act):
            act.activation(right[:, :, :].rearrange("p g e -> p (g e)"), m.LG[:, :], ACT.Sigmoid).then_inc(sig, 1)

        @block.vector
        def _(dve):
            then = chained(dve, own)
            dve.wait_ge(sig, 1)
            then(dve.tensor_scalar(left[:, :, :], right[:, :, :], -1.0, 1.0, ALU.mult, ALU.add))
            gate = m.GATE[:, :].rearrange("p (g e) -> p g e", e=8)
            for i in range(2):
                up = (left, right)[i][:, :, 0:1]
                for side in range(2):
                    then(dve.tensor_tensor(lv1[:, :, 2 * i + side:2 * i + side + 1], up, (left, right)[side][:, :, 1 + i:2 + i], ALU.mult))
            for side in range(2):
                then(dve.tensor_tensor(gate[:, :, side:8:2], lv1[:, :, :], (left, right)[side][:, :, 3:7], ALU.mult))


def first_best(dve, m, then, dst, src, tmp, top, shape):
    w = shape[-1]
    then(dve.tensor_reduce(top, src, AX, ALU.max))
    then(dve.tensor_tensor(tmp, src, top.unsqueeze(2).broadcast_to(shape), ALU.is_ge))
    then(dve.tensor_tensor(tmp, tmp, m.rank[0:shape[0], 0:w].unsqueeze(1).broadcast_to(shape), ALU.mult))
    then(dve.tensor_reduce(top, tmp, AX, ALU.max))
    then(dve.tensor_tensor(dst, tmp, top.unsqueeze(2).broadcast_to(shape), ALU.is_equal))


def best_gates(nc, m, name, best):
    with ExitStack() as ctx:
        sb = lambda s, shape: ctx.enter_context(nc.sbuf_tensor(f"{name}_{s}", shape, F32))
        sem = ctx.enter_context(semaphores(nc, name))
        own = sem("chain")
        exped = sem("exped")
        shifted = sem("shifted")
        top, tot = sb("top", [P, G]), sb("tot", [P, G])
        pr, one, two, tmp = (sb(s, [P, G, 8]) for s in ("pr", "one", "two", "tmp"))
        block = ctx.enter_context(nc.Block())
        shape = [P, G, 8]
        lg = m.LG[:, :].rearrange("p (g e) -> p g e", e=8)
        gate = m.GATE[:, :].rearrange("p (g e) -> p g e", e=8)
        wide = lambda x: x[:, :].unsqueeze(2).broadcast_to(shape)

        @block.scalar
        def _(act):
            act.wait_ge(shifted, 1)
            act.activation(pr[:, :, :].rearrange("p g e -> p (g e)"), pr[:, :, :].rearrange("p g e -> p (g e)"), ACT.Exp).then_inc(exped, 1)

        @block.vector
        def _(dve):
            then = chained(dve, own)
            then(dve.tensor_reduce(top[:, :], lg, AX, ALU.max))
            dve.tensor_tensor(pr[:, :, :], lg, wide(top), ALU.subtract).then_inc(shifted, 1)
            dve.wait_ge(exped, 1)
            then(dve.tensor_reduce(tot[:, :], pr[:, :, :], AX, ALU.add))
            then(dve.reciprocal(tot[:, :], tot[:, :]))
            then(dve.tensor_tensor(pr[:, :, :], pr[:, :, :], wide(tot), ALU.mult))
            first_best(dve, m, then, one[:, :, :], pr[:, :, :], tmp[:, :, :], top[:, :], shape)
            if best == 1:
                then(dve.tensor_tensor(pr[:, :, :], pr[:, :, :], one[:, :, :], ALU.mult))
                then(dve.tensor_reduce(top[:, :], pr[:, :, :], AX, ALU.max))
                then(dve.reciprocal(tot[:, :], top[:, :]))
                then(dve.tensor_tensor(top[:, :], top[:, :], tot[:, :], ALU.mult))
                then(dve.tensor_tensor(gate, one[:, :, :], wide(top), ALU.mult))
            else:
                then(dve.scalar_tensor_tensor(out=two[:, :, :], in0=one[:, :, :], scalar=-2.0, in1=pr[:, :, :], op0=ALU.mult, op1=ALU.add))
                first_best(dve, m, then, two[:, :, :], two[:, :, :], tmp[:, :, :], top[:, :], shape)
                then(dve.tensor_tensor(one[:, :, :], one[:, :, :], two[:, :, :], ALU.add))
                then(dve.tensor_tensor(gate, pr[:, :, :], one[:, :, :], ALU.mult))


PARTS = [(0, 0), (0, 1), (1, 0)]


def experts_phase(nc, m, name, w1, w2, b1, func, experts, chunks, b2=None, dst=None):
    nb = len(CHUNKS)
    adds = [] if b2 is None else [(0, 4, 4), (4, 1, 4), (5, 1, G - 5 * QUAD)]
    before = len(adds)
    with ExitStack() as ctx:
        sem = ctx.enter_context(semaphores(nc, name))
        sb = lambda s, shape, dt=F32: ctx.enter_context(nc.sbuf_tensor(f"{name}_{s}", shape, dt))
        loaded = [sem("loaded0"), sem("loaded1")]
        b_loaded = sem("b_loaded")
        hid_psum = sem("hid_psum")
        hid_ready = sem("hid_ready")
        w_high = sem("w_high")
        w_split = sem("w_split")
        x_split = sem("x_split")
        y_psum = sem("y_psum")
        y_used = sem("y_used")
        w1s = sb("w1s", [128, 2, chunks * 128])
        w2s = sb("w2s", [128, 2, chunks * 128])
        b1s = sb("b1s", [128, 2, chunks])
        w1p = sb("w1p", [128, 2, 2, chunks * 128], F32R)
        xp = sb("xp", [128, 2, G * P], F32R)
        hid = sb("hid", [128, 2, chunks, QUAD * P])
        if b2 is not None:
            b2s = sb("b2s", [128, D])
            gs = sb("gs", [P, nb * QUAD, SLOT])
            gT = sb("gT", [128, nb * P])
            gs_ready = sem("gs_ready")
            gt_psum = sem("gt_psum")
            gt_ready = sem("gt_ready")
            gb_psum = sem("gb_psum")
        block = ctx.enter_context(nc.Block())

        @block.sync
        def _(sp):
            if b2 is not None:
                sp.dma_start(b2s[:, :], b2).then_inc(b_loaded, 16)

            def load(e, u):
                sp.dma_start(b1s[:, u, :], b1[bass.ds(e, 1), :, :].rearrange("e p n -> (e p) n")).then_inc(loaded[u], 16)
                sp.dma_start(w1s[:, u, :], w1[bass.ds(e, 1), :, :].rearrange("e p n -> (e p) n")).then_inc(loaded[u], 16)
                sp.dma_start(w2s[:, u, :], w2[bass.ds(e, 1), :, :].rearrange("e p n -> (e p) n")).then_inc(loaded[u], 16)
            for e in range(min(2, experts)):
                load(e, e)
            if experts > 2:
                with sp.Fori(1, experts // 2) as j:
                    for u in range(2):
                        sp.wait_ge(y_psum, (j * 2 + (u - 1)) * nb)
                        load(j * 2 + u, u)

        @block.gpsimd
        def _(pool):
            def split(e, j, u):
                pool.wait_ge(loaded[u], (j + 1) * 48)
                if not isinstance(e, int) or e > 1:
                    pool.wait_ge(y_psum, (j * 2 + (u - 1)) * nb)
                ones = m.one.broadcast_to([128, chunks * 128])
                pool.tensor_tensor(w1p[:, u, 0, :], w1s[:, u, :], ones, ALU.mult).then_inc(w_high, 1)
                pool.wait_ge(w_high, e + 1)
                pool.tensor_tensor(w1p[:, u, 1, :], w1s[:, u, :], w1p[:, u, 0, :], ALU.subtract).then_inc(w_split, 1)
            for e in range(min(2, experts)):
                split(e, 0, e)
            if experts > 2:
                with pool.Fori(1, experts // 2) as j:
                    for u in range(2):
                        split(j * 2 + u, j, u)

        @block.tensor
        def _(pe):
            if b2 is not None:
                pe.wait_ge(gs_ready, 1)
                for n in range(nb):
                    mm = pe.transpose(m.bank[n // 4][:, n % 4 * P:(n % 4 + 1) * P],
                                      gs[:, n * QUAD:(n + 1) * QUAD, :].rearrange("p g e -> p (g e)"), m.ident[0:P, 0:P])
                mm.then_inc(gt_psum, 1)
                pe.wait_ge(b_loaded, 16)
                pe.wait_ge(gt_ready, 2)
                for i, (n0, ns, k) in enumerate(adds):
                    at_least(pe, y_used, i)
                    for n in range(n0, n0 + ns):
                        for g in range(k):
                            mm = pe.matmul(m.quad_bank[0:P, g, (n - n0) * D:(n - n0 + 1) * D], gT[SLOT * g:SLOT * g + 8, n * P:(n + 1) * P],
                                           b2s[SLOT * g:SLOT * g + 8, :], start=True, stop=True)
                    mm.then_inc(gb_psum, 1)
                pe.wait_ge(y_used, before)

            def expert(e, j, u):
                def up(n):
                    c0, k = CHUNKS[n]
                    for c in range(chunks):
                        i = n * chunks + c
                        if i >= 4:
                            pe.wait_ge(hid_ready, e * (nb * chunks) + (i - 3))
                        for a, b in PARTS:
                            mm = pe.matmul(m.quad_bank[:, i % 4, 0:k * P], w1p[:, u, a, c * 128:(c + 1) * 128],
                                           xp[:, b, c0 * P:(c0 + k) * P], start=((a, b) == PARTS[0]), stop=((a, b) == PARTS[-1]))
                        mm.then_inc(hid_psum, 1)

                def down(n):
                    c0, k = CHUNKS[n]
                    pe.wait_ge(hid_ready, e * (nb * chunks) + (n + 1) * chunks)
                    if n == 0:
                        at_least(pe, y_used, e * nb + before)
                    elif n > 1:
                        pe.wait_ge(y_used, e * nb + (n - 1 + before))
                    for g in range(k):
                        for c in range(chunks):
                            mm = pe.matmul(m.bank[n % 2][0:P, g * D:(g + 1) * D], hid[:, n % 2, c, g * P:(g + 1) * P],
                                           w2s[:, u, c * 128:(c + 1) * 128], start=(c == 0), stop=(c == chunks - 1))
                    mm.then_inc(y_psum, 1)
                pe.wait_ge(loaded[u], (j + 1) * 48)
                pe.wait_ge(w_split, e + 1)
                up(0)
                for n in range(1, nb):
                    up(n)
                    down(n - 1)
                down(nb - 1)
            pe.wait_ge(x_split, nb)
            if experts == 1:
                expert(0, 0, 0)
            else:
                with pe.Fori(0, experts // 2) as j:
                    for u in range(2):
                        expert(j * 2 + u, j, u)

        @block.scalar
        def _(act):
            if b2 is not None:
                act.wait_ge(gt_psum, 1)
                for b in range(2):
                    k = min(4, nb - 4 * b)
                    act.activation(gT[:, 4 * b * P:(4 * b + k) * P], m.bank[b][:, 0:k * P], ACT.Copy).then_inc(gt_ready, 1)

            def expert(e, j, u):
                act.wait_ge(loaded[u], (j + 1) * 48)
                for n, (c0, k) in enumerate(CHUNKS):
                    for c in range(chunks):
                        act.wait_ge(hid_psum, e * (nb * chunks) + (n * chunks + c + 1))
                        if n > 1 and c == 0:
                            act.wait_ge(y_psum, e * nb + (n - 1))
                        act.activation(hid[:, n % 2, c, 0:k * P], m.quad_bank[:, (n * chunks + c) % 4, 0:k * P], func,
                                       bias=b1s[:, u, c:c + 1]).then_inc(hid_ready, 1)
            if experts == 1:
                expert(0, 0, 0)
            else:
                with act.Fori(0, experts // 2) as j:
                    for u in range(2):
                        expert(j * 2 + u, j, u)

        @block.vector
        def _(dve):
            if b2 is not None:
                dve.memset(gs[:, :, :].rearrange("p g e -> p (g e)"), 0.0)
                dve.drain()
                dve.tensor_copy(gs[:, 0:G, 0:8], m.GATE[:, :].rearrange("p (g e) -> p g e", e=8)).then_inc(gs_ready, 1)
            for c0, k in CHUNKS:
                dve.tensor_copy(xp[:, 0, c0 * P:(c0 + k) * P], m.XT[:, c0 * P:(c0 + k) * P])
            dve.drain()
            for c0, k in CHUNKS:
                cols = slice(c0 * P, (c0 + k) * P)
                dve.tensor_tensor(xp[:, 1, cols], m.XT[:, cols], xp[:, 0, cols], ALU.subtract).then_inc(x_split, 1)
            if b2 is not None:
                for i, (n0, ns, k) in enumerate(adds):
                    dve.wait_ge(gb_psum, i + 1)
                    h = dst[:, n0 * QUAD * D:(n0 * QUAD + (ns - 1) * QUAD + k) * D].rearrange("p (n g d) -> p g n d", n=ns, d=D)
                    dve.tensor_tensor(h, h, m.quad_bank[0:P, 0:k, 0:ns * D].rearrange("p g (n d) -> p g n d", d=D), ALU.add).then_inc(y_used, 1)

            def expert(e):
                at_least(dve, y_used, e * nb + before)
                for n, (c0, k) in enumerate(CHUNKS):
                    dve.wait_ge(y_psum, e * nb + (n + 1))
                    y = m.bank[n % 2][0:P, 0:k * D]
                    if b2 is None:
                        h = dst[:, c0 * D:(c0 + k) * D]
                        dve.tensor_tensor(h, h, y, ALU.add).then_inc(y_used, 1)
                        continue
                    for g in range(c0, c0 + k):
                        h = dst[:, g * D:(g + 1) * D]
                        ins = dve.scalar_tensor_tensor(out=h, in0=y[:, (g - c0) * D:(g - c0 + 1) * D],
                                                       scalar=m.GATE[:, bass.ds(e + g * 8, 1)], in1=h,
                                                       op0=ALU.mult, op1=ALU.add)
                    ins.then_inc(y_used, 1)
            if experts == 1:
                expert(0)
            else:
                with dve.Fori(0, experts) as e:
                    expert(e)
            dve.wait_ge(y_used, experts * nb + before)


NS = 4
CW = 2 * D
TAPS = 4
PADDED = S + TAPS - 1


def time_steps(nc, m):
    with ExitStack() as ctx:
        sb = lambda s, shape: ctx.enter_context(nc.sbuf_tensor(f"dt_{s}", shape, F32))
        sem = ctx.enter_context(semaphores(nc, "dt"))
        own = sem("chain")
        absolute = sem("absolute")
        exped = sem("exped")
        u, r, r2, q = (sb(n, [P, G * 8]) for n in ("u", "r", "r2", "q"))
        a = sb("a", [P, 8])
        block = ctx.enter_context(nc.Block())

        @block.scalar
        def _(act):
            act.activation(a[:, :], m.small("A_log"), ACT.Exp).then_inc(exped, 1)
            act.wait_ge(absolute, 1)
            act.activation(u[:, :], r[:, :], ACT.Exp, scale=-1.0).then_inc(exped, 1)

        @block.vector
        def _(dve):
            then = chained(dve, own)
            dve.scalar_tensor_tensor(out=r[:, :], in0=m.LG[:, :], scalar=-1.0, in1=m.LG[:, :], op0=ALU.mult, op1=ALU.max).then_inc(absolute, 1)
            dve.wait_ge(exped, 2)
            then(dve.tensor_scalar(q[:, :], u[:, :], 2.0, None, ALU.add))
            then(dve.reciprocal(q[:, :], q[:, :]))
            then(dve.tensor_tensor(r[:, :], u[:, :], q[:, :], ALU.mult))
            then(dve.tensor_tensor(r2[:, :], r[:, :], r[:, :], ALU.mult))
            then(dve.tensor_scalar(q[:, :], r2[:, :], 1.0 / 17, None, ALU.mult))
            for k in (15, 13, 11, 9, 7, 5, 3):
                then(dve.scalar_tensor_tensor(out=q[:, :], in0=q[:, :], scalar=1.0 / k, in1=r2[:, :], op0=ALU.add, op1=ALU.mult))
            then(dve.scalar_tensor_tensor(out=q[:, :], in0=q[:, :], scalar=1.0, in1=r[:, :], op0=ALU.add, op1=ALU.mult))
            then(dve.tensor_scalar(u[:, :], m.LG[:, :], 0.0, None, ALU.max))
            then(dve.scalar_tensor_tensor(out=m.DT[:, :], in0=q[:, :], scalar=2.0, in1=u[:, :], op0=ALU.mult, op1=ALU.add))
            then(dve.scalar_tensor_tensor(out=m.DTA[:, :].rearrange("p (g e) -> p g e", e=8), in0=m.DT[:, :].rearrange("p (g e) -> p g e", e=8),
                                          scalar=-1.0, in1=a[:, :].unsqueeze(1).broadcast_to([P, G, 8]), op0=ALU.mult, op1=ALU.mult))


def state_space_phase(nc, m, io):
    with ExitStack() as ctx:
        sem = ctx.enter_context(semaphores(nc, "ss"))
        sb = lambda s, shape, dt=F32: ctx.enter_context(nc.sbuf_tensor(f"ss_{s}", shape, dt))
        w_loaded = sem("w_loaded")
        prepared = sem("prepared")
        xbc_psum = sem("xbc_psum")
        padded = sem("padded")
        conv = sem("conv")
        tanhed = sem("tanhed")
        silu = sem("silu")
        xts_ready = sem("xts_ready")
        xc_psum = sem("xc_psum")
        xc_ready = sem("xc_ready")
        cum_ready = sem("cum_ready")
        seg_psum = sem("seg_psum")
        decay = sem("decay")
        z_psum = sem("z_psum")
        z_tanh = sem("z_tanh")
        z_ready = sem("z_ready")
        masked = sem("masked")
        xdt_ready = sem("xdt_ready")
        mix_ready = sem("mix_ready")
        y_psum = sem("y_psum")
        yz_ready = sem("yz_ready")
        ssq_ready = sem("ssq_ready")
        rms_steps = sem("rms_steps")
        rms_ready = sem("rms_ready")
        yt_psum = sem("yt_psum")
        yt_ready = sem("yt_ready")
        o_psum = sem("o_psum")
        sum_ready = sem("sum_ready")
        stats = sem("stats")
        eps_added = sem("eps_added")
        rstd_ready = sem("rstd_ready")
        normed = sem("normed")
        scaled = sem("scaled")
        t_psum = sem("t_psum")
        t_ready = sem("t_ready")
        win = sb("win", [128, 6 * 128])
        wout = sb("wout", [128, 2, D])
        ch = sb("ch", [128, 24])
        half = sb("half", [128, 20])
        drow = sb("drow", [P, NS])
        dI = sb("dI", [P, NS, P])
        xp = sb("xp", [128, 2, 4 * TB, PADDED])
        cv = sb("cv", [128, 2, 4, P])
        th = sb("th", [128, 4 * P])
        sx = sb("sx", [128, 2, 4, P])
        xTs = sb("xTs", [128, 2, P])
        cum = sb("cum", [P, 2, NS, P])
        xc = sb("xc", [P, 2, CW + P])
        cbm = sb("cbm", [P, P])
        L = sb("L", [P, NS, P])
        M = sb("M", [P, 2, NS, P])
        xdt = sb("xdt", [P, 2, CW])
        zs = sb("zs", [P, 2, CW])
        yz = sb("yz", [P, 2, CW])
        sq = sb("sq", [P, CW])
        ssq = sb("ssq", [P, 2, 1])
        rms = sb("rms", [P, 2, 1])
        yT = sb("yT", [128, 2 * P])
        yt = sb("yt", [P, 2, D])
        bn6 = sb("bn6", [P, 2, 6])
        mv = sb("mv", [P, 2, 2])
        ve = sb("ve", [P, 2, 1])
        rstd = sb("rstd", [P, 2, 1])
        tt = sb("tt", [P, 2, D])
        seg_bank, y_bank, o_bank, t_bank = (m.quad_bank[:, b, :] for b in range(4))
        depth = 7
        block = ctx.enter_context(nc.Block())

        @block.sync
        def _(sp):
            for dst, src in ((win, io["ss_win"]), (ch, io["ss_ch"]), (drow, io["ss_drow"])):
                sp.dma_start(dst[:, :], src).then_inc(w_loaded, 16)
            sp.dma_start(wout[:, :, :], io["ss_wout"]).then_inc(w_loaded, 16)

        @block.gpsimd
        def _(pool):
            def step(t, par):
                q = 1 - par
                if live(t, 1):
                    g = t - 1
                    at_least(pool, z_psum, g - 1)
                    pool.tensor_copy(xTs[:, q, :], m.XT[:, bass.ts(g, P)]).then_inc(xts_ready, 1)
                if live(t, 5):
                    g = t - 5
                    pool.wait_ge(normed, g + 1)
                    at_least(pool, t_psum, g - 1)
                    pool.tensor_tensor(tt[:, q, :], yt[:, q, :], m.row("n1_g"), ALU.mult).then_inc(scaled, 1)
                    pool.wait_ge(scaled, g * 3 + 1)
                    pool.tensor_tensor(tt[:, q, :], tt[:, q, :], m.row("n1_b"), ALU.add).then_inc(scaled, 1)
                    pool.wait_ge(scaled, g * 3 + 2)
                    pool.tensor_tensor(m.T[:, bass.ts(g, D)], tt[:, q, :], m.row("ffn_b2"), ALU.add).then_inc(scaled, 1)
                if live(t, 3):
                    g = t - 3
                    pool.wait_ge(ssq_ready, g + 1)
                    pool.tensor_tensor(ssq[:, q, :], ssq[:, q, :], m.inv_cw[0:P, :], ALU.mult).then_inc(rms_steps, 1)
                    pool.wait_ge(rms_steps, g * 2 + 1)
                    pool.tensor_tensor(ssq[:, q, :], ssq[:, q, :], m.eps[0:P, :], ALU.add).then_inc(rms_steps, 1)
                    pool.wait_ge(rms_steps, g * 2 + 2)
                    at_least(pool, sum_ready, g - 1)
                    pool.tensor_tensor(rms[:, q, :], ssq[:, q, :], m.mhalf[0:P, :], ALU.pow).then_inc(rms_ready, 1)
                if live(t, 4):
                    g = t - 4
                    pool.wait_ge(stats, g * 2 + 2)
                    pool.tensor_tensor(ve[:, par, :], mv[:, par, 1:2], m.eps[0:P, :], ALU.add).then_inc(eps_added, 1)
                    pool.wait_ge(eps_added, g + 1)
                    at_least(pool, normed, g - 1)
                    pool.tensor_tensor(rstd[:, par, :], ve[:, par, :], m.mhalf[0:P, :], ALU.pow).then_inc(rstd_ready, 1)
            steps(pool, step, depth)
            pool.wait_ge(scaled, 3 * G)

        @block.tensor
        def _(pe):
            pe.wait_ge(w_loaded, 64)
            pe.wait_ge(prepared, 3)

            def step(t, par):
                q = 1 - par
                if live(t, 0):
                    g = t
                    at_least(pe, padded, g)
                    for c in range(4):
                        mm = pe.matmul(m.bank[2][:, c * P:(c + 1) * P], win[:, (2 + c) * 128:(3 + c) * 128],
                                       m.XT[:, bass.ts(g, P)], start=True, stop=True)
                    mm.then_inc(xbc_psum, 1)
                if live(t, 2):
                    g = t - 2
                    pe.wait_ge(cum_ready, g + 1)
                    at_least(pe, decay, g)
                    pe.matmul(seg_bank[0:P, 0:NS * P], m.later, cum[:, par, :, :].rearrange("p n j -> p (n j)"),
                              start=True, stop=True).then_inc(seg_psum, 1)
                    pe.wait_ge(silu, g + 1)
                    at_least(pe, xc_ready, g)
                    for c in range(2):
                        pe.transpose(m.bank[3][0:P, c * 128:(c + 1) * 128], sx[:, par, c, :], m.ident[:, :])
                    pe.matmul(m.bank[3][0:P, CW:CW + P], sx[:, par, 2, :], sx[:, par, 3, :], start=True, stop=True).then_inc(xc_psum, 1)
                    pe.wait_ge(xts_ready, g + 1)
                    at_least(pe, z_ready, g)
                    pe.matmul(m.bank[1][0:P, 0:CW], xTs[:, par, :], win[:, 0:CW], start=True, stop=True).then_inc(z_psum, 1)
                if live(t, 4):
                    g = t - 4
                    pe.wait_ge(yz_ready, g + 1)
                    at_least(pe, yt_ready, g)
                    for c in range(2):
                        mm = pe.transpose(m.bank[0][:, c * P:(c + 1) * P], yz[:, par, c * 128:(c + 1) * 128], m.ident[0:P, 0:P])
                    mm.then_inc(yt_psum, 1)
                if live(t, 3):
                    g = t - 3
                    pe.wait_ge(mix_ready, g + 1)
                    pe.wait_ge(xdt_ready, g + 1)
                    at_least(pe, yz_ready, g)
                    for n in range(NS):
                        cols = slice(n * 64, (n + 1) * 64)
                        pe.matmul(y_bank[0:P, cols], dI[:, n, :], xc[:, q, cols], start=True, stop=False, skip_group_check=True)
                        mm = pe.matmul(y_bank[0:P, cols], M[:, q, n, :], xdt[:, q, cols], start=False, stop=True, skip_group_check=True)
                    mm.then_inc(y_psum, 1)
                if live(t, 4):
                    g = t - 4
                    pe.wait_ge(yt_ready, g + 1)
                    at_least(pe, sum_ready, g)
                    for c in range(2):
                        mm = pe.matmul(o_bank[0:P, 0:D], yT[:, c * P:(c + 1) * P], wout[:, c, :], start=(c == 0), stop=(c == 1))
                    mm.then_inc(o_psum, 1)
                if live(t, 6):
                    g = t - 6
                    pe.wait_ge(scaled, g * 3 + 2)
                    at_least(pe, t_ready, g)
                    pe.transpose(t_bank[:, 0:P], tt[:, par, :], m.ident[0:P, 0:P]).then_inc(t_psum, 1)
            steps(pe, step, depth)

        @block.scalar
        def _(act):
            act.wait_ge(prepared, 3)

            def step(t, par):
                q = 1 - par
                if live(t, 0):
                    g = t
                    act.wait_ge(xbc_psum, g + 1)
                    at_least(act, conv, (g - 1) * 16)
                    act.activation(xp[:, par, :, TAPS - 1:PADDED], m.bank[2][:, 0:4 * P].rearrange("p (b s) -> p b s", s=S),
                                   ACT.Copy).then_inc(padded, 1)
                if live(t, 1):
                    g = t - 1
                    act.wait_ge(conv, g * 16 + 16)
                    at_least(act, silu, g)
                    act.activation(th[:, :], cv[:, q, :, :].rearrange("p c j -> p (c j)"), ACT.Tanh).then_inc(tanhed, 1)
                if live(t, 2):
                    g = t - 2
                    act.wait_ge(seg_psum, g + 1)
                    at_least(act, mix_ready, g)
                    act.activation(L[:, :, :].rearrange("p n j -> p (n j)"), seg_bank[0:P, 0:NS * P], ACT.Exp).then_inc(decay, 1)
                    act.wait_ge(xc_psum, g + 1)
                    at_least(act, y_psum, g - 1)
                    act.activation(xc[:, par, :], m.bank[3][0:P, 0:CW + P], ACT.Copy).then_inc(xc_ready, 1)
                    act.wait_ge(z_psum, g + 1)
                    at_least(act, yz_ready, g - 1)
                    act.activation(zs[:, par, :], m.bank[1][0:P, 0:CW], ACT.Tanh, scale=0.5).then_inc(z_tanh, 1)
                if live(t, 4):
                    g = t - 4
                    act.wait_ge(yt_psum, g + 1)
                    at_least(act, o_psum, g)
                    act.activation(yT[:, :], m.bank[0][:, 0:2 * P], ACT.Copy).then_inc(yt_ready, 1)
                if live(t, 3):
                    g = t - 3
                    act.wait_ge(yz_ready, g + 1)
                    at_least(act, rms_ready, g - 1)
                    at_least(act, ssq_ready, g)
                    act.activation(sq[:, :], yz[:, q, :], ACT.Square, accum_out=ssq[:, q, :]).then_inc(ssq_ready, 1)
                if live(t, 6):
                    g = t - 6
                    act.wait_ge(t_psum, g + 1)
                    act.activation(m.XT[:, bass.ts(g, P)], t_bank[:, 0:P], ACT.Copy).then_inc(t_ready, 1)
            steps(act, step, depth)

        @block.vector
        def _(dve):
            dve.wait_ge(w_loaded, 64)
            dve.memset(xp[:, :, :, 0:TAPS - 1].rearrange("p a b k -> p (a b) k"), 0.0).then_inc(prepared, 1)
            dve.tensor_scalar(half[:, :], ch[:, 0:20], 0.5, None, ALU.mult).then_inc(prepared, 1)
            for c in range(2):
                dve.tensor_scalar(wout[:, c, :], wout[:, c, :], ch[:, 20 + c:21 + c], None, ALU.mult)
            for n in range(NS):
                ins = dve.tensor_scalar(dI[:, n, :], m.ident[0:P, 0:P], drow[:, n:n + 1], None, ALU.mult)
            ins.then_inc(prepared, 1)
            dve.wait_ge(prepared, 3)

            def step(t, par):
                q = 1 - par
                if live(t, 1):
                    g = t - 1
                    dve.wait_ge(padded, g + 1)
                    at_least(dve, tanhed, g - 1)
                    at_least(dve, silu, g - 1)
                    for k in range(TAPS):
                        for c in range(4):
                            x = xp[:, q, c * TB:(c + 1) * TB, k:k + S]
                            y = cv[:, q, c, :].rearrange("p (b s) -> p b s", s=S)
                            tap = half[:, c * TAPS + k:c * TAPS + k + 1]
                            if k == 0:
                                dve.tensor_scalar(y, x, tap, half[:, 16 + c:17 + c], ALU.mult, ALU.add).then_inc(conv, 1)
                            else:
                                dve.wait_ge(conv, g * 16 + (4 * k + c - 3))
                                dve.scalar_tensor_tensor(out=y, in0=x, scalar=tap, in1=y, op0=ALU.mult, op1=ALU.add).then_inc(conv, 1)
                    at_least(dve, seg_psum, g - 1)
                    dve.tensor_tensor(cum[:, q, :, :], m.upto.unsqueeze(1).broadcast_to([P, NS, P]),
                                      m.DTA[:, bass.ds(g * 8, NS)].unsqueeze(2).broadcast_to([P, NS, P]), ALU.mult).then_inc(cum_ready, 1)
                if live(t, 2):
                    g = t - 2
                    dve.wait_ge(xc_ready, g + 1)
                    at_least(dve, mix_ready, g)
                    dve.tensor_tensor(cbm[:, :], xc[:, par, CW:CW + P], m.upto, ALU.mult).then_inc(masked, 1)
                    at_least(dve, y_psum, g - 1)
                    dve.tensor_tensor(xdt[:, par, :].rearrange("p (n c) -> p n c", n=NS), xc[:, par, 0:CW].rearrange("p (n c) -> p n c", n=NS),
                                      m.DT[:, bass.ds(g * 8, NS)].unsqueeze(2).broadcast_to([P, NS, 64]), ALU.mult).then_inc(xdt_ready, 1)
                    dve.wait_ge(decay, g + 1)
                    dve.wait_ge(masked, g + 1)
                    dve.tensor_tensor(M[:, par, :, :], L[:, :, :], cbm[:, :].unsqueeze(1).broadcast_to([P, NS, P]), ALU.mult).then_inc(mix_ready, 1)
                    dve.wait_ge(z_tanh, g + 1)
                    dve.scalar_tensor_tensor(out=zs[:, par, :], in0=zs[:, par, :], scalar=1.0, in1=m.bank[1][0:P, 0:CW],
                                             op0=ALU.add, op1=ALU.mult).then_inc(z_ready, 1)
                if live(t, 5):
                    g = t - 5
                    dve.wait_ge(rstd_ready, g + 1)
                    dve.tensor_scalar(yt[:, q, :], yt[:, q, :], mv[:, q, 0:1], rstd[:, q, :], ALU.subtract, ALU.mult).then_inc(normed, 1)
                if live(t, 1):
                    g = t - 1
                    dve.wait_ge(tanhed, g + 1)
                    at_least(dve, xc_psum, g - 1)
                    dve.scalar_tensor_tensor(out=sx[:, q, :, :].rearrange("p c j -> p (c j)"), in0=th[:, :], scalar=1.0,
                                             in1=cv[:, q, :, :].rearrange("p c j -> p (c j)"), op0=ALU.add, op1=ALU.mult).then_inc(silu, 1)
                if live(t, 3):
                    g = t - 3
                    dve.wait_ge(y_psum, g + 1)
                    at_least(dve, yt_psum, g - 1)
                    at_least(dve, ssq_ready, g - 1)
                    dve.wait_ge(z_ready, g + 1)
                    dve.scalar_tensor_tensor(out=yz[:, q, :], in0=y_bank[0:P, 0:CW], scalar=0.5, in1=zs[:, q, :],
                                             op0=ALU.mult, op1=ALU.mult).then_inc(yz_ready, 1)
                if live(t, 4):
                    g = t - 4
                    dve.wait_ge(o_psum, g + 1)
                    dve.wait_ge(rms_ready, g + 1)
                    at_least(dve, normed, g - 1)
                    at_least(dve, scaled, (g - 2) * 3 + 1) if not isinstance(t, int) or g > 1 else None
                    dve.scalar_tensor_tensor(out=yt[:, par, :], in0=o_bank[0:P, 0:D], scalar=rms[:, par, :],
                                             in1=m.XN[:, bass.ts(g, D)], op0=ALU.mult, op1=ALU.add).then_inc(sum_ready, 1)
                    dve.wait_ge(sum_ready, g + 1)
                    at_least(dve, eps_added, g - 1)
                    dve.bn_stats(bn6[:, par, :], yt[:, par, :]).then_inc(stats, 1)
                    dve.drain()
                    dve.bn_aggr(mv[:, par, :], bn6[:, par, :]).then_inc(stats, 1)
            steps(dve, step, depth)


def close_phase(nc, m):
    with ExitStack() as ctx:
        sem = ctx.enter_context(semaphores(nc, "cl"))
        sb = lambda s, shape: ctx.enter_context(nc.sbuf_tensor(f"cl_{s}", shape, F32))
        stats_ready = sem("stats_ready")
        var_eps = sem("var_eps")
        rstd_ready = sem("rstd_ready")
        normed = sem("normed")
        scaled = sem("scaled")
        moved = sem("moved")
        h_done = sem("h_done")
        bn6, mv, rstd = sb("bn6", [P, G, 6]), sb("mv", [P, G, 2]), sb("rstd", [P, G])
        wide = lambda row, k: m.row(row).unsqueeze(1).broadcast_to([P, k, D])
        block = ctx.enter_context(nc.Block())

        @block.gpsimd
        def _(pool):
            inverse_deviations(pool, m, mv, rstd, stats_ready, var_eps, rstd_ready)
            for n, (c, k) in enumerate(CHUNKS):
                pool.wait_ge(normed, n + 1)
                x = m.T[:, c * D:(c + k) * D].rearrange("p (g d) -> p g d", d=D)
                pool.tensor_tensor(x, x, wide("n3_g", k), ALU.mult).then_inc(scaled, 1)

        @block.vector
        def _(dve):
            group_statistics(dve, m.T, bn6, mv, stats_ready)
            for c, k in CHUNKS:
                h = m.H[:, c * D:(c + k) * D].rearrange("p (g d) -> p g d", d=D)
                ins = dve.tensor_tensor(h, h, wide("n3_b", k), ALU.add)
            ins.then_inc(moved, 1)
            dve.wait_ge(rstd_ready, 1)
            dve.wait_ge(stats_ready, 1)
            for c, k in CHUNKS:
                for g in range(c, c + k):
                    x = m.T[:, g * D:(g + 1) * D]
                    ins = dve.tensor_scalar(x, x, mv[:, g, 0:1], rstd[:, g:g + 1], ALU.subtract, ALU.mult)
                ins.then_inc(normed, 1)
            dve.wait_ge(moved, 1)
            for n, (c, k) in enumerate(CHUNKS):
                dve.wait_ge(scaled, n + 1)
                h = m.H[:, c * D:(c + k) * D]
                dve.tensor_tensor(h, h, m.T[:, c * D:(c + k) * D], ALU.add).then_inc(h_done, 1)
            dve.wait_ge(h_done, len(CHUNKS))


def batch_norm_phase(nc, m):
    real = BATCH * S
    parts = -(-real // 512)
    while real % parts:
        parts += 1
    part = real // parts
    with ExitStack() as ctx:
        sem = ctx.enter_context(semaphores(nc, "bn"))
        sb = lambda s, shape: ctx.enter_context(nc.sbuf_tensor(f"bn_{s}", shape, F32))
        own = sem("own")
        stats_ready = sem("stats_ready")
        pool_own = sem("pool_own")
        rstd_ready = sem("rstd_ready")
        affine_ready = sem("affine_ready")
        relued = sem("relued")
        turned = sem("turned")
        h_ready = sem("h_ready")
        bn6, mv, ve, rstd = sb("bn6", [128, parts, 6]), sb("mv", [128, 2]), sb("ve", [128, 1]), sb("rstd", [128, 1])
        scale, shift = sb("scale", [128, 1]), sb("shift", [128, 1])
        block = ctx.enter_context(nc.Block())

        @block.gpsimd
        def _(pool):
            pool.wait_ge(stats_ready, 1)
            pool.tensor_tensor(ve[:, :], mv[:, 1:2], m.eps, ALU.add).then_inc(pool_own, 1)
            pool.wait_ge(pool_own, 1)
            pool.tensor_tensor(rstd[:, :], ve[:, :], m.mhalf, ALU.pow).then_inc(rstd_ready, 1)

        @block.tensor
        def _(pe):
            for n, (c, k) in enumerate(CHUNKS):
                pe.wait_ge(relued, n + 1)
                at_least(pe, h_ready, n - 1)
                for g in range(k):
                    mm = pe.transpose(m.bank[n % 2][0:P, g * D:(g + 1) * D], m.YT[:, (c + g) * P:(c + g + 1) * P], m.ident[:, :])
                mm.then_inc(turned, 1)

        @block.scalar
        def _(act):
            act.wait_ge(affine_ready, 1)
            for n, (c, k) in enumerate(CHUNKS):
                y = m.YT[:, c * P:(c + k) * P]
                act.activation(y, y, ACT.Relu, scale=scale[:, :], bias=shift[:, :]).then_inc(relued, 1)

        @block.vector
        def _(dve):
            for n in range(parts):
                dve.bn_stats(bn6[:, n, :], m.YT[:, n * part:(n + 1) * part])
            dve.drain()
            dve.bn_aggr(mv[:, :], bn6[:, :, :]).then_inc(stats_ready, 1)
            then = chained(dve, own)
            dve.wait_ge(rstd_ready, 1)
            then(dve.tensor_tensor(scale[:, :], m.col("bn_gamma"), rstd[:, :], ALU.mult))
            then(dve.tensor_tensor(shift[:, :], mv[:, 0:1], scale[:, :], ALU.mult))
            dve.tensor_tensor(shift[:, :], m.col("bn_beta"), shift[:, :], ALU.subtract).then_inc(affine_ready, 1)
            for n, (c, k) in enumerate(CHUNKS):
                dve.wait_ge(turned, n + 1)
                h = m.H[:, c * D:(c + k) * D]
                dve.tensor_tensor(h, h, m.bank[n % 2][0:P, 0:k * D], ALU.add).then_inc(h_ready, 1)
            dve.wait_ge(h_ready, len(CHUNKS))


SETS = 3


def routes_phase(nc, m, io):
    B = G * TB
    with ExitStack() as ctx:
        sem = ctx.enter_context(semaphores(nc, "rt"))
        sb = lambda s, shape: ctx.enter_context(nc.sbuf_tensor(f"rt_{s}", shape, F32))
        w_loaded = sem("w_loaded")
        psum = sem("psum")
        hid_ready = sem("hid_ready")
        shifted = sem("shifted")
        exped = sem("exped")
        own = sem("own")
        spread_ready = sem("spread_ready")
        rw = sb("rw", [128, 128 + 1 + 8 + P + G])
        hid = sb("hid", [128, B])
        lg, pr, one, tmp = (sb(n, [B, 1, SETS]) for n in ("lg", "pr", "one", "tmp"))
        top, tot = sb("top", [B, 1]), sb("tot", [B, 1])
        spread = sb("spread", [B, G, SETS])
        block = ctx.enter_context(nc.Block())
        wide = lambda x: x[:, :].unsqueeze(2).broadcast_to([B, 1, SETS])

        @block.sync
        def _(sp):
            sp.dma_start(rw[:, :], io["rt_w"]).then_inc(w_loaded, 16)

        @block.tensor
        def _(pe):
            pe.wait_ge(w_loaded, 16)
            pe.matmul(m.bank[0][:, 0:B], rw[:, 0:128], m.MEANS[:, :], start=True, stop=True).then_inc(psum, 1)
            pe.wait_ge(hid_ready, 1)
            pe.matmul(m.bank[1][0:B, 0:8], hid[:, :], rw[:, 129:137], start=True, stop=True).then_inc(psum, 1)
            pe.wait_ge(spread_ready, 1)
            pe.matmul(m.bank[2][0:P, 0:G * SETS], rw[0:B, 137:137 + P], spread[:, :, :].rearrange("p g x -> p (g x)"),
                      start=True, stop=True).then_inc(psum, 1)

        @block.scalar
        def _(act):
            act.wait_ge(psum, 1)
            act.activation(hid[:, :], m.bank[0][:, 0:B], ACT.Relu, scale=1.0 / S, bias=rw[:, 128:129]).then_inc(hid_ready, 1)
            act.wait_ge(shifted, 1)
            act.activation(pr[:, 0, :], lg[:, 0, :], ACT.Exp).then_inc(exped, 1)

        @block.vector
        def _(dve):
            then = chained(dve, own)
            dve.wait_ge(w_loaded, 16)
            dve.wait_ge(psum, 2)
            then(dve.tensor_tensor(lg[:, 0, :], m.bank[1][0:B, 0:SETS], m.small("r_b2", SETS)[0:B, :], ALU.add))
            then(dve.tensor_reduce(top[:, :], lg[:, :, :], AX, ALU.max))
            dve.tensor_tensor(lg[:, :, :], lg[:, :, :], wide(top), ALU.subtract).then_inc(shifted, 1)
            dve.wait_ge(exped, 1)
            then(dve.tensor_reduce(tot[:, :], pr[:, :, :], AX, ALU.add))
            then(dve.reciprocal(tot[:, :], tot[:, :]))
            then(dve.tensor_tensor(pr[:, :, :], pr[:, :, :], wide(tot), ALU.mult))
            first_best(dve, m, then, one[:, :, :], pr[:, :, :], tmp[:, :, :], top[:, :], [B, 1, SETS])
            dve.tensor_tensor(spread[:, :, :], rw[0:B, 137 + P:137 + P + G].unsqueeze(2).broadcast_to([B, G, SETS]),
                              one[:, :, :].broadcast_to([B, G, SETS]), ALU.mult).then_inc(spread_ready, 1)
            dve.wait_ge(psum, 3)
            then(dve.tensor_copy(m.MSK[:, :], m.bank[2][0:P, 0:G * SETS]))


COLS = ["tok_b", "bn_gamma", "bn_beta"]
ROWS = ["a0_b_proj", "a0_gamma", "a0_beta", "small", "n1_g", "n1_b", "n3_g", "n3_b", "ffn_b2"]
SMALL = {"rb0": 0, "br": 8, "none": 16, "dt_bias": 24, "A_log": 32, "rank": 40, "r_b2": 48}


def build(nc, io, out):
    with ExitStack() as ctx:
        m = Shared()
        m.bank = [ctx.enter_context(nc.psum_tensor(f"bank{b}", [128, 512], F32)) for b in range(4)]
        m.quad_bank = ctx.enter_context(nc.psum_tensor("quad_bank", [128, 4, 512], F32))
        m.H = ctx.enter_context(nc.sbuf_tensor("H", [P, G * D], F32))
        m.const = ctx.enter_context(nc.sbuf_tensor("const", list(io["const"].shape), F32))
        m.cols = ctx.enter_context(nc.sbuf_tensor("cols", list(io["cols"].shape), F32))
        m.rows = ctx.enter_context(nc.sbuf_tensor("rows", list(io["rows"].shape), F32))
        m.bconst = ctx.enter_context(nc.sbuf_tensor("bconst", list(io["bconst"].shape), BF16))
        m.XN = ctx.enter_context(nc.sbuf_tensor("XN", [P, G * D], F32))
        m.row = lambda n: m.rows[:, ROWS.index(n) * D:(ROWS.index(n) + 1) * D]
        m.small = lambda n, w=8: m.row("small")[:, SMALL[n]:SMALL[n] + w]
        m.rank = m.small("rank")
        m.XT = ctx.enter_context(nc.sbuf_tensor("XT", [128, G * P], F32))
        m.LG = ctx.enter_context(nc.sbuf_tensor("LG", [P, G * 8], F32))
        m.GATE = ctx.enter_context(nc.sbuf_tensor("GATE", [P, G * 8], F32))
        m.ident = m.const[:, 0:128]
        m.mhalf = m.const[:, 128:129]
        m.eps = m.const[:, 129:130]
        m.inv_cw = m.const[:, 130:131]
        m.later = m.const[0:P, 131:131 + P]
        m.one = m.const[:, 131 + 2 * P:132 + 2 * P]
        m.upto = m.const[0:P, 131 + P:131 + 2 * P]
        m.T = ctx.enter_context(nc.sbuf_tensor("T", [P, G * D], F32))
        m.DT = ctx.enter_context(nc.sbuf_tensor("DT", [P, G * 8], F32))
        m.DTA = ctx.enter_context(nc.sbuf_tensor("DTA", [P, G * 8], F32))
        m.YT = ctx.enter_context(nc.sbuf_tensor("YT", [128, G * P], F32))
        m.MSK = ctx.enter_context(nc.sbuf_tensor("MSK", [P, G * SETS], F32))
        m.MEANS = ctx.enter_context(nc.sbuf_tensor("MEANS", [128, G * TB], F32))
        m.img = m.bconst[:, 0:P]
        m.not_img = m.bconst[:, P:5 * P]
        m.col = lambda n: m.cols[:, COLS.index(n):COLS.index(n) + 1]
        patch_phase(nc, m, io)
        w = Weights(io["a0_wv"], HD ** -0.5, io["a0_wqk"], io["a0_wo"])
        attention_phase(nc, m, "a0", w, ending="post_norm")
        prepare_phase(nc, m, "p0", io["f0_router"], m.small("rb0"))
        tree_gates(nc, m, "t0")
        experts_phase(nc, m, "f0", io["f0_w1"], io["f0_w2"], io["f0_b1"], ACT.Gelu, 8, 4, io["f0_b2"], m.H)
        prepare_phase(nc, m, "p1", io["ss_router"], m.small("dt_bias"))
        time_steps(nc, m)
        state_space_phase(nc, m, io)
        experts_phase(nc, m, "fs", io["fs_w1"], io["fs_w2"], io["fs_b1"], ACT.Gelu, 1, 4, None, m.T)
        close_phase(nc, m)
        prepare_phase(nc, m, "p2", io["f1_router"], m.small("br"))
        best_gates(nc, m, "t1", 1)
        experts_phase(nc, m, "f1", io["f1_w1"], io["f1_w2"], io["f1_b1"], ACT.Gelu, 8, 4, io["f1_b2"], m.H)
        w = Weights(io["a1_wv"], 64 ** -0.5, io["a1_wqk"], io["a1_wo"])
        attention_phase(nc, m, "a1", w, hd=64)
        prepare_phase(nc, m, "p3", io["f2_router"], m.small("none"))
        best_gates(nc, m, "t2", 2)
        experts_phase(nc, m, "f2", io["f2_w1"], io["f2_w2"], io["f2_b1"], ACT.Gelu_apprx_tanh, 8, 2, io["f2_b2"], m.H)
        w = Weights(io["a2_wv"], 64 ** -0.5, own=io["a2_own"], factors=io["a2_factors"])
        attention_phase(nc, m, "a2", w, ending="channels")
        batch_norm_phase(nc, m)
        prepare_phase(nc, m, "p4", means=True)
        routes_phase(nc, m, io)
        w = Weights(io["a3_wv"], HD ** -0.5, io["a3_wqk"], io["a3_wo"])
        attention_phase(nc, m, "a3", w, nx=SETS, masks=True)
        with ExitStack() as ctx2:
            stored = ctx2.enter_context(nc.semaphore("stored"))
            block = ctx2.enter_context(nc.Block())

            @block.sync
            def _(sp):
                h = m.H[:, :].rearrange("p (g d) -> p g d", d=D)
                full = BATCH // TB
                dst = out[0:full * TB].rearrange("(g b) s d -> (b s) g d", b=TB)
                sp.dma_start(dst, h[:, 0:full, :]).then_inc(stored, 16)
                sp.dma_start(out[full * TB:BATCH].rearrange("b s d -> (b s) d"),
                             h[0:(BATCH - full * TB) * S, full, :]).then_inc(stored, 16)
                sp.wait_ge(stored, 32)


def qk_tiles(wq, wk):
    z = np.zeros((128, 2, 2, 4, SLOT), wq.dtype)
    for i, w in enumerate((wq, wk)):
        z[:, i, :, :, 0:HD] = w.reshape(128, 2, 4, HD)
    return z.reshape(128, 512)


def head_rows(w):
    z = np.zeros((2, 4, SLOT, w.shape[1]), w.dtype)
    z[:, :, 0:HD] = w.reshape(2, 4, HD, w.shape[1])
    return z.reshape(2, 128, w.shape[1]).transpose(1, 0, 2)


def laid_out(a):
    f = np.float32
    x = a["x"]
    pad = np.zeros((G * TB, 3, 6, 16, 6, 16), f)
    pad[:BATCH] = x.reshape(BATCH, 3, 6, 16, 6, 16)
    pats = pad.transpose(1, 3, 5, 0, 2, 4).reshape(KC, 128, G * P).transpose(1, 0, 2)
    r = {}
    r["patches"] = pats
    r["tokw"] = a["L0_tok_w"].T.reshape(KC, 128, D).transpose(1, 0, 2).reshape(128, KC * D)
    const = np.zeros((128, 132 + 2 * P), f)
    const[:, 131 + 2 * P] = 1.0
    tok = np.arange(P)
    same = tok[:, None] // S == tok[None, :] // S
    const[:, 130] = 1.0 / CW
    const[0:P, 131:131 + P] = same & (tok[:, None] > tok[None, :])
    const[0:P, 131 + P:131 + 2 * P] = same & (tok[:, None] <= tok[None, :])
    const[:, 0:128] = np.eye(128, dtype=f)
    const[:, 128] = -0.5
    const[:, 129] = EPS
    r["const"] = const
    r["cols"] = np.stack([a["L0_tok_b"], a["L3_attn_gamma"], a["L3_attn_beta"]], 1)
    small = np.zeros(D, f)
    small[SMALL["rank"]:SMALL["rank"] + 8] = np.arange(8, 0, -1)
    for n, x in (("rb0", "L0_ffn_rb"), ("br", "L1_ffn_br"), ("dt_bias", "L1_attn_dt_bias"), ("A_log", "L1_attn_A_log"), ("r_b2", "L3_ffn_r_b2")):
        small[SMALL[n]:SMALL[n] + a[x].size] = a[x]
    rows = [a["L0_attn_b_proj"], a["L0_attn_ln_gamma"], a["L0_attn_ln_beta"], small] + [a["L1_attn_" + n] for n in ("n1_g", "n1_b", "n3_g", "n3_b", "ffn_b2")]
    r["rows"] = np.broadcast_to(np.concatenate(rows), (P, sum(x.size for x in rows)))
    b = np.zeros((128, 5 * P), f)
    for k in range(4):
        for i in range(TB):
            b[SLOT * k + i, i * S:(i + 1) * S] = 1
            for c in range(4):
                b[SLOT * k + i, P * (1 + c):P * (2 + c)] = NEG
                b[SLOT * k + i, P * (1 + c) + i * S:P * (1 + c) + (i + 1) * S] = 0
    r["bconst"] = b
    wqkv = a["L0_attn_w_qkv"].T
    r["a0_wqk"] = qk_tiles(wqkv[:, 0:128], wqkv[:, 128:256]).reshape(128, 1, 512)
    r["a0_wv"] = wqkv[:, 256:384].reshape(128, 1, 128)
    r["a0_wo"] = head_rows(a["L0_attn_w_proj"].T)
    padded = lambda w, n: np.concatenate([w, np.zeros((w.shape[0], n - w.shape[1]), f)], 1)
    r["f0_router"] = padded(a["L0_ffn_rw"].T, 8)
    for n, w1, b1, w2, b2 in (("f0", "L0_ffn_w1", "L0_ffn_b1", "L0_ffn_w2", "L0_ffn_b2"),
                              ("f1", "L1_ffn_W1", "L1_ffn_b1", "L1_ffn_W2", "L1_ffn_b2"),
                              ("f2", "L2_ffn_W1", "L2_ffn_b1", "L2_ffn_W2", "L2_ffn_b2")):
        e, hid = a[b1].shape
        r[n + "_w1"] = a[w1]
        r[n + "_b1"] = a[b1].reshape(e, hid // 128, 128).transpose(0, 2, 1)
        r[n + "_w2"] = a[w2].reshape(e, hid // 128, 128, D).transpose(0, 2, 1, 3).reshape(e, 128, hid // 128 * D)
        r[n + "_b2"] = np.concatenate([np.pad(a[b2], ((0, SLOT - 8), (0, 0)))] * QUAD)
    win = a["L1_attn_W_in"]
    r["ss_router"] = padded(win[:, 768:772], 8)
    r["ss_win"] = win[:, 0:768]
    ch = np.zeros((128, 24), f)
    ch[:, 0:16] = a["L1_attn_conv_w"].reshape(4, 128, TAPS).transpose(1, 0, 2).reshape(128, 16)
    ch[:, 16:20] = a["L1_attn_conv_b"].reshape(4, 128).T
    ch[:, 20:22] = a["L1_attn_gnorm_w"].reshape(2, 128).T
    r["ss_ch"] = ch
    r["ss_drow"] = np.broadcast_to(a["L1_attn_D_skip"], (P, NS))
    r["ss_wout"] = a["L1_attn_W_out"].reshape(2, 128, D).transpose(1, 0, 2)
    r["fs_w1"] = a["L1_attn_ffn_w1"][None]
    r["fs_b1"] = a["L1_attn_ffn_b1"].reshape(1, 4, 128).transpose(0, 2, 1)
    r["fs_w2"] = a["L1_attn_ffn_w2"].reshape(1, 4, 128, D).transpose(0, 2, 1, 3).reshape(1, 128, 4 * D)
    r["f1_router"] = a["L1_ffn_Wr"]
    r["f2_router"] = a["L2_ffn_Wg"]
    wq, wv = (a[n].transpose(1, 0, 2).reshape(128, 512) for n in ("L2_attn_WQ", "L2_attn_WV"))
    r["a1_wqk"] = np.concatenate([wq, wv], 1).reshape(128, 1, 1024)
    r["a1_wv"] = wv.reshape(128, 1, 512)
    r["a1_wo"] = a["L2_attn_WU"].reshape(4, 128, 128).transpose(1, 0, 2)
    eye = np.eye(128, dtype=f)
    r["a2_own"] = qk_tiles(eye, eye)[:, 0:256]
    r["a2_wv"] = eye.reshape(128, 1, 128)
    by_e = lambda w: np.concatenate([w.transpose(1, 0, 2).reshape(64, 128), np.zeros((64, 128), f)])
    same = np.kron(np.eye(NH, dtype=f), np.ones((HD, HD), f))
    wvb = np.zeros((4, 2, 64, NH, SLOT), f)
    for h in range(NH):
        wvb[h // 2, h % 2, :, h, 0:HD] = a["L3_attn_wv"][h]
    r["a2_factors"] = np.concatenate([by_e(a["L3_attn_wk"]), qk_tiles(by_e(a["L3_attn_wq"]), eye)[:, 0:256],
                                      qk_tiles(same, eye)[:, 0:256],
                                      wvb.reshape(4, 128, 256).transpose(1, 0, 2).reshape(128, 1024),
                                      a["L3_attn_wo"].T.reshape(4, 128, 128).transpose(1, 0, 2).reshape(128, 512)], 1)
    rt = np.zeros((128, 128 + 1 + 8 + P + G), f)
    rt[:, 0:32] = a["L3_ffn_r_w1"]
    rt[0:32, 128] = a["L3_ffn_r_b1"]
    rt[0:32, 129:132] = a["L3_ffn_r_w2"]
    image = np.arange(G * TB)
    rt[0:G * TB, 137:137 + P] = image[:, None] % TB == tok[None, :] // S
    rt[0:G * TB, 137 + P:] = image[:, None] // TB == np.arange(G)[None, :]
    r["rt_w"] = rt
    heads = lambda w: w.reshape(128, -1, HD).repeat(NH * HD // w.shape[1], axis=1).reshape(128, 128)
    ws = [[a[f"L3_ffn_{n}{i}"] for n in ("wq", "wk", "wv", "wo")] for i in range(SETS)]
    r["a3_wqk"] = np.stack([qk_tiles(wq, heads(wk)) for wq, wk, _, _ in ws], 1)
    r["a3_wv"] = np.stack([heads(wv) for _, _, wv, _ in ws], 1)
    r["a3_wo"] = np.concatenate([head_rows(wo) for _, _, _, wo in ws], 2)
    return {k: np.ascontiguousarray(v) for k, v in r.items()}


def kernel(**inputs):
    import concourse.bacc as bacc
    from concourse.bass_utils import run_bass_kernel_spmd

    nc = bacc.Bacc("TRN2", target_bir_lowering=False, num_devices=1)
    arrays = laid_out({k: np.asarray(v) for k, v in inputs.items()})
    aps = {k: nc.dram_tensor(f"in_{k}", v.shape, mybir.dt.from_np(v.dtype), kind="ExternalInput").ap()
           for k, v in arrays.items()}
    out = nc.dram_tensor("out", (BATCH, S, D), F32, kind="ExternalOutput").ap()
    build(nc, aps, out)
    r = run_bass_kernel_spmd(nc, [{f"in_{k}": v for k, v in arrays.items()}], core_ids=[0])
    return r.results[0]["out"]
```

```python
from contextlib import ExitStack, contextmanager

import numpy as np

import concourse.bass as bass
from concourse import mybir

F32 = mybir.dt.float32
BF16 = mybir.dt.bfloat16
F32R = mybir.dt.float32r
ALU = mybir.AluOpType
ACT = mybir.ActivationFunctionType
AX = mybir.AxisListType.X

BATCH = 64
S = 36
D = 128
PATCH_K = 3 * 16 * 16
KC = PATCH_K // 128
TB = 3
P = TB * S
G = -(-BATCH // TB)
NH = 8
HD = 16
SLOT = 32
QUAD = 4
CHUNKS = [(c, min(QUAD, G - c)) for c in range(0, G, QUAD)]
NT = BATCH * S // 128
BLOCKS = [(t, min(4, NT - t)) for t in range(0, NT, 4)]
EPS = 1e-5
NEG = -1.0e30


def steps(eng, step, depth):
    first = (depth + 2) // 2 * 2
    for t in range(first):
        step(t, t % 2)
    with eng.Fori(0, (G - first) // 2) as j:
        for u in range(2):
            step(j * 2 + (first + u), u)
    for t in range(G, G + depth - 1):
        step(t, t % 2)


def live(t, k):
    return not isinstance(t, int) or 0 <= t - k < G


def at_least(eng, sem, value):
    if not isinstance(value, int) or value > 0:
        eng.wait_ge(sem, value)


class Shared:
    pass


class Weights:

    def __init__(self, wv, scale, wqk=None, wo=None, own=None, factors=None):
        self.wqk, self.wv, self.wo, self.scale, self.own, self.factors = wqk, wv, wo, scale, own, factors
        self.fold = factors is not None


@contextmanager
def semaphores(nc, prefix, again=None):
    made = []
    with ExitStack() as ctx:
        def sem(name):
            made.append((again or ctx).enter_context(nc.semaphore(f"{prefix}_{name}")))
            return made[-1]
        yield sem
        if again is None:
            with nc.Block() as block:
                @block.gpsimd
                def _(pool):
                    for s in made:
                        pool.sem_clear(s)


def patch_phase(nc, m, io):
    with ExitStack() as ctx:
        sem = ctx.enter_context(semaphores(nc, "tok"))
        loaded = [sem(f"loaded{c}") for c in range(len(CHUNKS))]
        w_loaded = sem("w_loaded")
        rows_loaded = sem("rows_loaded")
        proj_psum = sem("proj_psum")
        biased = sem("biased")
        turned = sem("turned")
        h_ready = sem("h_ready")
        pats = ctx.enter_context(nc.sbuf_tensor("pats", [128, KC, G * P], F32))
        tokw = ctx.enter_context(nc.sbuf_tensor("tokw", [128, KC * D], F32))
        bload = ctx.enter_context(nc.sbuf_tensor("bload", list(io["bconst"].shape), F32))
        hT = ctx.enter_context(nc.sbuf_tensor("tok_hT", [128, 2, QUAD * P], F32))
        block = ctx.enter_context(nc.Block())

        @block.sync
        def _(sp):
            sp.dma_start(m.const[:, :], io["const"]).then_inc(w_loaded, 16)
            sp.dma_start(tokw[:, :], io["tokw"]).then_inc(w_loaded, 16)
            for n, (c, k) in enumerate(CHUNKS[0::2]):
                sp.dma_start(pats[:, :, c * P:(c + k) * P], io["patches"][:, :, c * P:(c + k) * P]).then_inc(loaded[2 * n], 16)

        @block.tensor
        def _(pe):
            pe.wait_ge(w_loaded, 48)

            def project(n):
                c, k = CHUNKS[n]
                pe.wait_ge(loaded[n], 16)
                at_least(pe, biased, n - 1)
                for kc in range(KC):
                    mm = pe.matmul(m.bank[n % 2][:, 0:k * P], tokw[:, kc * D:(kc + 1) * D],
                                   pats[:, kc, c * P:(c + k) * P], start=(kc == 0), stop=(kc == KC - 1))
                mm.then_inc(proj_psum, 1)

            def turn(n):
                c, k = CHUNKS[n]
                pe.wait_ge(biased, n + 1)
                at_least(pe, h_ready, n - 1)
                for g in range(k):
                    mm = pe.transpose(m.bank[2 + n % 2][0:P, g * D:(g + 1) * D],
                                      hT[:, n % 2, g * P:(g + 1) * P], m.ident[:, :])
                mm.then_inc(turned, 1)

            project(0)
            for n in range(1, len(CHUNKS)):
                project(n)
                turn(n - 1)
            turn(len(CHUNKS) - 1)

        @block.scalar
        def _(act):
            act.dma_start(m.cols[:, :], io["cols"]).then_inc(w_loaded, 16)
            for n, (c, k) in enumerate(CHUNKS[1::2]):
                act.dma_start(pats[:, :, c * P:(c + k) * P], io["patches"][:, :, c * P:(c + k) * P]).then_inc(loaded[2 * n + 1], 16)
            act.dma_start(bload[:, :], io["bconst"]).then_inc(rows_loaded, 16)
            act.dma_start(m.rows[:, :], io["rows"]).then_inc(rows_loaded, 16)
            act.wait_ge(w_loaded, 48)
            for n, (c, k) in enumerate(CHUNKS):
                act.wait_ge(proj_psum, n + 1)
                at_least(act, turned, n - 1)
                act.activation(hT[:, n % 2, 0:k * P], m.bank[n % 2][:, 0:k * P], ACT.Identity,
                               bias=m.col("tok_b")).then_inc(biased, 1)
            act.wait_ge(rows_loaded, 32)
            act.activation(m.bconst[:, :], bload[:, :], ACT.Copy)

        @block.vector
        def _(dve):
            for n, (c, k) in enumerate(CHUNKS):
                dve.wait_ge(turned, n + 1)
                dve.tensor_copy(m.H[:, c * D:(c + k) * D], m.bank[2 + n % 2][0:P, 0:k * D]).then_inc(h_ready, 1)
            dve.wait_ge(h_ready, len(CHUNKS))


def attention_phase(nc, m, name, w, hd=HD, nx=1, ending="add", masks=False):
    row = SLOT if hd == HD else hd
    heads_tile = 128 // row
    spare = row >= hd + TB
    used = hd + TB if spare else hd
    tiles = NH // heads_tile
    rounds = 2 * tiles // 4
    head_at = [n % tiles * heads_tile + n // tiles for n in range(NH)]
    post_norm = ending == "post_norm"
    depth = 7 if post_norm else 6
    with ExitStack() as ctx:
        sem = ctx.enter_context(semaphores(nc, name))
        sb = lambda s, shape, dt=F32: ctx.enter_context(nc.sbuf_tensor(f"{name}_{s}", shape, dt))
        w_loaded = sem("w_loaded")
        stat_chain = sem("stat_chain")
        var_eps = sem("var_eps")
        rstd_ready = sem("rstd_ready")
        xbase = sem("xbase")
        xn_ready = sem("xn_ready")
        xt_psum = sem("xt_psum")
        xt_ready = sem("xt_ready")
        qk_psum = sem("qk_psum")
        qk_ready = sem("qk_ready")
        v_psum = sem("v_psum")
        v_ready = sem("v_ready")
        s_psum = sem("s_psum")
        max_ready = sem("max_ready")
        shift_ready = sem("shift_ready")
        exps = sem("exps")
        pt_psum = sem("pt_psum")
        pt_ready = sem("pt_ready")
        rec_ready = sem("rec_ready")
        recs_ready = sem("recs_ready")
        o_psum = sem("o_psum")
        o_done = sem("o_done")
        y_psum = sem("y_psum")
        y_sum = sem("y_sum")
        y_done = sem("y_done")
        o_read = sem("o_read")
        pads_set = sem("pads_set")
        wqk = sb("wqk", [128, nx, 2 * tiles * 128])
        wv = sb("wv", [128, nx, NH * hd]) if w.wv is not None else None
        wo = sb("wo", [128, tiles, nx * D])
        bn6 = sb("bn6", [P, 2, 6])
        mv = sb("mv", [P, 2, 2])
        ve = sb("ve", [P, 2, 1])
        rstd = sb("rstd", [P, 2, 1])
        xn = sb("xn", [P, 2, nx, D])
        xT = sb("xT", [128, 2, nx, P])
        qk = sb("qk", [128, 2, 2 * tiles, P])
        v = sb("v", [P, 2, NH, row])
        mx = sb("mx", [P, NH])
        shift = sb("shift", [P, 2, NH])
        total = sb("total", [P, 2, NH])
        E = sb("E", [P, 2, NH, P])
        pT = sb("pT", [P, 2, NH, P])
        rec = sb("rec", [P, NH])
        recs = sb("recs", [P, 2, NH, row])
        recT = sb("recT", [128, tiles * P])
        oT = sb("oT", [128, tiles * P])
        if w.fold:
            f_in = sb("f_in", [128, 128 + 256 + 256 + 4 * 256 + 4 * 128])
            f_wk, f_wq, f_same = f_in[:, 0:128], f_in[:, 128:384], f_in[:, 384:640]
            f_wv = lambda c, tile: f_in[:, 640 + c * 256 + tile * 128:640 + c * 256 + (tile + 1) * 128]
            f_wo = lambda c: f_in[:, 1664 + c * 128:1664 + (c + 1) * 128]
            fold_psum = sem("fold_psum")
            folded = sem("folded")
        if masks:
            xb = sb("xb", [P, D])
        if post_norm:
            xres_ready = sem("xres_ready")
            post_stats = sem("post_stats")
            post_eps = sem("post_eps")
            post_rstd = sem("post_rstd")
            post_normed = sem("post_normed")
            post_scaled = sem("post_scaled")
            h_done = sem("h_done")
            yt = sb("yt", [P, 2, D])
            bnb = sb("bnb", [P, 2, 6])
            mvb = sb("mvb", [P, 2, 2])
            veb = sb("veb", [P, 2, 1])
            rstdb = sb("rstdb", [P, 2, 1])
        xbank, obank, ptbank, sbank = m.bank[0], m.bank[2], m.bank[3], m.quad_bank
        qkbank = [m.bank[1], m.quad_bank[:, 2, :]][0:rounds]
        o_at = obank[:, 0:tiles * P]
        z_at = obank[:, tiles * P:2 * tiles * P] if 2 * tiles * P <= 512 else m.quad_bank[:, 3, 0:tiles * P]
        scores = sbank[0:P, 0:heads_tile, 0:tiles * P].rearrange("p b (s j) -> p b s j", s=tiles)
        block = ctx.enter_context(nc.Block())

        @block.sync
        def _(sp):
            if not w.fold:
                sp.dma_start(wqk[:, :, :], w.wqk).then_inc(w_loaded, 16)
                sp.dma_start(wo[:, :, :], w.wo).then_inc(w_loaded, 16)
            else:
                sp.dma_start(wqk[:, 0, 0:256], w.own).then_inc(w_loaded, 16)
                sp.dma_start(f_in[:, :], w.factors).then_inc(w_loaded, 16)
            if w.wv is not None:
                sp.dma_start(wv[:, :, :], w.wv).then_inc(w_loaded, 16)

        @block.gpsimd
        def _(pool):
            def step(t, par):
                q = 1 - par
                if live(t, 0):
                    g = t
                    pool.wait_ge(stat_chain, g * 2 + 2)
                    at_least(pool, rstd_ready, g)
                    pool.tensor_tensor(ve[:, par, :], mv[:, par, 1:2], m.eps[0:P, :], ALU.add).then_inc(var_eps, 1)
                    pool.wait_ge(var_eps, g + 1)
                    at_least(pool, xn_ready, (g - 1) * nx)
                    pool.tensor_tensor(rstd[:, par, :], ve[:, par, :], m.mhalf[0:P, :], ALU.pow).then_inc(rstd_ready, 1)
                if post_norm and live(t, 1):
                    g = t - 1
                    pool.wait_ge(xn_ready, g + 1)
                    pool.tensor_tensor(m.XN[:, bass.ts(g, D)], xn[:, q, 0, :], m.row("a0_b_proj"), ALU.add).then_inc(xres_ready, 1)
                if post_norm and live(t, 6):
                    g = t - 6
                    pool.wait_ge(post_normed, g + 1)
                    pool.tensor_tensor(yt[:, par, :], yt[:, par, :], m.row("a0_gamma"), ALU.mult).then_inc(post_scaled, 1)
                    pool.wait_ge(post_scaled, g * 2 + 1)
                    pool.tensor_tensor(yt[:, par, :], yt[:, par, :], m.row("a0_beta"), ALU.add).then_inc(post_scaled, 1)
                    pool.wait_ge(post_scaled, g * 2 + 2)
                    h = m.H[:, bass.ts(g, D)]
                    pool.tensor_tensor(h, h, yt[:, par, :], ALU.add).then_inc(h_done, 1)
                if post_norm and live(t, 5):
                    g = t - 5
                    pool.wait_ge(post_stats, g * 2 + 2)
                    pool.tensor_tensor(veb[:, q, :], mvb[:, q, 1:2], m.eps[0:P, :], ALU.add).then_inc(post_eps, 1)
                    pool.wait_ge(post_eps, g + 1)
                    pool.tensor_tensor(rstdb[:, q, :], veb[:, q, :], m.mhalf[0:P, :], ALU.pow).then_inc(post_rstd, 1)
            steps(pool, step, depth)

        @block.tensor
        def _(pe):
            pe.wait_ge(w_loaded, 48 if w.wv is not None else 32)
            if w.fold:
                pe.matmul(m.bank[0][:, 0:256], f_wk, f_wq, start=True, stop=True).then_inc(fold_psum, 1)
                for tile in range(tiles):
                    for c in range(4):
                        mm = pe.matmul(m.bank[1][:, tile * 128:(tile + 1) * 128], f_wv(c, tile), f_wo(c), start=(c == 0), stop=(c == 3))
                mm.then_inc(fold_psum, 1)
                pe.wait_ge(folded, 2)
            pe.wait_ge(pads_set, 1)

            def probabilities(g, q, half):
                pe.wait_ge(exps, g * 2 + (half + 1))
                at_least(pe, pt_ready, g * 2 + half)
                for n in range(4 * half, 4 * half + 4):
                    mm = pe.transpose(ptbank[0:P, n % 4 * P:(n % 4 + 1) * P], E[:, q, n, :], m.ident[0:P, 0:P])
                mm.then_inc(pt_psum, 1)

            def queries_keys(g, par, r):
                at_least(pe, qk_ready, g * rounds + (r - (rounds - 1)))
                if spare:
                    pe.matmul(qkbank[r][:, 0:4 * P], m.image_rows[0:TB, :], m.image_marks[0:TB, :], start=True, stop=False,
                              skip_group_check=True)
                for n in range(4):
                    for x in range(nx):
                        c = (4 * r + n) * 128
                        mm = pe.matmul(qkbank[r][:, n * P:(n + 1) * P], wqk[:, x, c:c + 128], xT[:, par, x, :],
                                       start=(x == 0 and not spare), stop=(x == nx - 1), skip_group_check=True)
                mm.then_inc(qk_psum, 1)

            def scores_half(g, q, half):
                pe.wait_ge(qk_ready, g * rounds + rounds)
                at_least(pe, exps, g * 2 + (half - 1))
                banks = range(heads_tile // 2 * half, heads_tile // 2 * (half + 1))
                for b in banks if not spare else ():
                    pe.matmul(sbank[0:P, b, 0:tiles * P], m.img[row * b:row * b + TB, :],
                              m.not_img[row * b:row * b + TB, 0:tiles * P], start=True, stop=False, skip_group_check=True)
                for tile in range(tiles):
                    for b in banks:
                        mm = pe.matmul(sbank[0:P, b, tile * P:(tile + 1) * P], qk[row * b:row * b + used, q, tile, :],
                                       qk[row * b:row * b + used, q, tiles + tile, :], start=spare, stop=(spare or tile == tiles - 1),
                                       skip_group_check=True)
                mm.then_inc(s_psum, 1)

            def step(t, par):
                q = 1 - par
                if live(t, 3):
                    scores_half(t - 3, q, 0)
                if live(t, 2):
                    g = t - 2
                    pe.wait_ge(xn_ready, g * nx + nx)
                    at_least(pe, v_ready, g - 1)
                    for x in range(nx):
                        mm = pe.transpose(xbank[:, x * P:(x + 1) * P], xn[:, par, x, :], m.ident[0:P, 0:P])
                    mm.then_inc(xt_psum, 1)
                if live(t, 4):
                    probabilities(t - 4, par, 0)
                if live(t, 3):
                    scores_half(t - 3, q, 1)
                if live(t, 5):
                    g = t - 5
                    pe.wait_ge(o_done, g + 1)
                    if live(t, 2):
                        pe.wait_ge(xt_ready, g + 4)
                    elif live(t, 4):
                        pe.wait_ge(v_ready, g + 2)
                    for tile in range(tiles):
                        o = oT[:, tile * P:(tile + 1) * P]
                        if ending == "channels":
                            mm = pe.matmul(xbank[:, 0:P], wo[:, tile, :], o, start=(tile == 0), stop=(tile == tiles - 1))
                        else:
                            mm = pe.matmul(xbank[0:P, 0:nx * D], o, wo[:, tile, :], start=(tile == 0), stop=(tile == tiles - 1))
                    mm.then_inc(y_psum, 1)
                if live(t, 4):
                    probabilities(t - 4, par, 1)
                if live(t, 2):
                    pe.wait_ge(xt_ready, t - 2 + 1)
                    queries_keys(t - 2, par, 0)
                if live(t, 3):
                    g = t - 3
                    if live(t, 5):
                        pe.wait_ge(y_done, g - 1)
                    elif live(t, 2):
                        pe.wait_ge(xt_ready, g + 2)
                    if w.fold:
                        mm = pe.transpose(xbank[0:P, 0:D], xT[:, q, 0, :], m.ident[:, :])
                    for tile in range(tiles if w.wv is None and not w.fold else 0):
                        mm = pe.transpose(xbank[0:P, tile * 128:(tile + 1) * 128], qk[:, q, tiles + tile, :], m.ident[:, :])
                    for x in range(nx if w.wv is not None else 0):
                        mm = pe.matmul(xbank[0:P, 0:NH * hd], xT[:, q, x, :], wv[:, x, :], start=(x == 0), stop=(x == nx - 1))
                    mm.then_inc(v_psum, 1)
                if live(t, 2) and rounds == 2:
                    queries_keys(t - 2, par, 1)
                if live(t, 4):
                    g = t - 4
                    at_least(pe, o_done, g)
                    pe.wait_ge(recs_ready, g + 1)
                    for tile in range(tiles):
                        pe.transpose(z_at[:, tile * P:(tile + 1) * P],
                                     recs[:, par, tile * heads_tile:(tile + 1) * heads_tile, :].rearrange("p n c -> p (n c)"),
                                     m.ident[0:P, 0:P])
                    pe.wait_ge(pt_ready, g * 2 + 2)
                    pe.wait_ge(v_ready, g + 1)
                    for tile in range(tiles):
                        for r in range(heads_tile):
                            h = tile * heads_tile + r
                            mm = pe.matmul(o_at[row * r:row * (r + 1), tile * P:(tile + 1) * P], v[:, par, h, :],
                                           pT[:, par, head_at.index(h), :], start=True, stop=True)
                    mm.then_inc(o_psum, 1)
            steps(pe, step, depth)

        @block.scalar
        def _(act):
            act.wait_ge(pads_set, 1)

            def turned(g, par, half):
                act.wait_ge(pt_psum, g * 2 + half + 1)
                at_least(act, o_psum, g - 1)
                act.activation(pT[:, par, 4 * half:4 * half + 4, :].rearrange("p n j -> p (n j)"),
                               ptbank[0:P, 0:4 * P], ACT.Copy).then_inc(pt_ready, 1)

            def exponentials(g, q, half):
                act.wait_ge(shift_ready, g * 2 + half + 1)
                at_least(act, pt_psum, (g - 1) * 2)
                at_least(act, rec_ready, g - 1)
                for n in range(4 * half, 4 * half + 4):
                    e = act.activation(E[:, q, n, :], scores[:, n // tiles, n % tiles, :], ACT.Exp, scale=w.scale,
                                       bias=shift[:, q, n:n + 1], accum_out=total[:, q, n:n + 1])
                e.then_inc(exps, 1)

            def queries_keys(g, par, r):
                act.wait_ge(qk_psum, g * rounds + r + 1)
                at_least(act, s_psum, (g - 1) * 2)
                if w.wv is None and not w.fold:
                    at_least(act, v_psum, g - 1)
                act.activation(qk[:, par, 4 * r:4 * r + 4, :].rearrange("p n j -> p (n j)"), qkbank[r][:, 0:4 * P],
                               ACT.Copy).then_inc(qk_ready, 1)

            def step(t, par):
                q = 1 - par
                if live(t, 2):
                    g = t - 2
                    act.wait_ge(xt_psum, g + 1)
                    at_least(act, v_psum, g - 1)
                    act.activation(xT[:, par, :, :].rearrange("p x j -> p (x j)"), xbank[:, 0:nx * P], ACT.Copy).then_inc(xt_ready, 1)
                if live(t, 4):
                    turned(t - 4, par, 0)
                if live(t, 3):
                    exponentials(t - 3, q, 0)
                if live(t, 4):
                    turned(t - 4, par, 1)
                if live(t, 2):
                    queries_keys(t - 2, par, 0)
                if live(t, 3):
                    g = t - 3
                    act.wait_ge(v_psum, g + 1)
                    at_least(act, o_psum, g - 1)
                    act.activation(v[:, q, :, 0:hd], xbank[0:P, 0:NH * hd].rearrange("p (n c) -> p n c", n=NH),
                                   ACT.Copy).then_inc(v_ready, 1)
                if live(t, 2) and rounds == 2:
                    queries_keys(t - 2, par, 1)
                if live(t, 3):
                    exponentials(t - 3, q, 1)
            steps(act, step, depth)

        @block.vector
        def _(dve):
            if w.fold:
                dve.wait_ge(fold_psum, 1)
                dve.wait_ge(w_loaded, 32)
                dve.tensor_tensor(wqk[:, 0, 256:512], m.bank[0][:, 0:256], f_same, ALU.mult).then_inc(folded, 1)
                dve.wait_ge(fold_psum, 2)
                dve.tensor_copy(wo[:, :, :].rearrange("p t d -> p (t d)"), m.bank[1][:, 0:tiles * 128]).then_inc(folded, 1)
            if row > hd:
                dve.memset(v[:, :, :, hd:row].rearrange("p a n c -> p (a n) c"), 0.0)
            dve.drain().then_inc(pads_set, 1)

            def maxima(g, q, half):
                dve.wait_ge(s_psum, g * 2 + (half + 1))
                banks = heads_tile // 2
                top = mx[:, 4 * half:4 * half + 4]
                at_least(dve, shift_ready, g * 2 + (half - 1))
                dve.tensor_reduce(top.rearrange("p (b s) -> p b s", s=tiles),
                                  scores[:, banks * half:banks * (half + 1), :, :], AX, ALU.max).then_inc(max_ready, 1)
                dve.wait_ge(max_ready, g * 2 + half + 1)
                at_least(dve, exps, (g - 1) * 2)
                dve.tensor_scalar(shift[:, q, 4 * half:4 * half + 4], top, -w.scale, None, ALU.mult).then_inc(shift_ready, 1)

            def step(t, par):
                q = 1 - par
                if live(t, 3):
                    maxima(t - 3, q, 0)
                if live(t, 1):
                    g = t - 1
                    dve.wait_ge(rstd_ready, g + 1)
                    at_least(dve, xt_psum, g - 1)
                    if post_norm:
                        at_least(dve, xres_ready, g - 1)
                    x0 = xb[:, :] if masks else xn[:, q, 0, :]
                    if masks:
                        at_least(dve, xn_ready, g * nx)
                    dve.tensor_scalar(x0, m.H[:, bass.ts(g, D)], mv[:, q, 0:1], rstd[:, q, :],
                                      ALU.subtract, ALU.mult).then_inc(xbase if masks else xn_ready, 1)
                    if masks:
                        dve.wait_ge(xbase, g + 1)
                        for x in range(nx):
                            dve.tensor_scalar(xn[:, q, x, :], xb[:, :], m.MSK[:, bass.ds(g * nx + x, 1)], None,
                                              ALU.mult).then_inc(xn_ready, 1)
                if live(t, 3):
                    maxima(t - 3, q, 1)
                if live(t, 5):
                    g = t - 5
                    dve.wait_ge(y_psum, g + 1)
                    h = m.H[:, bass.ts(g, D)]
                    if masks:
                        for x in range(nx):
                            if x:
                                dve.wait_ge(y_sum, g * (nx - 1) + x)
                            dve.scalar_tensor_tensor(out=h, in0=xbank[0:P, x * D:(x + 1) * D], scalar=m.MSK[:, bass.ds(g * nx + x, 1)],
                                                     in1=h, op0=ALU.mult, op1=ALU.add).then_inc(y_sum if x < nx - 1 else y_done, 1)
                    elif ending == "add":
                        dve.tensor_tensor(h, h, xbank[0:P, 0:D], ALU.add).then_inc(y_done, 1)
                    elif ending == "channels":
                        dve.tensor_copy(m.YT[:, bass.ts(g, P)], xbank[:, 0:P]).then_inc(y_done, 1)
                    else:
                        dve.wait_ge(xres_ready, g + 1)
                        at_least(dve, h_done, g - 1)
                        dve.tensor_tensor(yt[:, q, :], m.XN[:, bass.ts(g, D)], xbank[0:P, 0:D], ALU.add).then_inc(y_done, 1)
                if live(t, 4):
                    g = t - 4
                    dve.wait_ge(exps, g * 2 + 2)
                    at_least(dve, recs_ready, g)
                    dve.reciprocal(rec[:, :], total[:, par, :]).then_inc(rec_ready, 1)
                    dve.wait_ge(rec_ready, g + 1)
                    at_least(dve, o_psum, g - 1)
                    dve.tensor_copy(recs[:, par, :, :].rearrange("p (t r) c -> p t r c", t=tiles),
                                    rec[:, :].rearrange("p (r t) -> p t r", t=tiles).unsqueeze(3)
                                    .broadcast_to([P, tiles, heads_tile, row])).then_inc(recs_ready, 1)
                if post_norm and live(t, 6):
                    g = t - 6
                    dve.wait_ge(post_rstd, g + 1)
                    dve.tensor_scalar(yt[:, par, :], yt[:, par, :], mvb[:, par, 0:1], rstdb[:, par, :],
                                      ALU.subtract, ALU.mult).then_inc(post_normed, 1)
                if live(t, 0):
                    g = t
                    at_least(dve, var_eps, g - 1)
                    at_least(dve, xn_ready, (g - 1) * nx)
                    dve.bn_stats(bn6[:, par, :], m.H[:, bass.ts(g, D)]).then_inc(stat_chain, 1)
                    dve.drain()
                    dve.bn_aggr(mv[:, par, :], bn6[:, par, :]).then_inc(stat_chain, 1)
                if post_norm and live(t, 5):
                    g = t - 5
                    dve.wait_ge(y_done, g + 1)
                    dve.bn_stats(bnb[:, q, :], yt[:, q, :]).then_inc(post_stats, 1)
                    dve.drain()
                    dve.bn_aggr(mvb[:, q, :], bnb[:, q, :]).then_inc(post_stats, 1)
                if live(t, 4):
                    g = t - 4
                    dve.wait_ge(o_psum, g + 1)
                    at_least(dve, o_done, g)
                    dve.tensor_copy(recT[:, :], z_at).then_inc(o_read, 1)
                    dve.wait_ge(o_read, g + 1)
                    at_least(dve, y_psum, g)
                    dve.tensor_tensor(oT[:, :], o_at, recT[:, :], ALU.mult).then_inc(o_done, 1)
            steps(dve, step, depth)
            dve.wait_ge(y_done, G)


def group_statistics(dve, src, bn6, mv, done):
    for c, k in CHUNKS:
        for g in range(c, c + k):
            dve.bn_stats(bn6[:, g, :], src[:, g * D:(g + 1) * D])
        dve.drain()
        for g in range(c, c + k):
            ins = dve.bn_aggr(mv[:, g, :], bn6[:, g, :])
        ins.then_inc(done, 1)


def inverse_deviations(pool, m, mv, rstd, stats_ready, var_eps, rstd_ready):
    for n, (c, k) in enumerate(CHUNKS):
        pool.wait_ge(stats_ready, n + 1)
        r = rstd[:, c:c + k]
        pool.tensor_tensor(r, mv[:, c:c + k, 1:2].rearrange("p g c -> p (g c)"), m.eps[0:P, :].broadcast_to([P, k]), ALU.add).then_inc(var_eps, 1)
        pool.wait_ge(var_eps, n + 1)
        pool.tensor_tensor(r, r, m.mhalf[0:P, :].broadcast_to([P, k]), ALU.pow).then_inc(rstd_ready, 1)


def prepare_phase(nc, m, name, router=None, bias=None, means=False, tiled=False):
    width, count = (128, NT) if tiled else (P, G)
    with ExitStack() as ctx:
        sem = ctx.enter_context(semaphores(nc, name, m.kept))
        sb = lambda s, shape, dt=F32: ctx.enter_context(nc.sbuf_tensor(f"{name}_{s}", shape, dt))
        w_loaded = sem("w_loaded")
        stats_ready = sem("stats_ready")
        var_eps = sem("var_eps")
        rstd_ready = sem("rstd_ready")
        xn_ready = sem("xn_ready")
        xt_psum = sem("xt_psum")
        xt_ready = sem("xt_ready")
        lg_psum = sem("lg_psum")
        done = sem("done")
        bn6 = sb("bn6", [P, G, 6])
        mv = sb("mv", [P, G, 2])
        rstd = sb("rstd", [P, G])
        wr = sb("wr", [128, 8]) if router is not None else None
        block = ctx.enter_context(nc.Block())

        @block.sync
        def _(sp):
            if router is not None:
                sp.dma_start(wr[:, :], router).then_inc(w_loaded, 16)

        @block.gpsimd
        def _(pool):
            inverse_deviations(pool, m, mv, rstd, stats_ready, var_eps, rstd_ready)

        @block.tensor
        def _(pe):
            if router is not None:
                pe.wait_ge(w_loaded, 16)

            def route(n):
                c, k = CHUNKS[n]
                pe.wait_ge(xt_ready, n + 1)
                for t in range(c * P // width, min((c + k) * P // width, count)):
                    mm = pe.matmul(m.bank[2][0:width, t * 8:(t + 1) * 8], m.XT[:, t * width:(t + 1) * width], wr[:, :], start=True, stop=True)
                return mm
            for n, (c, k) in enumerate(CHUNKS):
                pe.wait_ge(xn_ready, n + 1)
                at_least(pe, xt_ready, n - 1)
                for g in range(k):
                    mm = pe.transpose(m.bank[n % 2][:, g * P:(g + 1) * P], m.XN[:, (c + g) * D:(c + g + 1) * D], m.ident[0:P, 0:P])
                mm.then_inc(xt_psum, 1)
                if router is not None and n:
                    route(n - 1)
            if router is not None:
                route(len(CHUNKS) - 1).then_inc(lg_psum, 1)

        @block.scalar
        def _(act):
            for n, (c, k) in enumerate(CHUNKS):
                act.wait_ge(xt_psum, n + 1)
                act.activation(m.XT[:, c * P:(c + k) * P], m.bank[n % 2][:, 0:k * P], ACT.Copy).then_inc(xt_ready, 1)

        @block.vector
        def _(dve):
            group_statistics(dve, m.H, bn6, mv, stats_ready)
            dve.wait_ge(stats_ready, len(CHUNKS))
            for n, (c, k) in enumerate(CHUNKS):
                dve.wait_ge(rstd_ready, n + 1)
                for g in range(c, c + k):
                    ins = dve.tensor_scalar(m.XN[:, g * D:(g + 1) * D], m.H[:, g * D:(g + 1) * D], mv[:, g, 0:1],
                                            rstd[:, g:g + 1], ALU.subtract, ALU.mult)
                ins.then_inc(xn_ready, 1)
            if means:
                for n, (c, k) in enumerate(CHUNKS):
                    dve.wait_ge(xt_ready, n + 1)
                    dve.tensor_reduce(m.MEANS[:, c * TB:(c + k) * TB], m.XT[:, c * P:(c + k) * P].rearrange("p (b s) -> p b s", s=S),
                                      AX, ALU.add).then_inc(done, 1)
                dve.wait_ge(done, len(CHUNKS))
            if router is not None:
                dve.wait_ge(lg_psum, 1)
                dve.tensor_tensor(m.LG[0:width, 0:count * 8].rearrange("p (g e) -> p g e", e=8),
                                  m.bank[2][0:width, 0:count * 8].rearrange("p (g e) -> p g e", e=8),
                                  bias.unsqueeze(1).broadcast_to([width, count, 8]), ALU.add).then_inc(done, 1)
                dve.wait_ge(done, 1)


def chained(eng, sem):
    count = [0]

    def then(instruction):
        count[0] += 1
        instruction.then_inc(sem, 1)
        eng.wait_ge(sem, count[0])
    return then


def first_best(dve, m, then, dst, src, tmp, top, shape):
    w = shape[-1]
    then(dve.tensor_reduce(top, src, AX, ALU.max))
    then(dve.tensor_tensor(tmp, src, top.unsqueeze(2).broadcast_to(shape), ALU.is_ge))
    then(dve.tensor_tensor(tmp, tmp, m.rank[0:shape[0], 0:w].unsqueeze(1).broadcast_to(shape), ALU.mult))
    then(dve.tensor_reduce(top, tmp, AX, ALU.max))
    then(dve.tensor_tensor(dst, tmp, top.unsqueeze(2).broadcast_to(shape), ALU.is_equal))


def tree_gates(m, sem, sb):
    own, sig = sem("gate_chain"), sem("gate_sigmoid")
    left, right, lv1 = sb("left", [128, NT, 8]), sb("right", [128, NT, 8]), sb("lv1", [128, NT, 4])

    def first(dve):
        pass

    def middle(act):
        act.activation(right[:, :, :].rearrange("p g e -> p (g e)"), m.LG[:, 0:NT * 8], ACT.Sigmoid).then_inc(sig, 1)

    def last(dve):
        then = chained(dve, own)
        dve.wait_ge(sig, 1)
        then(dve.tensor_scalar(left[:, :, :], right[:, :, :], -1.0, 1.0, ALU.mult, ALU.add))
        gate = m.GATE[:, :].rearrange("p (g e) -> p g e", e=8)
        for i in range(2):
            up = (left, right)[i][:, :, 0:1]
            for side in range(2):
                then(dve.tensor_tensor(lv1[:, :, 2 * i + side:2 * i + side + 1], up, (left, right)[side][:, :, 1 + i:2 + i], ALU.mult))
        for side in range(2):
            then(dve.tensor_tensor(gate[:, :, side:8:2], lv1[:, :, :], (left, right)[side][:, :, 3:7], ALU.mult))
    return first, middle, last


def best_gates(m, sem, sb, best):
    own, own2, exped, shifted = sem("gate_start"), sem("gate_chain"), sem("gate_exped"), sem("gate_shifted")
    top, tot = sb("top", [128, NT]), sb("tot", [128, NT])
    pr, one, two, tmp = (sb(s, [128, NT, 8]) for s in ("pr", "one", "two", "tmp"))
    shape = [128, NT, 8]
    gate = m.GATE[:, :].rearrange("p (g e) -> p g e", e=8)
    wide = lambda x: x[:, :].unsqueeze(2).broadcast_to(shape)

    def first(dve):
        then = chained(dve, own)
        then(dve.tensor_reduce(top[:, :], m.TLG, AX, ALU.max))
        dve.tensor_tensor(pr[:, :, :], m.TLG, wide(top), ALU.subtract).then_inc(shifted, 1)

    def middle(act):
        act.wait_ge(shifted, 1)
        act.activation(pr[:, :, :].rearrange("p g e -> p (g e)"), pr[:, :, :].rearrange("p g e -> p (g e)"), ACT.Exp).then_inc(exped, 1)

    def last(dve):
        then = chained(dve, own2)
        dve.wait_ge(exped, 1)
        then(dve.tensor_reduce(tot[:, :], pr[:, :, :], AX, ALU.add))
        then(dve.reciprocal(tot[:, :], tot[:, :]))
        then(dve.tensor_tensor(pr[:, :, :], pr[:, :, :], wide(tot), ALU.mult))
        first_best(dve, m, then, one[:, :, :], pr[:, :, :], tmp[:, :, :], top[:, :], shape)
        if best == 1:
            then(dve.tensor_tensor(pr[:, :, :], pr[:, :, :], one[:, :, :], ALU.mult))
            then(dve.tensor_reduce(top[:, :], pr[:, :, :], AX, ALU.max))
            then(dve.reciprocal(tot[:, :], top[:, :]))
            then(dve.tensor_tensor(top[:, :], top[:, :], tot[:, :], ALU.mult))
            then(dve.tensor_tensor(gate, one[:, :, :], wide(top), ALU.mult))
        else:
            then(dve.scalar_tensor_tensor(out=two[:, :, :], in0=one[:, :, :], scalar=-2.0, in1=pr[:, :, :], op0=ALU.mult, op1=ALU.add))
            first_best(dve, m, then, two[:, :, :], two[:, :, :], tmp[:, :, :], top[:, :], shape)
            then(dve.tensor_tensor(one[:, :, :], one[:, :, :], two[:, :, :], ALU.add))
            then(dve.tensor_tensor(gate, pr[:, :, :], one[:, :, :], ALU.mult))
    return first, middle, last


PARTS = [(0, 0), (0, 1), (1, 0)]


def experts_phase(nc, m, name, w1, w2, b1, func, experts, chunks, b2=None, dst=None, gates=None):
    W, count, blocks = (P, G, CHUNKS) if b2 is None else (128, NT, BLOCKS)
    nb = len(blocks)
    before = 0 if b2 is None else 1
    every = before + experts * nb
    with ExitStack() as ctx:
        sem = ctx.enter_context(semaphores(nc, name))
        sb = lambda s, shape, dt=F32: ctx.enter_context(nc.sbuf_tensor(f"{name}_{s}", shape, dt))
        w1_loaded = [sem("w1_loaded0"), sem("w1_loaded1")]
        loaded = [sem("loaded0"), sem("loaded1")]
        b_loaded = sem("b_loaded")
        hid_psum = sem("hid_psum")
        hid_ready = sem("hid_ready")
        w_high = sem("w_high")
        w_split = sem("w_split")
        x_split = sem("x_split")
        y_psum = sem("y_psum")
        y_used = sem("y_used")
        w1s = sb("w1s", [128, 2, chunks * 128])
        w2s = sb("w2s", [128, 2, chunks * 128])
        b1s = sb("b1s", [128, 2, chunks])
        w1p = sb("w1p", [128, 2, 2, chunks * 128], F32R)
        xp = sb("xp", [128, 2, count * W], F32R)
        hid = sb("hid", [128, 2, chunks, QUAD * W])
        if b2 is not None:
            b2s = sb("b2s", [128, QUAD, D])
            gs = sb("gs", [128, nb * QUAD, SLOT])
            gT = sb("gT", [128, nb * 128])
            dst = sb("y", [128, NT * D])
            yt_psum = sem("yt_psum")
            yt_ready = sem("yt_ready")
            back_psum = sem("back_psum")
            h_done = sem("h_done")
            gs_ready = sem("gs_ready")
            gt_psum = sem("gt_psum")
            gt_ready = sem("gt_ready")
            gates_first, gates_middle, gates_last = gates(m, sem, sb)
        block = ctx.enter_context(nc.Block())

        @block.sync
        def _(sp):
            def load(e, u):
                sp.dma_start(w1s[:, u, :], w1[bass.ds(e, 1), :, :].rearrange("e p n -> (e p) n")).then_inc(w1_loaded[u], 16)
                sp.dma_start(b1s[:, u, :], b1[bass.ds(e, 1), :, :].rearrange("e p n -> (e p) n")).then_inc(loaded[u], 16)
                sp.dma_start(w2s[:, u, :], w2[bass.ds(e, 1), :, :].rearrange("e p n -> (e p) n")).then_inc(loaded[u], 16)
            for e in range(min(2, experts)):
                load(e, e)
            if b2 is not None:
                sp.dma_start(b2s[:, :, :], b2).then_inc(b_loaded, 16)
            if experts > 2:
                with sp.Fori(1, experts // 2) as j:
                    for u in range(2):
                        sp.wait_ge(y_psum, (j * 2 + (u - 1)) * nb)
                        load(j * 2 + u, u)

        @block.gpsimd
        def _(pool):
            def split(e, j, u):
                pool.wait_ge(w1_loaded[u], (j + 1) * 16)
                if not isinstance(e, int) or e > 1:
                    pool.wait_ge(y_psum, (j * 2 + (u - 1)) * nb)
                ones = m.one.broadcast_to([128, chunks * 128])
                pool.tensor_tensor(w1p[:, u, 0, :], w1s[:, u, :], ones, ALU.mult).then_inc(w_high, 1)
                pool.wait_ge(w_high, e + 1)
                pool.tensor_tensor(w1p[:, u, 1, :], w1s[:, u, :], w1p[:, u, 0, :], ALU.subtract).then_inc(w_split, 1)
            for e in range(min(2, experts)):
                split(e, 0, e)
            if experts > 2:
                with pool.Fori(1, experts // 2) as j:
                    for u in range(2):
                        split(j * 2 + u, j, u)

        @block.tensor
        def _(pe):
            def expert(e, j, u):
                def up(n):
                    c0, k = blocks[n]
                    for c in range(chunks):
                        i = n * chunks + c
                        if i >= 4:
                            pe.wait_ge(hid_ready, e * (nb * chunks) + (i - 3))
                        for a, b in PARTS:
                            mm = pe.matmul(m.quad_bank[:, i % 4, 0:k * W], w1p[:, u, a, c * 128:(c + 1) * 128],
                                           xp[:, b, c0 * W:(c0 + k) * W], start=((a, b) == PARTS[0]), stop=((a, b) == PARTS[-1]))
                        mm.then_inc(hid_psum, 1)

                def down(n):
                    c0, k = blocks[n]
                    pe.wait_ge(hid_ready, e * (nb * chunks) + (n + 1) * chunks)
                    if n == 0:
                        at_least(pe, y_used, e * nb + before)
                    elif n > 1:
                        pe.wait_ge(y_used, e * nb + (n - 1 + before))
                    for g in range(k):
                        for c in range(chunks):
                            mm = pe.matmul(m.bank[n % 2][0:W, g * D:(g + 1) * D], hid[:, n % 2, c, g * W:(g + 1) * W],
                                           w2s[:, u, c * 128:(c + 1) * 128], start=(c == 0), stop=(c == chunks - 1))
                    mm.then_inc(y_psum, 1)
                pe.wait_ge(w_split, e + 1)
                up(0)
                pe.wait_ge(loaded[u], (j + 1) * 32)
                for n in range(1, nb):
                    up(n)
                    down(n - 1)
                down(nb - 1)
            pe.wait_ge(x_split, nb)
            if experts == 1:
                expert(0, 0, 0)
            else:
                with pe.Fori(0, experts // 2) as j:
                    for u in range(2):
                        expert(j * 2 + u, j, u)
            if b2 is not None:
                pe.wait_ge(gs_ready, 1)
                for n in range(nb):
                    mm = pe.transpose(m.quad_bank[:, n // 4, n % 4 * 128:(n % 4 + 1) * 128],
                                      gs[:, n * QUAD:(n + 1) * QUAD, :].rearrange("p g e -> p (g e)"), m.ident[:, :])
                mm.then_inc(gt_psum, 1)
                pe.wait_ge(b_loaded, 16)
                pe.wait_ge(gt_ready, 2)
                pe.wait_ge(y_used, every)
                for n, (t0, k) in enumerate(blocks):
                    at_least(pe, yt_ready, n - 1)
                    for t in range(k):
                        out = m.bank[n % 2][:, t * 128:(t + 1) * 128]
                        pe.matmul(out, dst[:, (t0 + t) * D:(t0 + t + 1) * D], m.ident[:, :], start=True, stop=False)
                        mm = pe.matmul(out, b2s[:, t, :], gT[:, n * 128:(n + 1) * 128], start=False, stop=True)
                    mm.then_inc(yt_psum, 1)
                for n, (c, k) in enumerate(CHUNKS):
                    pe.wait_ge(yt_ready, min(nb, -(-(c + k) * P // 512)))
                    at_least(pe, h_done, n - 1)
                    for g in range(k):
                        tokens = min(P, NT * 128 - (c + g) * P)
                        mm = pe.transpose(m.bank[2 + n % 2][0:tokens, g * D:(g + 1) * D], m.YT[:, (c + g) * P:(c + g) * P + tokens], m.ident[:, :])
                    mm.then_inc(back_psum, 1)

        @block.scalar
        def _(act):
            if b2 is not None:
                gates_middle(act)

            def expert(e, j, u):
                act.wait_ge(loaded[u], (j + 1) * 32)
                for n, (c0, k) in enumerate(blocks):
                    for c in range(chunks):
                        act.wait_ge(hid_psum, e * (nb * chunks) + (n * chunks + c + 1))
                        if n > 1 and c == 0:
                            act.wait_ge(y_psum, e * nb + (n - 1))
                        act.activation(hid[:, n % 2, c, 0:k * W], m.quad_bank[:, (n * chunks + c) % 4, 0:k * W], func,
                                       bias=b1s[:, u, c:c + 1]).then_inc(hid_ready, 1)
            if experts == 1:
                expert(0, 0, 0)
            else:
                with act.Fori(0, experts // 2) as j:
                    for u in range(2):
                        expert(j * 2 + u, j, u)
            if b2 is not None:
                act.wait_ge(gt_psum, 1)
                for b in range(2):
                    k = min(4, nb - 4 * b)
                    act.activation(gT[:, 4 * b * 128:(4 * b + k) * 128], m.quad_bank[:, b, 0:k * 128], ACT.Copy).then_inc(gt_ready, 1)
                for n, (t0, k) in enumerate(blocks):
                    act.wait_ge(yt_psum, n + 1)
                    act.activation(m.YT[:, t0 * 128:(t0 + k) * 128], m.bank[n % 2][:, 0:k * 128], ACT.Copy).then_inc(yt_ready, 1)

        @block.vector
        def _(dve):
            if b2 is not None:
                gates_first(dve)
            for c0, k in blocks:
                dve.tensor_copy(xp[:, 0, c0 * W:(c0 + k) * W], m.XT[:, c0 * W:(c0 + k) * W])
            dve.drain()
            for c0, k in blocks:
                cols = slice(c0 * W, (c0 + k) * W)
                dve.tensor_tensor(xp[:, 1, cols], m.XT[:, cols], xp[:, 0, cols], ALU.subtract).then_inc(x_split, 1)
            if b2 is not None:
                dve.memset(dst[:, :], 0.0).then_inc(y_used, 1)
                dve.memset(gs[:, :, :].rearrange("p g e -> p (g e)"), 0.0)
                gates_last(dve)
                dve.drain()
                dve.tensor_copy(gs[:, 0:NT, 0:8], m.GATE[:, :].rearrange("p (g e) -> p g e", e=8)).then_inc(gs_ready, 1)

            def expert(e):
                at_least(dve, y_used, e * nb + before)
                for n, (c0, k) in enumerate(blocks):
                    dve.wait_ge(y_psum, e * nb + (n + 1))
                    y = m.bank[n % 2][0:W, 0:k * D]
                    if b2 is None:
                        h = dst[:, c0 * D:(c0 + k) * D]
                        dve.tensor_tensor(h, h, y, ALU.add).then_inc(y_used, 1)
                        continue
                    for g in range(c0, c0 + k):
                        h = dst[:, g * D:(g + 1) * D]
                        ins = dve.scalar_tensor_tensor(out=h, in0=y[:, (g - c0) * D:(g - c0 + 1) * D],
                                                       scalar=m.GATE[:, bass.ds(e + g * 8, 1)], in1=h,
                                                       op0=ALU.mult, op1=ALU.add)
                    ins.then_inc(y_used, 1)
            if experts == 1:
                expert(0)
            else:
                with dve.Fori(0, experts) as e:
                    expert(e)
            dve.wait_ge(y_used, every)
            if b2 is not None:
                for n, (c, k) in enumerate(CHUNKS):
                    dve.wait_ge(back_psum, n + 1)
                    full = k if (c + k) * P <= NT * 128 else k - 1
                    h = m.H[:, c * D:(c + full) * D]
                    ins = dve.tensor_tensor(h, h, m.bank[2 + n % 2][0:P, 0:full * D], ALU.add)
                    if full < k:
                        last = NT * 128 - (c + full) * P
                        h = m.H[0:last, (c + full) * D:(c + k) * D]
                        ins = dve.tensor_tensor(h, h, m.bank[2 + n % 2][0:last, full * D:k * D], ALU.add)
                    ins.then_inc(h_done, 1)
                dve.wait_ge(h_done, len(CHUNKS))


NS = 4
CW = 2 * D
TAPS = 4
PADDED = S + TAPS - 1


def time_steps(nc, m):
    with ExitStack() as ctx:
        sb = lambda s, shape: ctx.enter_context(nc.sbuf_tensor(f"dt_{s}", shape, F32))
        sem = ctx.enter_context(semaphores(nc, "dt", m.kept))
        own = sem("chain")
        absolute = sem("absolute")
        exped = sem("exped")
        u, r, r2, q = (sb(n, [P, G * 8]) for n in ("u", "r", "r2", "q"))
        a = sb("a", [P, 8])
        block = ctx.enter_context(nc.Block())

        @block.scalar
        def _(act):
            act.activation(a[:, :], m.small("A_log"), ACT.Exp).then_inc(exped, 1)
            act.wait_ge(absolute, 1)
            act.activation(u[:, :], r[:, :], ACT.Exp, scale=-1.0).then_inc(exped, 1)

        @block.vector
        def _(dve):
            then = chained(dve, own)
            dve.scalar_tensor_tensor(out=r[:, :], in0=m.LG[0:P, :], scalar=-1.0, in1=m.LG[0:P, :], op0=ALU.mult, op1=ALU.max).then_inc(absolute, 1)
            dve.wait_ge(exped, 2)
            then(dve.tensor_scalar(q[:, :], u[:, :], 2.0, None, ALU.add))
            then(dve.reciprocal(q[:, :], q[:, :]))
            then(dve.tensor_tensor(r[:, :], u[:, :], q[:, :], ALU.mult))
            then(dve.tensor_tensor(r2[:, :], r[:, :], r[:, :], ALU.mult))
            then(dve.tensor_scalar(q[:, :], r2[:, :], 1.0 / 17, None, ALU.mult))
            for k in (15, 13, 11, 9, 7, 5, 3):
                then(dve.scalar_tensor_tensor(out=q[:, :], in0=q[:, :], scalar=1.0 / k, in1=r2[:, :], op0=ALU.add, op1=ALU.mult))
            then(dve.scalar_tensor_tensor(out=q[:, :], in0=q[:, :], scalar=1.0, in1=r[:, :], op0=ALU.add, op1=ALU.mult))
            then(dve.tensor_scalar(u[:, :], m.LG[0:P, :], 0.0, None, ALU.max))
            then(dve.scalar_tensor_tensor(out=m.DT[:, :], in0=q[:, :], scalar=2.0, in1=u[:, :], op0=ALU.mult, op1=ALU.add))
            then(dve.scalar_tensor_tensor(out=m.DTA[:, :].rearrange("p (g e) -> p g e", e=8), in0=m.DT[:, :].rearrange("p (g e) -> p g e", e=8),
                                          scalar=-1.0, in1=a[:, :].unsqueeze(1).broadcast_to([P, G, 8]), op0=ALU.mult, op1=ALU.mult))


def state_space_phase(nc, m, io):
    with ExitStack() as ctx:
        sem = ctx.enter_context(semaphores(nc, "ss"))
        sb = lambda s, shape, dt=F32: ctx.enter_context(nc.sbuf_tensor(f"ss_{s}", shape, dt))
        w_loaded = sem("w_loaded")
        prepared = sem("prepared")
        padded = sem("padded")
        xbc_psum = sem("xbc_psum")
        cv_ready = sem("cv_ready")
        silu = sem("silu")
        xts_ready = sem("xts_ready")
        xc_psum = sem("xc_psum")
        xc_ready = sem("xc_ready")
        cum_ready = sem("cum_ready")
        seg_psum = sem("seg_psum")
        decay = sem("decay")
        z_psum = sem("z_psum")
        z_tanh = sem("z_tanh")
        z_ready = sem("z_ready")
        masked = sem("masked")
        xdt_ready = sem("xdt_ready")
        mix_ready = sem("mix_ready")
        y_psum = sem("y_psum")
        xd_ready = sem("xd_ready")
        ys_ready = sem("ys_ready")
        yz_ready = sem("yz_ready")
        ssq_ready = sem("ssq_ready")
        rms_steps = sem("rms_steps")
        rms_ready = sem("rms_ready")
        yt_psum = sem("yt_psum")
        yt_ready = sem("yt_ready")
        o_psum = sem("o_psum")
        sum_ready = sem("sum_ready")
        stats = sem("stats")
        eps_added = sem("eps_added")
        rstd_ready = sem("rstd_ready")
        normed = sem("normed")
        scaled = sem("scaled")
        t_psum = sem("t_psum")
        t_ready = sem("t_ready")
        win = sb("win", [128, 6 * 128])
        wout = sb("wout", [128, 2, D])
        ch = sb("ch", [128, 24])
        half = sb("half", [128, 20])
        wtap = sb("wtap", [128, TAPS, 512])
        drow = sb("drow", [P, NS])
        xd = sb("xd", [P, 2, CW])
        ys = sb("ys", [P, CW])
        xp = sb("xp", [128, 2, TB, PADDED])
        cv = sb("cv", [128, 2, 4, P])
        th = sb("th", [128, 2, 4, P])
        sx = sb("sx", [128, 2, 4, P])
        xTs = sb("xTs", [128, 2, P])
        cum = sb("cum", [P, 2, NS, P])
        xc = sb("xc", [P, 2, CW + P])
        cbm = sb("cbm", [P, P])
        L = sb("L", [P, NS, P])
        M = sb("M", [P, 2, NS, P])
        xdt = sb("xdt", [P, 2, CW])
        zs = sb("zs", [P, 2, CW])
        yz = sb("yz", [P, 2, CW])
        sq = sb("sq", [P, CW])
        ssq = sb("ssq", [P, 2, 1])
        rms = sb("rms", [P, 2, 1])
        yT = sb("yT", [128, 2 * P])
        yt = sb("yt", [P, 2, D])
        bn6 = sb("bn6", [P, 2, 6])
        mv = sb("mv", [P, 2, 2])
        ve = sb("ve", [P, 2, 1])
        rstd = sb("rstd", [P, 2, 1])
        tt = sb("tt", [P, 2, D])
        seg_bank, y_bank, o_bank, t_bank = (m.quad_bank[:, b, :] for b in range(4))
        depth = 7
        block = ctx.enter_context(nc.Block())

        @block.sync
        def _(sp):
            for dst, src in ((win, io["ss_win"]), (ch, io["ss_ch"]), (drow, io["ss_drow"])):
                sp.dma_start(dst[:, :], src).then_inc(w_loaded, 16)
            sp.dma_start(wout[:, :, :], io["ss_wout"]).then_inc(w_loaded, 16)
            sp.dma_start(wtap[:, :, :], io["ss_taps"]).then_inc(w_loaded, 16)

        @block.gpsimd
        def _(pool):
            def step(t, par):
                q = 1 - par
                if live(t, 1):
                    g = t - 1
                    at_least(pool, z_psum, g - 1)
                    pool.tensor_copy(xTs[:, q, :], m.XT[:, bass.ts(g, P)]).then_inc(xts_ready, 1)
                if live(t, 5):
                    g = t - 5
                    pool.wait_ge(normed, g + 1)
                    at_least(pool, t_psum, g - 1)
                    pool.tensor_tensor(tt[:, q, :], yt[:, q, :], m.row("n1_g"), ALU.mult).then_inc(scaled, 1)
                    pool.wait_ge(scaled, g * 3 + 1)
                    pool.tensor_tensor(tt[:, q, :], tt[:, q, :], m.row("n1_b"), ALU.add).then_inc(scaled, 1)
                    pool.wait_ge(scaled, g * 3 + 2)
                    pool.tensor_tensor(m.T[:, bass.ts(g, D)], tt[:, q, :], m.row("ffn_b2"), ALU.add).then_inc(scaled, 1)
                if live(t, 2):
                    g = t - 2
                    pool.wait_ge(xc_ready, g + 1)
                    at_least(pool, yz_ready, g - 1)
                    pool.tensor_tensor(xd[:, par, :].rearrange("p (n c) -> p n c", n=NS), xc[:, par, 0:CW].rearrange("p (n c) -> p n c", n=NS),
                                       drow[:, :].unsqueeze(2).broadcast_to([P, NS, 64]), ALU.mult).then_inc(xd_ready, 1)
                if live(t, 3):
                    g = t - 3
                    pool.wait_ge(ssq_ready, g + 1)
                    pool.tensor_tensor(ssq[:, q, :], ssq[:, q, :], m.inv_cw[0:P, :], ALU.mult).then_inc(rms_steps, 1)
                    pool.wait_ge(rms_steps, g * 2 + 1)
                    pool.tensor_tensor(ssq[:, q, :], ssq[:, q, :], m.eps[0:P, :], ALU.add).then_inc(rms_steps, 1)
                    pool.wait_ge(rms_steps, g * 2 + 2)
                    at_least(pool, sum_ready, g - 1)
                    pool.tensor_tensor(rms[:, q, :], ssq[:, q, :], m.mhalf[0:P, :], ALU.pow).then_inc(rms_ready, 1)
                if live(t, 4):
                    g = t - 4
                    pool.wait_ge(stats, g * 2 + 2)
                    pool.tensor_tensor(ve[:, par, :], mv[:, par, 1:2], m.eps[0:P, :], ALU.add).then_inc(eps_added, 1)
                    pool.wait_ge(eps_added, g + 1)
                    at_least(pool, normed, g - 1)
                    pool.tensor_tensor(rstd[:, par, :], ve[:, par, :], m.mhalf[0:P, :], ALU.pow).then_inc(rstd_ready, 1)
            steps(pool, step, depth)
            pool.wait_ge(scaled, 3 * G)

        @block.tensor
        def _(pe):
            pe.wait_ge(w_loaded, 80)
            pe.wait_ge(prepared, 4)

            def step(t, par):
                q = 1 - par
                if live(t, 2):
                    g = t - 2
                    pe.wait_ge(cum_ready, g + 1)
                    at_least(pe, decay, g)
                    pe.matmul(seg_bank[0:P, 0:NS * P], m.later, cum[:, par, :, :].rearrange("p n j -> p (n j)"),
                              start=True, stop=True).then_inc(seg_psum, 1)
                    pe.wait_ge(silu, g + 1)
                    at_least(pe, xc_ready, g)
                    for c in range(2):
                        pe.transpose(m.bank[3][0:P, c * 128:(c + 1) * 128], sx[:, par, c, :], m.ident[:, :])
                    pe.matmul(m.bank[3][0:P, CW:CW + P], sx[:, par, 2, :], sx[:, par, 3, :], start=True, stop=True).then_inc(xc_psum, 1)
                    pe.wait_ge(xts_ready, g + 1)
                    at_least(pe, z_ready, g)
                    pe.matmul(m.bank[1][0:P, 0:CW], xTs[:, par, :], win[:, 0:CW], start=True, stop=True).then_inc(z_psum, 1)
                if live(t, 4):
                    g = t - 4
                    pe.wait_ge(yz_ready, g + 1)
                    at_least(pe, yt_ready, g)
                    for c in range(2):
                        mm = pe.transpose(m.bank[0][:, c * P:(c + 1) * P], yz[:, par, c * 128:(c + 1) * 128], m.ident[0:P, 0:P])
                    mm.then_inc(yt_psum, 1)
                if live(t, 3):
                    g = t - 3
                    pe.wait_ge(mix_ready, g + 1)
                    pe.wait_ge(xdt_ready, g + 1)
                    at_least(pe, ys_ready, g)
                    for n in range(NS):
                        cols = slice(n * 64, (n + 1) * 64)
                        mm = pe.matmul(y_bank[0:P, cols], M[:, q, n, :], xdt[:, q, cols], start=True, stop=True)
                    mm.then_inc(y_psum, 1)
                if live(t, 0):
                    g = t
                    pe.wait_ge(padded, g + 1)
                    at_least(pe, cv_ready, g)
                    for c in range(4):
                        for k in range(TAPS):
                            mm = pe.matmul(m.bank[2][:, c * P:(c + 1) * P], wtap[:, k, c * 128:(c + 1) * 128],
                                           xp[:, par, :, k:k + S], start=(k == 0), stop=(k == TAPS - 1))
                    mm.then_inc(xbc_psum, 1)
                if live(t, 4):
                    g = t - 4
                    pe.wait_ge(yt_ready, g + 1)
                    at_least(pe, sum_ready, g)
                    for c in range(2):
                        mm = pe.matmul(o_bank[0:P, 0:D], yT[:, c * P:(c + 1) * P], wout[:, c, :], start=(c == 0), stop=(c == 1))
                    mm.then_inc(o_psum, 1)
                if live(t, 6):
                    g = t - 6
                    pe.wait_ge(scaled, g * 3 + 2)
                    at_least(pe, t_ready, g)
                    pe.transpose(t_bank[:, 0:P], tt[:, par, :], m.ident[0:P, 0:P]).then_inc(t_psum, 1)
            steps(pe, step, depth)

        @block.scalar
        def _(act):
            act.wait_ge(prepared, 4)

            def step(t, par):
                q = 1 - par
                if live(t, 2):
                    g = t - 2
                    act.wait_ge(seg_psum, g + 1)
                    at_least(act, mix_ready, g)
                    act.activation(L[:, :, :].rearrange("p n j -> p (n j)"), seg_bank[0:P, 0:NS * P], ACT.Exp).then_inc(decay, 1)
                    act.wait_ge(xc_psum, g + 1)
                    at_least(act, xdt_ready, g - 1)
                    at_least(act, mix_ready, g - 1)
                    at_least(act, xd_ready, g - 1)
                    act.activation(xc[:, par, :], m.bank[3][0:P, 0:CW + P], ACT.Copy).then_inc(xc_ready, 1)
                    act.wait_ge(z_psum, g + 1)
                    at_least(act, yz_ready, g - 1)
                    act.activation(zs[:, par, :], m.bank[1][0:P, 0:CW], ACT.Tanh, scale=0.5).then_inc(z_tanh, 1)
                if live(t, 4):
                    g = t - 4
                    act.wait_ge(yt_psum, g + 1)
                    at_least(act, o_psum, g)
                    act.activation(yT[:, :], m.bank[0][:, 0:2 * P], ACT.Copy).then_inc(yt_ready, 1)
                if live(t, 0):
                    g = t
                    act.wait_ge(xbc_psum, g + 1)
                    at_least(act, silu, g - 1)
                    for c in range(4):
                        x = m.bank[2][:, c * P:(c + 1) * P]
                        act.activation(cv[:, par, c, :], x, ACT.Identity, scale=0.5, bias=half[:, 16 + c:17 + c])
                        th_c = act.activation(th[:, par, c, :], x, ACT.Tanh, scale=0.5, bias=half[:, 16 + c:17 + c])
                    th_c.then_inc(cv_ready, 1)
                if live(t, 3):
                    g = t - 3
                    act.wait_ge(yz_ready, g + 1)
                    at_least(act, rms_ready, g - 1)
                    at_least(act, ssq_ready, g)
                    act.activation(sq[:, :], yz[:, q, :], ACT.Square, accum_out=ssq[:, q, :]).then_inc(ssq_ready, 1)
                if live(t, 6):
                    g = t - 6
                    act.wait_ge(t_psum, g + 1)
                    act.activation(m.XT[:, bass.ts(g, P)], t_bank[:, 0:P], ACT.Copy).then_inc(t_ready, 1)
            steps(act, step, depth)

        @block.vector
        def _(dve):
            dve.memset(xp[:, :, :, 0:TAPS - 1].rearrange("p a b k -> p (a b) k"), 0.0).then_inc(prepared, 1)
            dve.wait_ge(w_loaded, 80)
            dve.tensor_tensor(wtap[:, :, :], wtap[:, :, :], win[:, CW:CW + 512].unsqueeze(1).broadcast_to([128, TAPS, 512]),
                              ALU.mult).then_inc(prepared, 1)
            dve.tensor_scalar(half[:, :], ch[:, 0:20], 0.5, None, ALU.mult).then_inc(prepared, 1)
            for c in range(2):
                dve.tensor_scalar(wout[:, c, :], wout[:, c, :], ch[:, 20 + c:21 + c], None, ALU.mult)
            dve.drain().then_inc(prepared, 1)
            dve.wait_ge(prepared, 4)

            def step(t, par):
                q = 1 - par
                if live(t, 0):
                    g = t
                    at_least(dve, xbc_psum, g - 1)
                    dve.tensor_scalar(xp[:, par, :, TAPS - 1:PADDED], m.XT[:, bass.ts(g, P)].rearrange("p (b s) -> p b s", s=S),
                                      1.0, None, ALU.mult).then_inc(padded, 1)
                if live(t, 1):
                    g = t - 1
                    dve.wait_ge(cv_ready, g + 1)
                    at_least(dve, xc_psum, g - 1)
                    dve.scalar_tensor_tensor(out=sx[:, q, :, :].rearrange("p c j -> p (c j)"), in0=th[:, q, :, :].rearrange("p c j -> p (c j)"),
                                             scalar=1.0, in1=cv[:, q, :, :].rearrange("p c j -> p (c j)"), op0=ALU.add, op1=ALU.mult).then_inc(silu, 1)
                    at_least(dve, seg_psum, g - 1)
                    dve.tensor_tensor(cum[:, q, :, :], m.upto.unsqueeze(1).broadcast_to([P, NS, P]),
                                      m.DTA[:, bass.ds(g * 8, NS)].unsqueeze(2).broadcast_to([P, NS, P]), ALU.mult).then_inc(cum_ready, 1)
                if live(t, 2):
                    g = t - 2
                    dve.wait_ge(xc_ready, g + 1)
                    at_least(dve, mix_ready, g)
                    dve.tensor_tensor(cbm[:, :], xc[:, par, CW:CW + P], m.upto, ALU.mult).then_inc(masked, 1)
                    at_least(dve, y_psum, g - 1)
                    dve.tensor_tensor(xdt[:, par, :].rearrange("p (n c) -> p n c", n=NS), xc[:, par, 0:CW].rearrange("p (n c) -> p n c", n=NS),
                                      m.DT[:, bass.ds(g * 8, NS)].unsqueeze(2).broadcast_to([P, NS, 64]), ALU.mult).then_inc(xdt_ready, 1)
                    dve.wait_ge(decay, g + 1)
                    dve.wait_ge(masked, g + 1)
                    dve.tensor_tensor(M[:, par, :, :], L[:, :, :], cbm[:, :].unsqueeze(1).broadcast_to([P, NS, P]), ALU.mult).then_inc(mix_ready, 1)
                    dve.wait_ge(z_tanh, g + 1)
                    dve.scalar_tensor_tensor(out=zs[:, par, :], in0=zs[:, par, :], scalar=1.0, in1=m.bank[1][0:P, 0:CW],
                                             op0=ALU.add, op1=ALU.mult).then_inc(z_ready, 1)
                if live(t, 5):
                    g = t - 5
                    dve.wait_ge(rstd_ready, g + 1)
                    dve.tensor_scalar(yt[:, q, :], yt[:, q, :], mv[:, q, 0:1], rstd[:, q, :], ALU.subtract, ALU.mult).then_inc(normed, 1)
                if live(t, 3):
                    g = t - 3
                    dve.wait_ge(y_psum, g + 1)
                    at_least(dve, yt_psum, g - 1)
                    at_least(dve, ssq_ready, g - 1)
                    dve.wait_ge(z_ready, g + 1)
                    dve.wait_ge(xd_ready, g + 1)
                    dve.tensor_tensor(ys[:, :], xd[:, q, :], y_bank[0:P, 0:CW], ALU.add).then_inc(ys_ready, 1)
                    dve.wait_ge(ys_ready, g + 1)
                    dve.scalar_tensor_tensor(out=yz[:, q, :], in0=ys[:, :], scalar=0.5, in1=zs[:, q, :],
                                             op0=ALU.mult, op1=ALU.mult).then_inc(yz_ready, 1)
                if live(t, 4):
                    g = t - 4
                    dve.wait_ge(o_psum, g + 1)
                    dve.wait_ge(rms_ready, g + 1)
                    at_least(dve, normed, g - 1)
                    at_least(dve, scaled, (g - 2) * 3 + 1) if not isinstance(t, int) or g > 1 else None
                    dve.scalar_tensor_tensor(out=yt[:, par, :], in0=o_bank[0:P, 0:D], scalar=rms[:, par, :],
                                             in1=m.XN[:, bass.ts(g, D)], op0=ALU.mult, op1=ALU.add).then_inc(sum_ready, 1)
                    dve.wait_ge(sum_ready, g + 1)
                    at_least(dve, eps_added, g - 1)
                    dve.bn_stats(bn6[:, par, :], yt[:, par, :]).then_inc(stats, 1)
                    dve.drain()
                    dve.bn_aggr(mv[:, par, :], bn6[:, par, :]).then_inc(stats, 1)
            steps(dve, step, depth)


def close_phase(nc, m):
    with ExitStack() as ctx:
        sem = ctx.enter_context(semaphores(nc, "cl", m.kept))
        sb = lambda s, shape: ctx.enter_context(nc.sbuf_tensor(f"cl_{s}", shape, F32))
        stats_ready = sem("stats_ready")
        var_eps = sem("var_eps")
        rstd_ready = sem("rstd_ready")
        normed = sem("normed")
        scaled = sem("scaled")
        moved = sem("moved")
        h_done = sem("h_done")
        bn6, mv, rstd = sb("bn6", [P, G, 6]), sb("mv", [P, G, 2]), sb("rstd", [P, G])
        wide = lambda row, k: m.row(row).unsqueeze(1).broadcast_to([P, k, D])
        block = ctx.enter_context(nc.Block())

        @block.gpsimd
        def _(pool):
            inverse_deviations(pool, m, mv, rstd, stats_ready, var_eps, rstd_ready)
            for n, (c, k) in enumerate(CHUNKS):
                pool.wait_ge(normed, n + 1)
                x = m.T[:, c * D:(c + k) * D].rearrange("p (g d) -> p g d", d=D)
                pool.tensor_tensor(x, x, wide("n3_g", k), ALU.mult).then_inc(scaled, 1)

        @block.vector
        def _(dve):
            group_statistics(dve, m.T, bn6, mv, stats_ready)
            for c, k in CHUNKS:
                h = m.H[:, c * D:(c + k) * D].rearrange("p (g d) -> p g d", d=D)
                ins = dve.tensor_tensor(h, h, wide("n3_b", k), ALU.add)
            ins.then_inc(moved, 1)
            dve.wait_ge(stats_ready, len(CHUNKS))
            for n, (c, k) in enumerate(CHUNKS):
                dve.wait_ge(rstd_ready, n + 1)
                for g in range(c, c + k):
                    x = m.T[:, g * D:(g + 1) * D]
                    ins = dve.tensor_scalar(x, x, mv[:, g, 0:1], rstd[:, g:g + 1], ALU.subtract, ALU.mult)
                ins.then_inc(normed, 1)
            dve.wait_ge(moved, 1)
            for n, (c, k) in enumerate(CHUNKS):
                dve.wait_ge(scaled, n + 1)
                h = m.H[:, c * D:(c + k) * D]
                dve.tensor_tensor(h, h, m.T[:, c * D:(c + k) * D], ALU.add).then_inc(h_done, 1)
            dve.wait_ge(h_done, len(CHUNKS))


def batch_norm_phase(nc, m):
    real = BATCH * S
    parts = -(-real // 512)
    while real % parts:
        parts += 1
    part = real // parts
    with ExitStack() as ctx:
        sem = ctx.enter_context(semaphores(nc, "bn", m.kept))
        sb = lambda s, shape: ctx.enter_context(nc.sbuf_tensor(f"bn_{s}", shape, F32))
        own = sem("own")
        stats_ready = sem("stats_ready")
        pool_own = sem("pool_own")
        rstd_ready = sem("rstd_ready")
        affine_ready = sem("affine_ready")
        relued = sem("relued")
        turned = sem("turned")
        h_ready = sem("h_ready")
        bn6, mv, ve, rstd = sb("bn6", [128, parts, 6]), sb("mv", [128, 2]), sb("ve", [128, 1]), sb("rstd", [128, 1])
        scale, shift = sb("scale", [128, 1]), sb("shift", [128, 1])
        block = ctx.enter_context(nc.Block())

        @block.gpsimd
        def _(pool):
            pool.wait_ge(stats_ready, 1)
            pool.tensor_tensor(ve[:, :], mv[:, 1:2], m.eps, ALU.add).then_inc(pool_own, 1)
            pool.wait_ge(pool_own, 1)
            pool.tensor_tensor(rstd[:, :], ve[:, :], m.mhalf, ALU.pow).then_inc(rstd_ready, 1)

        @block.tensor
        def _(pe):
            for n, (c, k) in enumerate(CHUNKS):
                pe.wait_ge(relued, n + 1)
                at_least(pe, h_ready, n - 1)
                for g in range(k):
                    mm = pe.transpose(m.bank[n % 2][0:P, g * D:(g + 1) * D], m.YT[:, (c + g) * P:(c + g + 1) * P], m.ident[:, :])
                mm.then_inc(turned, 1)

        @block.scalar
        def _(act):
            act.wait_ge(affine_ready, 1)
            for n, (c, k) in enumerate(CHUNKS):
                y = m.YT[:, c * P:(c + k) * P]
                act.activation(y, y, ACT.Relu, scale=scale[:, :], bias=shift[:, :]).then_inc(relued, 1)

        @block.vector
        def _(dve):
            for n in range(parts):
                dve.bn_stats(bn6[:, n, :], m.YT[:, n * part:(n + 1) * part])
            dve.drain()
            dve.bn_aggr(mv[:, :], bn6[:, :, :]).then_inc(stats_ready, 1)
            then = chained(dve, own)
            dve.wait_ge(rstd_ready, 1)
            then(dve.tensor_tensor(scale[:, :], m.col("bn_gamma"), rstd[:, :], ALU.mult))
            then(dve.tensor_tensor(shift[:, :], mv[:, 0:1], scale[:, :], ALU.mult))
            dve.tensor_tensor(shift[:, :], m.col("bn_beta"), shift[:, :], ALU.subtract).then_inc(affine_ready, 1)
            for n, (c, k) in enumerate(CHUNKS):
                dve.wait_ge(turned, n + 1)
                h = m.H[:, c * D:(c + k) * D]
                dve.tensor_tensor(h, h, m.bank[n % 2][0:P, 0:k * D], ALU.add).then_inc(h_ready, 1)
            dve.wait_ge(h_ready, len(CHUNKS))


SETS = 3


def routes_phase(nc, m, io):
    B = G * TB
    with ExitStack() as ctx:
        sem = ctx.enter_context(semaphores(nc, "rt", m.kept))
        sb = lambda s, shape: ctx.enter_context(nc.sbuf_tensor(f"rt_{s}", shape, F32))
        w_loaded = sem("w_loaded")
        psum = sem("psum")
        hid_ready = sem("hid_ready")
        shifted = sem("shifted")
        exped = sem("exped")
        own = sem("own")
        spread_ready = sem("spread_ready")
        rw = sb("rw", [128, 128 + 1 + 8 + P + G])
        hid = sb("hid", [128, B])
        lg, pr, one, tmp = (sb(n, [B, 1, SETS]) for n in ("lg", "pr", "one", "tmp"))
        top, tot = sb("top", [B, 1]), sb("tot", [B, 1])
        spread = sb("spread", [B, G, SETS])
        block = ctx.enter_context(nc.Block())
        wide = lambda x: x[:, :].unsqueeze(2).broadcast_to([B, 1, SETS])

        @block.sync
        def _(sp):
            sp.dma_start(rw[:, :], io["rt_w"]).then_inc(w_loaded, 16)

        @block.tensor
        def _(pe):
            pe.wait_ge(w_loaded, 16)
            pe.matmul(m.bank[0][:, 0:B], rw[:, 0:128], m.MEANS[:, :], start=True, stop=True).then_inc(psum, 1)
            pe.wait_ge(hid_ready, 1)
            pe.matmul(m.bank[1][0:B, 0:8], hid[:, :], rw[:, 129:137], start=True, stop=True).then_inc(psum, 1)
            pe.wait_ge(spread_ready, 1)
            pe.matmul(m.bank[2][0:P, 0:G * SETS], rw[0:B, 137:137 + P], spread[:, :, :].rearrange("p g x -> p (g x)"),
                      start=True, stop=True).then_inc(psum, 1)

        @block.scalar
        def _(act):
            act.wait_ge(psum, 1)
            act.activation(hid[:, :], m.bank[0][:, 0:B], ACT.Relu, scale=1.0 / S, bias=rw[:, 128:129]).then_inc(hid_ready, 1)
            act.wait_ge(shifted, 1)
            act.activation(pr[:, 0, :], lg[:, 0, :], ACT.Exp).then_inc(exped, 1)

        @block.vector
        def _(dve):
            then = chained(dve, own)
            dve.wait_ge(w_loaded, 16)
            dve.wait_ge(psum, 2)
            then(dve.tensor_tensor(lg[:, 0, :], m.bank[1][0:B, 0:SETS], m.small("r_b2", SETS)[0:B, :], ALU.add))
            then(dve.tensor_reduce(top[:, :], lg[:, :, :], AX, ALU.max))
            dve.tensor_tensor(lg[:, :, :], lg[:, :, :], wide(top), ALU.subtract).then_inc(shifted, 1)
            dve.wait_ge(exped, 1)
            then(dve.tensor_reduce(tot[:, :], pr[:, :, :], AX, ALU.add))
            then(dve.reciprocal(tot[:, :], tot[:, :]))
            then(dve.tensor_tensor(pr[:, :, :], pr[:, :, :], wide(tot), ALU.mult))
            first_best(dve, m, then, one[:, :, :], pr[:, :, :], tmp[:, :, :], top[:, :], [B, 1, SETS])
            dve.tensor_tensor(spread[:, :, :], rw[0:B, 137 + P:137 + P + G].unsqueeze(2).broadcast_to([B, G, SETS]),
                              one[:, :, :].broadcast_to([B, G, SETS]), ALU.mult).then_inc(spread_ready, 1)
            dve.wait_ge(psum, 3)
            then(dve.tensor_copy(m.MSK[:, :], m.bank[2][0:P, 0:G * SETS]))


COLS = ["tok_b", "bn_gamma", "bn_beta"]
ROWS = ["a0_b_proj", "a0_gamma", "a0_beta", "small", "n1_g", "n1_b", "n3_g", "n3_b", "ffn_b2"]
SMALL = {"rb0": 0, "br": 8, "none": 16, "dt_bias": 24, "A_log": 32, "rank": 40, "r_b2": 48}


def build(nc, io, out):
    with ExitStack() as ctx:
        m = Shared()
        m.kept = ctx
        m.bank = [ctx.enter_context(nc.psum_tensor(f"bank{b}", [128, 512], F32)) for b in range(4)]
        m.quad_bank = ctx.enter_context(nc.psum_tensor("quad_bank", [128, 4, 512], F32))
        m.H = ctx.enter_context(nc.sbuf_tensor("H", [P, G * D], F32))
        m.const = ctx.enter_context(nc.sbuf_tensor("const", list(io["const"].shape), F32))
        m.cols = ctx.enter_context(nc.sbuf_tensor("cols", list(io["cols"].shape), F32))
        m.rows = ctx.enter_context(nc.sbuf_tensor("rows", list(io["rows"].shape), F32))
        m.bconst = ctx.enter_context(nc.sbuf_tensor("bconst", list(io["bconst"].shape), BF16))
        m.XN = ctx.enter_context(nc.sbuf_tensor("XN", [P, G * D], F32))
        m.row = lambda n, p=P: m.rows[0:p, ROWS.index(n) * D:(ROWS.index(n) + 1) * D]
        m.small = lambda n, w=8, p=P: m.row("small", p)[:, SMALL[n]:SMALL[n] + w]
        m.rank = m.small("rank", p=128)
        m.XT = ctx.enter_context(nc.sbuf_tensor("XT", [128, G * P], F32))
        m.LG = ctx.enter_context(nc.sbuf_tensor("LG", [128, G * 8], F32))
        m.TLG = m.LG[:, 0:NT * 8].rearrange("p (t e) -> p t e", e=8)
        m.GATE = ctx.enter_context(nc.sbuf_tensor("GATE", [128, NT * 8], F32))
        m.ident = m.const[:, 0:128]
        m.mhalf = m.const[:, 128:129]
        m.eps = m.const[:, 129:130]
        m.inv_cw = m.const[:, 130:131]
        m.later = m.const[0:P, 131:131 + P]
        m.one = m.const[:, 131 + 2 * P:132 + 2 * P]
        m.upto = m.const[0:P, 131 + P:131 + 2 * P]
        m.T = ctx.enter_context(nc.sbuf_tensor("T", [P, G * D], F32))
        m.DT = ctx.enter_context(nc.sbuf_tensor("DT", [P, G * 8], F32))
        m.DTA = ctx.enter_context(nc.sbuf_tensor("DTA", [P, G * 8], F32))
        m.YT = ctx.enter_context(nc.sbuf_tensor("YT", [128, G * P], F32))
        m.MSK = ctx.enter_context(nc.sbuf_tensor("MSK", [P, G * SETS], F32))
        m.MEANS = ctx.enter_context(nc.sbuf_tensor("MEANS", [128, G * TB], F32))
        m.img = m.bconst[:, 0:P]
        m.not_img = m.bconst[:, P:5 * P]
        m.image_marks = m.bconst[:, 5 * P:9 * P]
        m.image_rows = m.bconst[:, 9 * P:9 * P + 128]
        m.col = lambda n: m.cols[:, COLS.index(n):COLS.index(n) + 1]
        patch_phase(nc, m, io)
        w = Weights(io["a0_wv"], HD ** -0.5, io["a0_wqk"], io["a0_wo"])
        attention_phase(nc, m, "a0", w, ending="post_norm")
        prepare_phase(nc, m, "p0", io["f0_router"], m.small("rb0", p=128), tiled=True)
        experts_phase(nc, m, "f0", io["f0_w1"], io["f0_w2"], io["f0_b1"], ACT.Gelu, 8, 4, io["f0_b2"], gates=tree_gates)
        prepare_phase(nc, m, "p1", io["ss_router"], m.small("dt_bias"))
        time_steps(nc, m)
        state_space_phase(nc, m, io)
        experts_phase(nc, m, "fs", io["fs_w1"], io["fs_w2"], io["fs_b1"], ACT.Gelu, 1, 4, None, m.T)
        close_phase(nc, m)
        prepare_phase(nc, m, "p2", io["f1_router"], m.small("br", p=128), tiled=True)
        experts_phase(nc, m, "f1", io["f1_w1"], io["f1_w2"], io["f1_b1"], ACT.Gelu, 8, 4, io["f1_b2"], gates=lambda *a: best_gates(*a, 1))
        w = Weights(None, 64 ** -0.5, io["a1_wqk"], io["a1_wo"])
        attention_phase(nc, m, "a1", w, hd=64)
        prepare_phase(nc, m, "p3", io["f2_router"], m.small("none", p=128), tiled=True)
        experts_phase(nc, m, "f2", io["f2_w1"], io["f2_w2"], io["f2_b1"], ACT.Gelu_apprx_tanh, 8, 2, io["f2_b2"], gates=lambda *a: best_gates(*a, 2))
        w = Weights(None, 64 ** -0.5, own=io["a2_own"], factors=io["a2_factors"])
        attention_phase(nc, m, "a2", w, ending="channels")
        batch_norm_phase(nc, m)
        prepare_phase(nc, m, "p4", means=True)
        routes_phase(nc, m, io)
        w = Weights(io["a3_wv"], HD ** -0.5, io["a3_wqk"], io["a3_wo"])
        attention_phase(nc, m, "a3", w, nx=SETS, masks=True)
        with ExitStack() as ctx2:
            stored = ctx2.enter_context(nc.semaphore("stored"))
            block = ctx2.enter_context(nc.Block())

            @block.sync
            def _(sp):
                h = m.H[:, :].rearrange("p (g d) -> p g d", d=D)
                full = BATCH // TB
                dst = out[0:full * TB].rearrange("(g b) s d -> (b s) g d", b=TB)
                sp.dma_start(dst, h[:, 0:full, :]).then_inc(stored, 16)
                sp.dma_start(out[full * TB:BATCH].rearrange("b s d -> (b s) d"),
                             h[0:(BATCH - full * TB) * S, full, :]).then_inc(stored, 16)
                sp.wait_ge(stored, 32)


def qk_tiles(wq, wk):
    z = np.zeros((128, 2, 2, 4, SLOT), wq.dtype)
    for i, w in enumerate((wq, wk)):
        z[:, i, :, :, 0:HD] = w.reshape(128, 2, 4, HD)
    return z.reshape(128, 512)


def head_rows(w):
    z = np.zeros((2, 4, SLOT, w.shape[1]), w.dtype)
    z[:, :, 0:HD] = w.reshape(2, 4, HD, w.shape[1])
    return z.reshape(2, 128, w.shape[1]).transpose(1, 0, 2)


def laid_out(a):
    f = np.float32
    x = a["x"]
    pad = np.zeros((G * TB, 3, 6, 16, 6, 16), f)
    pad[:BATCH] = x.reshape(BATCH, 3, 6, 16, 6, 16)
    pats = pad.transpose(1, 3, 5, 0, 2, 4).reshape(KC, 128, G * P).transpose(1, 0, 2)
    r = {}
    r["patches"] = pats
    r["tokw"] = a["L0_tok_w"].T.reshape(KC, 128, D).transpose(1, 0, 2).reshape(128, KC * D)
    const = np.zeros((128, 132 + 2 * P), f)
    const[:, 131 + 2 * P] = 1.0
    tok = np.arange(P)
    same = tok[:, None] // S == tok[None, :] // S
    const[:, 130] = 1.0 / CW
    const[0:P, 131:131 + P] = same & (tok[:, None] > tok[None, :])
    const[0:P, 131 + P:131 + 2 * P] = same & (tok[:, None] <= tok[None, :])
    const[:, 0:128] = np.eye(128, dtype=f)
    const[:, 128] = -0.5
    const[:, 129] = EPS
    r["const"] = const
    r["cols"] = np.stack([a["L0_tok_b"], a["L3_attn_gamma"], a["L3_attn_beta"]], 1)
    small = np.zeros(D, f)
    small[SMALL["rank"]:SMALL["rank"] + 8] = np.arange(8, 0, -1)
    for n, x in (("rb0", "L0_ffn_rb"), ("br", "L1_ffn_br"), ("dt_bias", "L1_attn_dt_bias"), ("A_log", "L1_attn_A_log"), ("r_b2", "L3_ffn_r_b2")):
        small[SMALL[n]:SMALL[n] + a[x].size] = a[x]
    rows = [a["L0_attn_b_proj"], a["L0_attn_ln_gamma"], a["L0_attn_ln_beta"], small] + [a["L1_attn_" + n] for n in ("n1_g", "n1_b", "n3_g", "n3_b", "ffn_b2")]
    r["rows"] = np.broadcast_to(np.concatenate(rows), (128, sum(x.size for x in rows)))
    b = np.zeros((128, 9 * P + 128), f)
    for i in range(TB):
        for c in range(4):
            b[i, 9 * P + SLOT * c + HD + i] = 1
            here = slice((5 + c) * P + i * S, (5 + c) * P + (i + 1) * S)
            if c < 2:
                b[i, here] = 1
            else:
                b[i, (5 + c) * P:(6 + c) * P] = NEG
                b[i, here] = 0
    for k in range(4):
        for i in range(TB):
            b[SLOT * k + i, i * S:(i + 1) * S] = 1
            for c in range(4):
                b[SLOT * k + i, P * (1 + c):P * (2 + c)] = NEG
                b[SLOT * k + i, P * (1 + c) + i * S:P * (1 + c) + (i + 1) * S] = 0
    r["bconst"] = b
    wqkv = a["L0_attn_w_qkv"].T
    r["a0_wqk"] = qk_tiles(wqkv[:, 0:128], wqkv[:, 128:256]).reshape(128, 1, 512)
    r["a0_wv"] = wqkv[:, 256:384].reshape(128, 1, 128)
    r["a0_wo"] = head_rows(a["L0_attn_w_proj"].T)
    padded = lambda w, n: np.concatenate([w, np.zeros((w.shape[0], n - w.shape[1]), f)], 1)
    r["f0_router"] = padded(a["L0_ffn_rw"].T, 8)
    for n, w1, b1, w2, b2 in (("f0", "L0_ffn_w1", "L0_ffn_b1", "L0_ffn_w2", "L0_ffn_b2"),
                              ("f1", "L1_ffn_W1", "L1_ffn_b1", "L1_ffn_W2", "L1_ffn_b2"),
                              ("f2", "L2_ffn_W1", "L2_ffn_b1", "L2_ffn_W2", "L2_ffn_b2")):
        e, hid = a[b1].shape
        r[n + "_w1"] = a[w1]
        r[n + "_b1"] = a[b1].reshape(e, hid // 128, 128).transpose(0, 2, 1)
        r[n + "_w2"] = a[w2].reshape(e, hid // 128, 128, D).transpose(0, 2, 1, 3).reshape(e, 128, hid // 128 * D)
        spread = np.zeros((QUAD, SLOT, QUAD, D), f)
        for t in range(QUAD):
            spread[t, 0:e, t] = a[b2]
        r[n + "_b2"] = spread.reshape(128, QUAD, D)
    win = a["L1_attn_W_in"]
    r["ss_router"] = padded(win[:, 768:772], 8)
    r["ss_win"] = win[:, 0:768]
    r["ss_taps"] = np.broadcast_to(a["L1_attn_conv_w"].T, (128, TAPS, 512))
    ch = np.zeros((128, 24), f)
    ch[:, 0:16] = a["L1_attn_conv_w"].reshape(4, 128, TAPS).transpose(1, 0, 2).reshape(128, 16)
    ch[:, 16:20] = a["L1_attn_conv_b"].reshape(4, 128).T
    ch[:, 20:22] = a["L1_attn_gnorm_w"].reshape(2, 128).T
    r["ss_ch"] = ch
    r["ss_drow"] = np.broadcast_to(a["L1_attn_D_skip"], (P, NS))
    r["ss_wout"] = a["L1_attn_W_out"].reshape(2, 128, D).transpose(1, 0, 2)
    r["fs_w1"] = a["L1_attn_ffn_w1"][None]
    r["fs_b1"] = a["L1_attn_ffn_b1"].reshape(1, 4, 128).transpose(0, 2, 1)
    r["fs_w2"] = a["L1_attn_ffn_w2"].reshape(1, 4, 128, D).transpose(0, 2, 1, 3).reshape(1, 128, 4 * D)
    r["f1_router"] = a["L1_ffn_Wr"]
    r["f2_router"] = a["L2_ffn_Wg"]
    wq, wv = (a[n].transpose(1, 0, 2).reshape(128, 512) for n in ("L2_attn_WQ", "L2_attn_WV"))
    r["a1_wqk"] = np.concatenate([wq, wv], 1).reshape(128, 1, 1024)
    r["a1_wo"] = a["L2_attn_WU"].reshape(4, 128, 128).transpose(1, 0, 2)
    eye = np.eye(128, dtype=f)
    r["a2_own"] = qk_tiles(eye, eye)[:, 0:256]
    by_e = lambda w: np.concatenate([w.transpose(1, 0, 2).reshape(64, 128), np.zeros((64, 128), f)])
    same = np.kron(np.eye(NH, dtype=f), np.ones((HD, HD), f))
    wvb = np.zeros((4, 2, 64, NH, SLOT), f)
    for h in range(NH):
        wvb[h // 2, h % 2, :, h, 0:HD] = a["L3_attn_wv"][h]
    r["a2_factors"] = np.concatenate([by_e(a["L3_attn_wk"]), qk_tiles(by_e(a["L3_attn_wq"]), eye)[:, 0:256],
                                      qk_tiles(same, eye)[:, 0:256],
                                      wvb.reshape(4, 128, 256).transpose(1, 0, 2).reshape(128, 1024),
                                      a["L3_attn_wo"].T.reshape(4, 128, 128).transpose(1, 0, 2).reshape(128, 512)], 1)
    rt = np.zeros((128, 128 + 1 + 8 + P + G), f)
    rt[:, 0:32] = a["L3_ffn_r_w1"]
    rt[0:32, 128] = a["L3_ffn_r_b1"]
    rt[0:32, 129:132] = a["L3_ffn_r_w2"]
    image = np.arange(G * TB)
    rt[0:G * TB, 137:137 + P] = image[:, None] % TB == tok[None, :] // S
    rt[0:G * TB, 137 + P:] = image[:, None] // TB == np.arange(G)[None, :]
    r["rt_w"] = rt
    heads = lambda w: w.reshape(128, -1, HD).repeat(NH * HD // w.shape[1], axis=1).reshape(128, 128)
    ws = [[a[f"L3_ffn_{n}{i}"] for n in ("wq", "wk", "wv", "wo")] for i in range(SETS)]
    r["a3_wqk"] = np.stack([qk_tiles(wq, heads(wk)) for wq, wk, _, _ in ws], 1)
    r["a3_wv"] = np.stack([heads(wv) for _, _, wv, _ in ws], 1)
    r["a3_wo"] = np.concatenate([head_rows(wo) for _, _, _, wo in ws], 2)
    return {k: np.ascontiguousarray(v) for k, v in r.items()}


def kernel(**inputs):
    import concourse.bacc as bacc
    from concourse.bass_utils import run_bass_kernel_spmd

    nc = bacc.Bacc("TRN2", target_bir_lowering=False, num_devices=1)
    arrays = laid_out({k: np.asarray(v) for k, v in inputs.items()})
    aps = {k: nc.dram_tensor(f"in_{k}", v.shape, mybir.dt.from_np(v.dtype), kind="ExternalInput").ap()
           for k, v in arrays.items()}
    out = nc.dram_tensor("out", (BATCH, S, D), F32, kind="ExternalOutput").ap()
    build(nc, aps, out)
    r = run_bass_kernel_spmd(nc, [{f"in_{k}": v for k, v in arrays.items()}], core_ids=[0])
    return r.results[0]["out"]
```
